# Optimizing a Trainium2 kernel written in Bass

```python
import numpy as np
import jax
import jax.numpy as jnp

def _softmax(x, axis=-1):
    return jax.nn.softmax(x, axis=axis)

def _gelu(x):
    return jax.nn.gelu(x, approximate=True)

def _silu(x):
    return jax.nn.silu(x)

def _sigmoid(x):
    return jax.nn.sigmoid(x)

def _layernorm(x, axis=-1, eps=1e-05):
    m = jnp.mean(x, axis=axis, keepdims=True)
    v = jnp.var(x, axis=axis, keepdims=True)
    return (x - m) / jnp.sqrt(v + eps)

def _scatter_add(tgt, idx, src, axis=0):
    return tgt.at[idx].add(src)

def _segment_sum(src, seg, n):
    return jax.ops.segment_sum(src, seg, n)
kernel_name = 'mk_vit_tower_postln_d2_tok_img768_r4_195dc9'

def setup_inputs(seed: int=0):
    np.random.seed(seed)
    _w = jnp.asarray

    def _rec_inputs():
        import jax
        import jax.numpy as jnp
        _rk = jax.random.key(seed)
        x = -0.00040386 + 0.999972 * jax.random.normal(jax.random.fold_in(_rk, 1), (8, 3, 128, 128), jnp.float32)
        return x
    x = _rec_inputs()

    def _L0_tok_setup():
        import jax, jax.numpy as jnp
        import numpy as np
        B, C, H, W = (16, 3, 128, 128)
        P = 16
        DIM = 192
        HEADS = 12
        DH = 64
        INNER = HEADS * DH
        MLP = 768
        EPS = 1e-05

        def layernorm(x, g, b):
            mu = jnp.mean(x, axis=-1, keepdims=True)
            var = jnp.var(x, axis=-1, keepdims=True)
            return (x - mu) * jax.lax.rsqrt(var + EPS) * g + b
        key = jax.random.key(seed)
        ks = jax.random.split(key, 8)
        patch_dim = C * P * P
        s = lambda d: 1.0 / np.sqrt(d)
        return {'x': jax.random.normal(ks[0], (B, C, H, W), jnp.float32), 'w_patch': jax.random.normal(ks[1], (patch_dim, DIM), jnp.float32) * s(patch_dim), 'b_patch': jnp.zeros((DIM,), jnp.float32), 'g1': jnp.ones((DIM,), jnp.float32), 'beta1': jnp.zeros((DIM,), jnp.float32), 'w_qkv': jax.random.normal(ks[2], (DIM, 3 * INNER), jnp.float32) * s(DIM), 'w_out': jax.random.normal(ks[3], (INNER, DIM), jnp.float32) * s(INNER), 'b_out': jnp.zeros((DIM,), jnp.float32), 'g2': jnp.ones((DIM,), jnp.float32), 'beta2': jnp.zeros((DIM,), jnp.float32), 'w_ff1': jax.random.normal(ks[4], (DIM, MLP), jnp.float32) * s(DIM), 'b_ff1': jnp.zeros((MLP,), jnp.float32), 'w_ff2': jax.random.normal(ks[5], (MLP, DIM), jnp.float32) * s(MLP), 'b_ff2': jnp.zeros((DIM,), jnp.float32)}
    _L0_tok_all = _L0_tok_setup()
    _L0_tok_in = {k: v for k, v in _L0_tok_all.items() if k in ('w_patch', 'b_patch', 'g1', 'beta1', 'w_qkv', 'w_out', 'b_out', 'g2', 'beta2', 'w_ff1', 'b_ff1', 'w_ff2', 'b_ff2')}
    del _L0_tok_all

    def _L0_attn_setup():
        import jax, jax.numpy as jnp
        import numpy as np
        B, S, H = (2, 512, 192)
        E, NH, WIN = (4, 12, 64)
        HD = H // NH
        NEG = -1e+30

        def _sliding_mask(seq_len, window):
            i = jnp.arange(seq_len)
            d = i[:, None] - i[None, :]
            return (d >= 0) & (d < window)
        key = jax.random.key(seed)
        ks = jax.random.split(key, 7)
        s = 0.02
        return {'x': jax.random.normal(ks[0], (B, S, H), jnp.float32), 'wq': jax.random.normal(ks[1], (E, H, H), jnp.float32) * s, 'wk': jax.random.normal(ks[2], (E, H, H), jnp.float32) * s, 'wv': jax.random.normal(ks[3], (E, H, H), jnp.float32) * s, 'wo': jax.random.normal(ks[4], (E, H, H), jnp.float32) * s, 'w_gate': jax.random.normal(ks[5], (H, E * H), jnp.float32) * s, 'w_up': jax.random.normal(ks[6], (E, H, H), jnp.float32).reshape(H, E * H) * 0 + jax.random.normal(jax.random.fold_in(key, 7), (H, E * H), jnp.float32) * s}
    _L0_attn_all = _L0_attn_setup()
    _L0_attn_in = {k: v for k, v in _L0_attn_all.items() if k in ('wq', 'wk', 'wv', 'wo', 'w_gate', 'w_up')}
    del _L0_attn_all

    def _L0_ffn_setup():
        import jax, jax.numpy as jnp
        import numpy as np
        B, N, D, E, F, K = (2, 512, 192, 8, 768, 2)
        V_MAX = 3.0
        FEAT_CLAMP = 10.0

        def bk_green_diag(a):
            aT = jnp.swapaxes(a, 0, 1)

            def step(c, ai):
                d = ai - 1.0 / c
                return (d, d)
            d0 = aT[0]
            _, d_rest = jax.lax.scan(step, d0, aT[1:])
            d = jnp.concatenate([d0[None], d_rest], axis=0)
            eN = aT[-1]
            _, e_rest = jax.lax.scan(step, eN, aT[:-1], reverse=True)
            e = jnp.concatenate([e_rest, eN[None]], axis=0)
            G = 1.0 / (d + e - aT)
            return jnp.swapaxes(G, 0, 1)
        key = jax.random.key(seed)
        ks = jax.random.split(key, 8)
        s = lambda k, shape, sc: jax.random.normal(k, shape, jnp.float32) * sc
        return {'x': s(ks[0], (B, N, D), 1.0), 'v_w': s(ks[1], (D,), 0.02), 'v_b': jnp.zeros((), jnp.float32), 'gate_w': s(ks[2], (D, E), 0.02), 'gate_b': jnp.zeros((E,), jnp.float32), 'w1': s(ks[3], (E, D, F), 0.02), 'b1': jnp.zeros((E, F), jnp.float32), 'w2': s(ks[4], (E, F, D), 0.02), 'b2': jnp.zeros((E, D), jnp.float32), 'out_w': s(ks[5], (2, D), 0.02), 'out_b': jnp.zeros((D,), jnp.float32), 'bk_scale': jnp.ones((D,), jnp.float32)}
    _L0_ffn_all = _L0_ffn_setup()
    _L0_ffn_in = {k: v for k, v in _L0_ffn_all.items() if k in ('v_w', 'v_b', 'gate_w', 'gate_b', 'w1', 'b1', 'w2', 'b2', 'out_w', 'out_b', 'bk_scale')}
    del _L0_ffn_all

    def _L1_attn_setup():
        import jax, jax.numpy as jnp
        import numpy as np
        B, N, E, H = (2, 512, 192, 12)
        D = E // H
        G = 16
        LN_EPS = 1e-05

        def _layernorm(x, w, b):
            mu = jnp.mean(x, axis=-1, keepdims=True)
            var = jnp.mean(jnp.square(x - mu), axis=-1, keepdims=True)
            return (x - mu) * jax.lax.rsqrt(var + LN_EPS) * w + b
        key = jax.random.key(seed)
        ks = jax.random.split(key, 8)
        s = E ** (-0.5)
        x = jax.random.normal(ks[0], (B, N, E), jnp.float32)
        log_slope = -2.0 ** (-8.0 * (jnp.arange(H, dtype=jnp.float32) + 1.0) / H)
        Wq = jax.random.normal(ks[1], (E, E), jnp.float32) * s
        Wk = jax.random.normal(ks[2], (E, E), jnp.float32) * s
        Wv = jax.random.normal(ks[3], (E, E), jnp.float32) * s
        Wo = jax.random.normal(ks[4], (E, E), jnp.float32) * s
        Wg1 = jax.random.normal(ks[5], (E, G), jnp.float32) * s
        Wg2 = jax.random.normal(ks[6], (G, E), jnp.float32) * G ** (-0.5)
        ln_w = jnp.ones((E,), jnp.float32)
        ln_b = jnp.zeros((E,), jnp.float32)
        return {'x': x, 'log_slope': log_slope, 'Wq': Wq, 'Wk': Wk, 'Wv': Wv, 'Wo': Wo, 'Wg1': Wg1, 'Wg2': Wg2, 'ln_w': ln_w, 'ln_b': ln_b}
    _L1_attn_all = _L1_attn_setup()
    _L1_attn_in = {k: v for k, v in _L1_attn_all.items() if k in ('log_slope', 'Wq', 'Wk', 'Wv', 'Wo', 'Wg1', 'Wg2', 'ln_w', 'ln_b')}
    del _L1_attn_all

    def _L1_ffn_setup():
        import jax, jax.numpy as jnp
        import numpy as np
        GT0 = [[0, 1, 0, 0, 1, 0], [0, 1, 0, 0, 0, 1], [0, 0, 1, 0, 1, 0], [0, 0, 1, 0, 0, 1], [0, 0, 0, 1, 1, 0], [0, 0, 0, 1, 0, 1]]
        NCLS = 6
        K = 1

        def _expert_pairs():
            pairs = []
            for i in range(NCLS):
                p = [(j - 1, k - 1) for j in range(1, 6) for k in range(1, 6) if j != k and GT0[i][j] == 1 and (GT0[i][k] == 1)]
                pairs.append(p)
            return pairs
        PAIRS = _expert_pairs()
        B, P, D, H = (64, 64, 192, 768)

        def _gelu(t):
            return jax.nn.gelu(t, approximate=False)
        key = jax.random.key(seed)
        ks = jax.random.split(key, 8)
        s = 0.02
        x = jax.random.normal(ks[0], (B, NCLS + P, D), dtype=jnp.float32)
        mids = jax.random.randint(ks[1], (B,), 0, 6)
        moe0_W1 = jax.random.normal(ks[2], (D, H), dtype=jnp.float32) * s
        moe0_b1 = jnp.zeros((H,), jnp.float32)
        moe0_W2 = jax.random.normal(ks[3], (H, D), dtype=jnp.float32) * s
        moe0_b2 = jnp.zeros((D,), jnp.float32)
        A1_W = jax.random.normal(ks[4], (5, D, H), dtype=jnp.float32) * s
        A1_b = jnp.zeros((5, H), jnp.float32)
        A2_W = jax.random.normal(ks[5], (5, H, D), dtype=jnp.float32) * s
        A2_b = jnp.zeros((5, D), jnp.float32)
        G_W = jax.random.normal(ks[6], (NCLS, D, 2), dtype=jnp.float32) * s
        return {'x': x, 'moe0_W1': moe0_W1, 'moe0_b1': moe0_b1, 'moe0_W2': moe0_W2, 'moe0_b2': moe0_b2, 'A1_W': A1_W, 'A1_b': A1_b, 'A2_W': A2_W, 'A2_b': A2_b, 'G_W': G_W, 'mids': mids}
    _L1_ffn_all = _L1_ffn_setup()
    _L1_ffn_in = {k: v for k, v in _L1_ffn_all.items() if k in ('moe0_W1', 'moe0_b1', 'moe0_W2', 'moe0_b2', 'A1_W', 'A1_b', 'A2_W', 'A2_b', 'G_W', 'mids')}
    del _L1_ffn_all
    return {'x': x, 'L0_tok_w_patch': _L0_tok_in['w_patch'], 'L0_tok_b_patch': _L0_tok_in['b_patch'], 'L0_tok_g1': _L0_tok_in['g1'], 'L0_tok_beta1': _L0_tok_in['beta1'], 'L0_tok_w_qkv': _L0_tok_in['w_qkv'], 'L0_tok_w_out': _L0_tok_in['w_out'], 'L0_tok_b_out': _L0_tok_in['b_out'], 'L0_tok_g2': _L0_tok_in['g2'], 'L0_tok_beta2': _L0_tok_in['beta2'], 'L0_tok_w_ff1': _L0_tok_in['w_ff1'], 'L0_tok_b_ff1': _L0_tok_in['b_ff1'], 'L0_tok_w_ff2': _L0_tok_in['w_ff2'], 'L0_tok_b_ff2': _L0_tok_in['b_ff2'], 'L0_attn_wq': _L0_attn_in['wq'], 'L0_attn_wk': _L0_attn_in['wk'], 'L0_attn_wv': _L0_attn_in['wv'], 'L0_attn_wo': _L0_attn_in['wo'], 'L0_attn_w_gate': _L0_attn_in['w_gate'], 'L0_attn_w_up': _L0_attn_in['w_up'], 'L0_ffn_v_w': _L0_ffn_in['v_w'], 'L0_ffn_v_b': _L0_ffn_in['v_b'], 'L0_ffn_gate_w': _L0_ffn_in['gate_w'], 'L0_ffn_gate_b': _L0_ffn_in['gate_b'], 'L0_ffn_w1': _L0_ffn_in['w1'], 'L0_ffn_b1': _L0_ffn_in['b1'], 'L0_ffn_w2': _L0_ffn_in['w2'], 'L0_ffn_b2': _L0_ffn_in['b2'], 'L0_ffn_out_w': _L0_ffn_in['out_w'], 'L0_ffn_out_b': _L0_ffn_in['out_b'], 'L0_ffn_bk_scale': _L0_ffn_in['bk_scale'], 'L1_attn_log_slope': _L1_attn_in['log_slope'], 'L1_attn_Wq': _L1_attn_in['Wq'], 'L1_attn_Wk': _L1_attn_in['Wk'], 'L1_attn_Wv': _L1_attn_in['Wv'], 'L1_attn_Wo': _L1_attn_in['Wo'], 'L1_attn_Wg1': _L1_attn_in['Wg1'], 'L1_attn_Wg2': _L1_attn_in['Wg2'], 'L1_attn_ln_w': _L1_attn_in['ln_w'], 'L1_attn_ln_b': _L1_attn_in['ln_b'], 'L1_ffn_moe0_W1': _L1_ffn_in['moe0_W1'], 'L1_ffn_moe0_b1': _L1_ffn_in['moe0_b1'], 'L1_ffn_moe0_W2': _L1_ffn_in['moe0_W2'], 'L1_ffn_moe0_b2': _L1_ffn_in['moe0_b2'], 'L1_ffn_A1_W': _L1_ffn_in['A1_W'], 'L1_ffn_A1_b': _L1_ffn_in['A1_b'], 'L1_ffn_A2_W': _L1_ffn_in['A2_W'], 'L1_ffn_A2_b': _L1_ffn_in['A2_b'], 'L1_ffn_G_W': _L1_ffn_in['G_W'], 'L1_ffn_mids': _L1_ffn_in['mids']}

def reference(x, L0_tok_w_patch, L0_tok_b_patch, L0_tok_g1, L0_tok_beta1, L0_tok_w_qkv, L0_tok_w_out, L0_tok_b_out, L0_tok_g2, L0_tok_beta2, L0_tok_w_ff1, L0_tok_b_ff1, L0_tok_w_ff2, L0_tok_b_ff2, L0_attn_wq, L0_attn_wk, L0_attn_wv, L0_attn_wo, L0_attn_w_gate, L0_attn_w_up, L0_ffn_v_w, L0_ffn_v_b, L0_ffn_gate_w, L0_ffn_gate_b, L0_ffn_w1, L0_ffn_b1, L0_ffn_w2, L0_ffn_b2, L0_ffn_out_w, L0_ffn_out_b, L0_ffn_bk_scale, L1_attn_log_slope, L1_attn_Wq, L1_attn_Wk, L1_attn_Wv, L1_attn_Wo, L1_attn_Wg1, L1_attn_Wg2, L1_attn_ln_w, L1_attn_ln_b, L1_ffn_moe0_W1, L1_ffn_moe0_b1, L1_ffn_moe0_W2, L1_ffn_moe0_b2, L1_ffn_A1_W, L1_ffn_A1_b, L1_ffn_A2_W, L1_ffn_A2_b, L1_ffn_G_W, L1_ffn_mids):
    import jax
    import jax.numpy as jnp

    def _L0_tok_ref(x, w_patch, b_patch, g1, beta1, w_qkv, w_out, b_out, g2, beta2, w_ff1, b_ff1, w_ff2, b_ff2):
        import jax, jax.numpy as jnp
        import numpy as np
        B, C, H, W = (16, 3, 128, 128)
        P = 16
        DIM = 192
        HEADS = 12
        DH = 64
        INNER = HEADS * DH
        MLP = 768
        EPS = 1e-05

        def layernorm(x, g, b):
            mu = jnp.mean(x, axis=-1, keepdims=True)
            var = jnp.var(x, axis=-1, keepdims=True)
            return (x - mu) * jax.lax.rsqrt(var + EPS) * g + b
        b = x.shape[0]
        hp, wp = (H // P, W // P)
        xp = x.reshape(b, C, hp, P, wp, P)
        xp = xp.transpose(0, 2, 4, 3, 5, 1).reshape(b, hp * wp, P * P * C)
        t = xp @ w_patch + b_patch
        h = layernorm(t, g1, beta1)
        qkv = h @ w_qkv
        q, k, v = jnp.split(qkv, 3, axis=-1)
        split_heads = lambda z: z.reshape(b, -1, HEADS, DH).transpose(0, 2, 1, 3)
        q, k, v = map(split_heads, (q, k, v))
        scale = DH ** (-0.5)
        dots = jnp.einsum('bhid,bhjd->bhij', q, k) * scale
        attn = jax.nn.softmax(dots, axis=-1)
        o = jnp.einsum('bhij,bhjd->bhid', attn, v)
        o = o.transpose(0, 2, 1, 3).reshape(b, -1, INNER)
        t = o @ w_out + b_out + t
        h = layernorm(t, g2, beta2)
        h = jax.nn.gelu(h @ w_ff1 + b_ff1, approximate=False)
        t = h @ w_ff2 + b_ff2 + t
        return t

    def _L0_attn_ref(x, wq, wk, wv, wo, w_gate, w_up):
        import jax, jax.numpy as jnp
        import numpy as np
        B, S, H = (2, 512, 192)
        E, NH, WIN = (4, 12, 64)
        HD = H // NH
        NEG = -1e+30

        def _sliding_mask(seq_len, window):
            i = jnp.arange(seq_len)
            d = i[:, None] - i[None, :]
            return (d >= 0) & (d < window)
        b, s, h = x.shape
        nh, hd = (NH, h // NH)
        mask = _sliding_mask(s, WIN)
        scale = jnp.float32(1.0 / np.sqrt(hd))
        outs = []
        for e in range(wq.shape[0]):
            q = (x @ wq[e].T).reshape(b, s, nh, hd).transpose(0, 2, 1, 3)
            k = (x @ wk[e].T).reshape(b, s, nh, hd).transpose(0, 2, 1, 3)
            v = (x @ wv[e].T).reshape(b, s, nh, hd).transpose(0, 2, 1, 3)
            scores = jnp.einsum('bhqd,bhkd->bhqk', q, k) * scale
            scores = jnp.where(mask, scores, NEG)
            attn = jax.nn.softmax(scores, axis=-1)
            o = jnp.einsum('bhqk,bhkd->bhqd', attn, v)
            o = o.transpose(0, 2, 1, 3).reshape(b, s, h)
            outs.append(o @ wo[e].T)
        fused = jnp.concatenate(outs, axis=-1)
        gate = jax.nn.silu(fused @ w_gate.T)
        value = fused @ w_up.T
        return gate * value

    def _L0_ffn_ref(x, v_w, v_b, gate_w, gate_b, w1, b1, w2, b2, out_w, out_b, bk_scale):
        import jax, jax.numpy as jnp
        import numpy as np
        B, N, D, E, F, K = (2, 512, 192, 8, 768, 2)
        V_MAX = 3.0
        FEAT_CLAMP = 10.0

        def bk_green_diag(a):
            aT = jnp.swapaxes(a, 0, 1)

            def step(c, ai):
                d = ai - 1.0 / c
                return (d, d)
            d0 = aT[0]
            _, d_rest = jax.lax.scan(step, d0, aT[1:])
            d = jnp.concatenate([d0[None], d_rest], axis=0)
            eN = aT[-1]
            _, e_rest = jax.lax.scan(step, eN, aT[:-1], reverse=True)
            e = jnp.concatenate([e_rest, eN[None]], axis=0)
            G = 1.0 / (d + e - aT)
            return jnp.swapaxes(G, 0, 1)
        v = jnp.clip(x @ v_w + v_b, -V_MAX, V_MAX)
        a = (-2.0 + v).astype(jnp.complex64) - 1j
        G = bk_green_diag(a)
        feats = jnp.stack([G.real, G.imag], axis=-1)
        logits = x @ gate_w + gate_b
        probs = jax.nn.softmax(logits, axis=-1)
        topv, topi = jax.lax.top_k(probs, K)
        topv = topv / jnp.sum(topv, axis=-1, keepdims=True)
        comb = jnp.sum(topv[..., None] * jax.nn.one_hot(topi, E, dtype=x.dtype), axis=2)
        h = jax.nn.gelu(jnp.einsum('bnd,edf->bnef', x, w1) + b1)
        y = jnp.einsum('bnef,efd->bned', h, w2) + b2
        ffn_out = jnp.einsum('bne,bned->bnd', comb, y)
        feats_c = jnp.clip(feats, -FEAT_CLAMP, FEAT_CLAMP)
        spec_out = feats_c @ out_w + out_b
        return ffn_out + bk_scale * spec_out

    def _L1_attn_ref(x, log_slope, Wq, Wk, Wv, Wo, Wg1, Wg2, ln_w, ln_b):
        import jax, jax.numpy as jnp
        import numpy as np
        B, N, E, H = (2, 512, 192, 12)
        D = E // H
        G = 16
        LN_EPS = 1e-05

        def _layernorm(x, w, b):
            mu = jnp.mean(x, axis=-1, keepdims=True)
            var = jnp.mean(jnp.square(x - mu), axis=-1, keepdims=True)
            return (x - mu) * jax.lax.rsqrt(var + LN_EPS) * w + b
        b, n, e = x.shape
        h = log_slope.shape[0]
        d = e // h
        silu = jax.nn.silu
        q = silu(x @ Wq).reshape(b, n, h, d).transpose(0, 2, 1, 3)
        k = silu(x @ Wk).reshape(b, n, h, d).transpose(0, 2, 1, 3)
        v = silu(x @ Wv).reshape(b, n, h, d).transpose(0, 2, 1, 3)
        idx = jnp.arange(n, dtype=jnp.float32)
        diff = idx[:, None] - idx[None, :]
        keep = diff >= 0
        decay = jnp.where(keep, jnp.exp(log_slope[:, None, None] * jnp.maximum(diff, 0.0)), 0.0)
        energy = jnp.einsum('bhnd,bhmd->bhnm', q, k) * decay
        out = jnp.einsum('bhnm,bhmd->bhnd', energy, v)
        out = out.transpose(0, 2, 1, 3).reshape(b, n, e)
        gate = jax.nn.sigmoid(x @ Wg1 @ Wg2)
        out = out * gate
        out = out @ Wo
        out = _layernorm(out, ln_w, ln_b)
        return out

    def _L1_ffn_ref(x, moe0_W1, moe0_b1, moe0_W2, moe0_b2, A1_W, A1_b, A2_W, A2_b, G_W, mids):
        import jax, jax.numpy as jnp
        import numpy as np
        GT0 = [[0, 1, 0, 0, 1, 0], [0, 1, 0, 0, 0, 1], [0, 0, 1, 0, 1, 0], [0, 0, 1, 0, 0, 1], [0, 0, 0, 1, 1, 0], [0, 0, 0, 1, 0, 1]]
        NCLS = 6
        K = 1

        def _expert_pairs():
            pairs = []
            for i in range(NCLS):
                p = [(j - 1, k - 1) for j in range(1, 6) for k in range(1, 6) if j != k and GT0[i][j] == 1 and (GT0[i][k] == 1)]
                pairs.append(p)
            return pairs
        PAIRS = _expert_pairs()
        B, P, D, H = (64, 64, 192, 768)

        def _gelu(t):
            return jax.nn.gelu(t, approximate=False)
        cls_tokens = x[:, :NCLS]
        patch_tokens = x[:, NCLS:]
        patch_out = _gelu(patch_tokens @ moe0_W1 + moe0_b1) @ moe0_W2 + moe0_b2
        cls_outs = []
        for i in range(NCLS):
            tok = cls_tokens[:, i]
            eouts = [_gelu(tok @ A1_W[a] + A1_b[a]) @ A2_W[c] + A2_b[c] for a, c in PAIRS[i]]
            out = jnp.stack(eouts, axis=-1)
            gate = jax.nn.softmax(tok @ G_W[i], axis=-1)
            thr = jnp.sort(gate, axis=-1)[..., -(K + 1)]
            mask = (gate > thr[..., None]).astype(gate.dtype)
            g = gate * mask
            g = g / jnp.clip(jnp.sum(g, axis=-1, keepdims=True), 1e-06)
            cls_outs.append(jnp.sum(out * g[:, None, :], axis=-1))
        cls_out = jnp.stack(cls_outs, axis=1)
        return jnp.concatenate([cls_out, patch_out], axis=1)
    h = _L0_tok_ref(x, L0_tok_w_patch, L0_tok_b_patch, L0_tok_g1, L0_tok_beta1, L0_tok_w_qkv, L0_tok_w_out, L0_tok_b_out, L0_tok_g2, L0_tok_beta2, L0_tok_w_ff1, L0_tok_b_ff1, L0_tok_w_ff2, L0_tok_b_ff2)
    h = _layernorm(h + _L0_attn_ref(h, L0_attn_wq, L0_attn_wk, L0_attn_wv, L0_attn_wo, L0_attn_w_gate, L0_attn_w_up), axis=-1)
    h = _layernorm(h + _L0_ffn_ref(h, L0_ffn_v_w, L0_ffn_v_b, L0_ffn_gate_w, L0_ffn_gate_b, L0_ffn_w1, L0_ffn_b1, L0_ffn_w2, L0_ffn_b2, L0_ffn_out_w, L0_ffn_out_b, L0_ffn_bk_scale), axis=-1)
    h = _layernorm(h + _L1_attn_ref(h, L1_attn_log_slope, L1_attn_Wq, L1_attn_Wk, L1_attn_Wv, L1_attn_Wo, L1_attn_Wg1, L1_attn_Wg2, L1_attn_ln_w, L1_attn_ln_b), axis=-1)
    h = _layernorm(h + _L1_ffn_ref(h, L1_ffn_moe0_W1, L1_ffn_moe0_b1, L1_ffn_moe0_W2, L1_ffn_moe0_b2, L1_ffn_A1_W, L1_ffn_A1_b, L1_ffn_A2_W, L1_ffn_A2_b, L1_ffn_G_W, L1_ffn_mids), axis=-1)
    return h

_drawn_inputs = setup_inputs


def setup_inputs(seed=0):
    import zlib

    import numpy as np

    out = dict(_drawn_inputs(seed))
    spreads = {'L0_tok_b_patch': (0.0, 0.1),
     'L0_tok_g1': (1.0, 0.2),
     'L0_tok_beta1': (0.0, 0.1),
     'L0_tok_b_out': (0.0, 0.1),
     'L0_tok_g2': (1.0, 0.2),
     'L0_tok_beta2': (0.0, 0.1),
     'L0_tok_b_ff1': (0.0, 0.1),
     'L0_tok_b_ff2': (0.0, 0.1),
     'L0_ffn_gate_b': (0.0, 0.1),
     'L0_ffn_b1': (0.0, 0.1),
     'L0_ffn_b2': (0.0, 0.1),
     'L0_ffn_out_b': (0.0, 0.1),
     'L0_ffn_bk_scale': (1.0, 0.2),
     'L1_attn_ln_w': (1.0, 0.2),
     'L1_attn_ln_b': (0.0, 0.1),
     'L1_ffn_moe0_b1': (0.0, 0.308),
     'L1_ffn_moe0_b2': (0.0, 0.1),
     'L1_ffn_A1_b': (0.0, 0.8),
     'L1_ffn_A2_b': (0.0, 0.277)}
    factors = {'L0_attn_wq': 8.0,
     'L0_attn_wk': 8.0,
     'L0_attn_wv': 8.0,
     'L0_attn_wo': 8.0,
     'L0_attn_w_gate': 8.0,
     'L0_attn_w_up': 8.0,
     'L0_ffn_v_w': 8.0,
     'L0_ffn_out_w': 2.934}
    for name, (base, spread) in spreads.items():
        noise = np.random.default_rng([zlib.crc32(name.encode()), seed]).standard_normal(out[name].shape)
        drawn = base * np.exp(spread * noise) if base else spread * noise
        out[name] = jnp.asarray(drawn.astype(out[name].dtype))
    for name, factor in factors.items():
        out[name] = (out[name] * factor).astype(out[name].dtype)
    return out
```

```python
from contextlib import ExitStack

import numpy as np

import concourse.bass as bass
from concourse import mybir

F32 = mybir.dt.float32
I32 = mybir.dt.int32
ALU = mybir.AluOpType
ACT = mybir.ActivationFunctionType
AX = mybir.AxisListType

P = 128
B, C, IMG, PATCH = 8, 3, 128, 16
GRID = IMG // PATCH
S = GRID * GRID
T = B * S
NT = T // P
D = 192
DB = D - P
CH = ((0, P), (P, DB))
H = 12
PAIRS = H // 2
DH0 = 64
DH = D // H
MLP = 768
NF = MLP // P
EA = 4
EM = 8
NCLS = 6
NC = NCLS * B
EPS = 1e-5
NEG = -1e30
R_FF1, R_MOE, R_M0, R_A1, R_LNA, R_LNB = 0, NF, NF * 9, NF * 10, NF * 15, NF * 15 + 4
NROWS = R_LNB + 4


def vit_tower(nc, a, out):
    ctx = ExitStack()
    with ctx:
        def sb(name, shape, dt=F32):
            return ctx.enter_context(nc.sbuf_tensor(name, shape, dt))

        def sem(name):
            return ctx.enter_context(nc.semaphore(name))

        def carve(region):
            at = [0]

            def take(*dims, rows=P):
                n = int(np.prod(dims))
                v = region[0:rows, at[0]:at[0] + n]
                at[0] += n
                assert at[0] <= region.shape[1], at[0]
                names = ["a", "b", "c", "d", "e"][:len(dims)]
                if len(dims) > 1:
                    v = v.rearrange(f"p ({' '.join(names)}) -> p {' '.join(names)}", **dict(zip(names, dims)))
                return v
            return take

        ps = ctx.enter_context(nc.psum_tensor("ps", [P, 8, 512], F32))

        ident = sb("ident", [P, P])
        tok = sb("tok", [P, NT, D])
        xn = sb("xn", [P, NT, D])
        xT = sb("xT", [P, 2, T])
        rowc = sb("rowc", [P, P])
        colc = sb("colc", [P, P])
        bn = sb("bn", [P, NT, 6])
        mv = sb("mv", [P, NT, 2])
        rstd = sb("rstd", [P, NT])
        neghalf = sb("neghalf", [P, NT])
        causal = sb("causal", [P, S])
        par_i = sb("par_i", [P, 1], I32)
        parity = sb("parity", [P, 2])
        bc = {n: sb("bc_" + n, [P, D]) for n in
              ("b_patch", "b_out", "b_ff2", "ln_w", "ln_b", "m0_b2")}
        gateb = sb("gateb", [P, EM])
        slopes = sb("slopes", [P, H])
        slope = sb("slope", [P, PAIRS])
        dist = sb("dist", [P, S])
        decay = sb("decay", [P, PAIRS, S])

        front = sb("front", [P, 22960])
        wide = sb("wide", [P, 9216])
        turned = sb("turned", [P, 9216])

        take = carve(front)
        wqkv = take(2, 3 * H * DH0)
        wout = take(PAIRS, D)
        wff1 = take(2, MLP)
        wff2 = take(NF, D)
        wpatch = take(2, C, D)
        oT0 = take(PAIRS, T)
        qbd = take(2, B, 2, S)
        kT0 = take(2, T)
        v0 = take(2, NT, P)
        p0 = take(2, B, S)
        pT0 = take(2, NT, P)
        mx0 = take(2, B)
        take = carve(front[:, 9600:])
        xr = take(C, 1024)
        xpT = take(2 * C, T)
        xq = take(C, GRID, P)
        ffh = carve(front[:, 9600 + PAIRS * T:])(NF, T)
        rawo = carve(front[:, 19600:])(2, EA, 2, PAIRS * DH)
        del take

        take = carve(front)
        qm = take(2, 2, B, 2, S)
        kT1 = take(2, 2, T)
        vbd = take(2, NT, PAIRS, 2, 2 * DH + 1)
        p1 = take(2, PAIRS, 2, S)
        pT1 = take(2, PAIRS, P)
        mx1 = take(2, 2 * PAIRS)
        rc1 = take(2, 2 * PAIRS)
        o1 = take(2, 2, PAIRS, DH)
        oT1 = take(2, T)
        fT = take(EA, 2, T)
        gsb = take(NT, D)
        last_at = 19600

        takew = carve(wide)
        raw = takew(2, EA, 4, D)
        rawg = takew(2, 2, MLP)
        takew = carve(wide)
        NSLOT = 3
        w1s = takew(NSLOT, 2, MLP)
        w2s = takew(NSLOT, NF, D)
        m0w2 = takew(NF, D)
        taket = carve(turned)
        wT = taket(2, EA, 3, D)
        woT = taket(2, EA, D)
        wguT = taket(EA, 2, 2 * D)

        take = carve(front[:, last_at:])
        m0w1 = take(2, MLP)
        wq3 = take(4, 2, D)
        wg1 = take(2, 16)
        wg2 = take(D, rows=16)
        take = carve(front)
        hT = take(2, NF, T)
        a1w = take(5, 2, MLP)
        a2w = take(5, NF, D)
        take = carve(turned)
        q3 = take(2, T)
        km3 = take(2, B, 2, S)
        ksb = take(2, T)
        xd = carve(wide[:, 2048:])(2, B, 2, S)
        vbd3 = take(B, PAIRS, 2, DH)
        E3a = take(2, PAIRS, 2, S)
        g1T = take(T, rows=16)
        gate3 = take(NT, D)
        E3 = E3a, carve(wide)(2, PAIRS, 2, S)
        take = carve(turned)
        hcls = take(5, NF, NC)
        hmix = take(5, NF, NC)
        small = sb("small", [P, 3540])
        take = carve(small)
        gw = take(2, EM)
        gwc = take(2, NCLS, 2)
        vw = take(2, 1)
        vb = take(1)
        lg = take(NT, EM)
        pr = take(NT, EM)
        cmp = take(NT, EM, EM)
        ceq = take(NT, EM, EM)
        lower = take(EM, EM)
        lmx = take(NT)
        comb = take(NT, EM)
        combT = take(T)
        b2m = take(D)
        ow3 = take(D)
        bk3 = take(D)
        clsx = take(D)
        xcls = take(2, NC)
        cls_l = take(2, NC)
        cls_m = take(2, NC)
        cls_s = take(NC)
        mcls = take(5, NC)
        a2b = take(5, D)
        del take
        line = sb("line", [16, 5, T])
        vrow, vrev, frow = line[0:1, 0, :], line[0:1, 1, :], line[0:3, 2, :]
        take = carve(line[0:16, 3:5, :].rearrange("p a b -> p (a b)"))
        chA = take(S, rows=16)
        alt = take(S, rows=16)
        chr_ = take(4, rows=16)
        chB = take(S, 2, rows=16)
        chS = take(S, 2, rows=16)
        chE = take(S, 2, rows=8)
        chG = take(2, S, rows=8)
        chQ = take(2, S, rows=8)
        chF = take(2, S, rows=8)

        names = """x_in wpatch_in rows_in bcast_in wqkv_in wout_in ff_in raw_in rawg_in small_in
            s3_in m0_in a_in rowmv_in chE_in chF_in out_done
            ident_made xq_done rawo_done xd_done xcls_done consts_made rows_zero colc_mm colc_done
            xr_T xpT_act xpT_dve patch_mm
            wt_mm wt_act wt_dve
            var_ready rstd_ready ln_done xT_mm xT_act xT_dve
            q0_mm k0_mm v0_mm q0_done kv0_done s0_mm s0_read sub0 exp0 p0_done t0_mm pT0_done
            pv0_mm oT0_done zeros_made
            tok_mm tok_done bias_added
            h_mm h_act y_mm y_done
            qk1_mm qk1_dve qk1_act v1_mm v1_done s1_mm s1_read sub1 exp1 t1_mm pT1_done pv1_mm o1_done
            ot1_mm ot1_done wo1_mm fT_act fT_dve gu_mm silu_done
            lg_mm lg_sub lg_exp comb_done combT_mm combT_done v_mm chain_in spec_ready feat_out extra_mm
            gate1_mm gate1_done gate3_mm gate3_done q3_mm q3_done k3_done v3_mm v3_done km_done
            e3_mm e3_done pv3_mm og_done decay_exp decay_done dist_ready
            cl_mm cl_sub cl_exp mcls_done hc_mm hc_add hc_done hmix_done cls_mm clsx_mm cls_out_ready
            fin_ready dve_step pool_step zero_cls""".split()
        s = {n: sem(n) for n in names}
        slot_in = [sem(f"slot_in{i}") for i in range(NSLOT)]

        def col(i):
            return colc[:, i:i + 1]

        def two(bank):
            return ps[:, bank:bank + 2, 0:2 * D]

        def two_t(bank, i):
            return ps[:, bank + i // 2, (i % 2) * D:(i % 2) * D + D]

        def pairs_of(x):
            return x.rearrange("p (a b) d -> p a (b d)", a=2)

        tok2, xn2 = pairs_of(tok[:, :, :]), pairs_of(xn[:, :, :])

        def patch_in(j):
            return ps[:, j, :].rearrange("p (w b h) -> p h b w", w=4, h=2)

        def patch_out(j):
            c, half = divmod(j, 2)
            v = xpT[:, 2 * c:2 * c + 2, :].rearrange("p h (b w) -> p h b w", w=GRID)
            return v[:, :, :, 4 * half:4 * half + 4]

        block = ctx.enter_context(nc.Block())

        @block.sync
        def _(sp):
            def load(dst, src, name):
                sp.dma_start(dst, src).then_inc(s[name], 16)

            for b in range(B):
                load(xr[16 * b:16 * b + 16], a["x"][b].rearrange("c (hh r) w -> hh c (r w)", r=8), "x_in")
            load(wpatch.rearrange("p a c n -> p a (c n)"),
                 a["w_patch"].rearrange("(ph k c) n -> k ph (c n)", ph=2, c=C), "wpatch_in")
            sp.wait_ge(s["rows_zero"], 1)
            for r, name in ((R_FF1, "b_ff1"), (R_M0, "m0_b1")):
                load(rowc[r:r + NF], a[name].rearrange("(f p) -> f p", p=P), "rows_in")
            load(rowc[R_MOE:R_MOE + NF * EM], a["b1"].rearrange("e (f p) -> (e f) p", p=P), "rows_in")
            load(rowc[R_A1:R_A1 + NF * 5], a["a1b"].rearrange("e (f p) -> (e f) p", p=P), "rows_in")
            for k, name in enumerate(("g1", "beta1", "g2", "beta2")):
                g = a[name].rearrange("(o n) -> o n", o=1)
                load(rowc[R_LNA + k:R_LNA + k + 1], g[:, 0:P], "rows_in")
                load(rowc[R_LNB + k:R_LNB + k + 1, 0:DB], g[:, P:D], "rows_in")
            for n in ("b_patch", "b_out", "b_ff2", "ln_w", "ln_b", "m0_b2"):
                load(bc[n][:, :], a[n].partition_broadcast(P), "bcast_in")
            load(slopes[:, :], a["slope"].partition_broadcast(P), "bcast_in")
            load(wqkv[:, 0], a["w_qkv"][0:P], "wqkv_in")
            load(wqkv[0:DB, 1], a["w_qkv"][P:D], "wqkv_in")
            for m, name in enumerate(("wq", "wk", "wv", "wo")):
                w = a[name].rearrange("e o i -> o e i")
                load(raw[:, 0, :, m, :], w[0:P], "raw_in")
                load(raw[0:DB, 1, :, m, :], w[P:D], "raw_in")
            for m, name in enumerate(("w_gate", "w_up")):
                load(rawg[:, 0, m, :], a[name][0:P], "rawg_in")
                load(rawg[0:DB, 1, m, :], a[name][P:D], "rawg_in")
            load(wout, a["w_out"].rearrange("(f p) n -> p f n", p=P), "wout_in")
            load(wff1[:, 0], a["w_ff1"][0:P], "ff_in")
            load(wff1[0:DB, 1], a["w_ff1"][P:D], "ff_in")
            load(wff2, a["w_ff2"].rearrange("(f p) n -> p f n", p=P), "ff_in")
            for c, (r0, n) in enumerate(CH):
                load(gw[0:n, c, :], a["gate_w"][r0:r0 + n], "small_in")
                load(vw[0:n, c, :], a["v_w"].rearrange("(p o) -> p o", o=1)[r0:r0 + n], "small_in")
                load(gwc[0:n, c, :, :], a["gcls"].rearrange("i d q -> d i q")[r0:r0 + n], "small_in")
            load(vb[0:1], a["v_b"].rearrange("(p o) -> p o", o=1), "small_in")
            load(gateb[:, :], a["gate_b"].partition_broadcast(P), "small_in")
            load(b2m[0:EM], a["b2"], "small_in")
            load(ow3[0:2], a["out_w"], "small_in")
            load(ow3[2:3], a["out_b"].rearrange("(o n) -> o n", o=1), "small_in")
            load(bk3[0:3], a["bk"].partition_broadcast(3), "small_in")
            load(a2b[0:1], a["a2b"].rearrange("(o e) n -> o e n", o=1), "small_in")
            sp.wait_ge(s["y_mm"], 1)
            for m, name in enumerate(("Wq", "Wk", "Wv", "Wo")):
                for c, (r0, n) in enumerate(CH):
                    load(wq3[0:n, m, c, :], a[name][r0:r0 + n], "s3_in")
            for c, (r0, n) in enumerate(CH):
                load(wg1[0:n, c, :], a["Wg1"][r0:r0 + n], "s3_in")
                load(m0w1[0:n, c], a["m0w1"][r0:r0 + n], "m0_in")
            load(wg2, a["Wg2"], "s3_in")
            sp.wait_ge(s["wt_mm"], EA)
            load(m0w2, a["m0w2"].rearrange("(f p) n -> p f n", p=P), "m0_in")
            for e in range(EM):
                k = e % NSLOT
                if e >= NSLOT:
                    sp.wait_ge(s["y_mm"], 1 + e - NSLOT + 1)
                for c, (r0, n) in enumerate(CH):
                    sp.dma_start(w1s[0:n, k, c], a["w1"][e, r0:r0 + n]).then_inc(slot_in[k], 16)
                sp.dma_start(w2s[:, k], a["w2"][e].rearrange("(f p) n -> p f n", p=P)).then_inc(slot_in[k], 16)
                if e == NSLOT - 1:
                    sp.wait_ge(s["gu_mm"], NT)
                    sp.wait_ge(s["silu_done"], NT)
                    sp.wait_ge(s["ln_done"], 3)
                    for x in range(5):
                        for c, (r0, n) in enumerate(CH):
                            load(a1w[0:n, x, c], a["a1w"][x, r0:r0 + n], "a_in")
                        load(a2w[:, x], a["a2w"][x].rearrange("(f p) n -> p f n", p=P), "a_in")
                    sp.wait_ge(s["chain_in"], 1)
                    load(chA[0:8], vrow.rearrange("o (b n) -> o b n", n=S), "rowmv_in")
                    load(chA[8:16], vrev.rearrange("o (b n) -> o b n", n=S), "rowmv_in")
                    sp.wait_ge(s["chain_in"], 2)
                    load(chE, chS[8:16], "chE_in")
                    sp.wait_ge(s["feat_out"], 1)
                    for k2 in range(2):
                        load(frow[k2:k2 + 1].rearrange("o (b n) -> o b n", n=S), chF[:, k2, :], "chF_in")
            o3 = out
            sp.wait_ge(s["fin_ready"], 1)
            for b in range(B):
                r = S * (b % 2)
                sp.dma_start(o3[b, NCLS:S, :], xn[r + NCLS:r + S, b // 2, :]).then_inc(s["out_done"], 16)
            sp.wait_ge(s["fin_ready"], 2)
            for i in range(NCLS):
                sp.dma_start(o3[:, i, :], clsx[i * B:(i + 1) * B, :]).then_inc(s["out_done"], 16)
            sp.wait_ge(s["out_done"], 16 * (B + NCLS))

        @block.gpsimd
        def _(pool):
            steps = [0]

            def link(ins):
                steps[0] += 1
                ins.then_inc(s["pool_step"], 1)
                pool.wait_ge(s["pool_step"], steps[0])

            told = {}

            def tell(ins, name):
                told[name] = told.get(name, 0) + 1
                ins.then_inc(s[name], 1)
                pool.wait_ge(s[name], told[name])

            link(pool.memset(ident[:, :], 0.0))
            tell(pool.affine_select(out=ident[:, :], in_=ident[:, :], compare_op=ALU.not_equal, fill=1.0, base=0,
                                    pattern=[[-1, P]], channel_multiplier=1), "ident_made")
            tell(pool.memset(rowc[:, :], 0.0), "rows_zero")
            link(pool.memset(neghalf[:, :], -0.5))
            link(pool.iota(par_i[:, :], pattern=[[0, 1]], base=0, channel_multiplier=1))
            link(pool.memset(causal[:, :], 0.0))
            for h in range(2):
                r = slice(64 * h, 64 * h + 64)
                link(pool.affine_select(out=causal[r], in_=causal[r], compare_op=ALU.is_ge, fill=NEG, base=0,
                                        pattern=[[-1, S]], channel_multiplier=1))
                link(pool.iota(dist[r, :], pattern=[[1, S]], base=0, channel_multiplier=-1,
                               allow_small_or_imprecise_dtypes=True))
            link(pool.memset(lower, 1.0))
            link(pool.affine_select(out=lower, in_=lower, compare_op=ALU.is_gt, fill=0.0, base=0,
                                    pattern=[[1, EM], [-1, EM]], channel_multiplier=0))
            link(pool.memset(alt, -1.0))
            link(pool.memset(alt.rearrange("p (n c) -> p n c", c=2)[:, :, 0], 1.0))
            link(pool.memset(frow, 1.0))
            tell(pool.memset(mcls, 0.0), "consts_made")
            pool.wait_ge(s["patch_mm"], 2)
            for k in range(2):
                for h in range(2):
                    link(pool.memset(qbd[64 * h:64 * h + 64, k, :, 1 - h, :], 0.0))
            tell(pool.memset(qbd[64:P, 0, 0:1, 0, :], 0.0), "zeros_made")

            pool.wait_ge(s["raw_in"], 16 * 8)
            for c, (r0, n) in enumerate(CH):
                for e in range(EA):
                    ins = pool.tensor_copy(rawo[0:n, c, e].rearrange("p h (a d) -> p h a d", a=PAIRS),
                                           raw[0:n, c, e, 3, :].rearrange("p (a h d) -> p h a d", a=PAIRS, h=2))
            tell(ins, "rawo_done")

            lns = [0]

            def rsqrt(n=NT, rows=P):
                lns[0] += 1
                pool.wait_ge(s["var_ready"], lns[0])
                link(pool.tensor_scalar(rstd[0:rows, 0:n], mv[0:rows, 0:n, 1], EPS, None, ALU.add))
                tell(pool.tensor_tensor(rstd[0:rows, 0:n], rstd[0:rows, 0:n], neghalf[0:rows, 0:n], ALU.pow),
                     "rstd_ready")

            def add_bias(name, n):
                pool.wait_ge(s["ln_done"], n)
                if n == 1:
                    pool.wait_ge(s["bcast_in"], 7 * 16)
                for i in range(NT):
                    ins = pool.tensor_tensor(tok[:, i, :], tok[:, i, :], bc[name][:, :], ALU.add)
                tell(ins, "bias_added")

            rsqrt()
            add_bias("b_out", 1)
            rsqrt()
            add_bias("b_ff2", 2)
            pool.wait_ge(s["tok_done"], 3)
            link(pool.memset(vbd, 0.0))
            for k in range(2):
                for im in range(2):
                    r = slice(64 * im, 64 * im + 64)
                    ins = pool.memset(vbd[r, k, :, :, im, 2 * DH:2 * DH + 1], 1.0)
                    if (k, im) != (1, 1):
                        link(ins)
            tell(ins, "zeros_made")
            pool.wait_ge(s["decay_exp"], 1)
            for h in range(2):
                r = slice(64 * h, 64 * h + 64)
                ins = pool.affine_select(out=decay[r], in_=decay[r], compare_op=ALU.is_ge, fill=0.0, base=0,
                                         pattern=[[0, PAIRS], [1, S]], channel_multiplier=-1)
                if h == 0:
                    link(ins)
            tell(ins, "decay_done")
            rsqrt()
            pool.wait_ge(s["gu_mm"], NT)
            tell(pool.memset(vbd3, 0.0), "zeros_made")
            rsqrt()
            rsqrt()
            rsqrt()
            pool.wait_ge(s["tok_done"], 6)
            tell(pool.memset(hmix, 0.0), "zeros_made")
            rsqrt()
            rsqrt(1, NC)

        @block.scalar
        def _(act):
            for j in range(3):
                act.wait_ge(s["xr_T"], 2 * j + 2)
                act.activation(patch_out(2 * j + 1), patch_in(2 * j + 1), ACT.Copy).then_inc(s["xpT_act"], 1)

            def turned_weights(e):
                act.wait_ge(s["wt_mm"], e + 1)
                act.activation(wT[:, 0, e, 0:2, :], ps[:, 0, 0:2 * D].rearrange("p (a b) -> p a b", a=2), ACT.Copy)
                act.activation(wT[:, 0, e, 2, :], ps[:, 1, 0:D], ACT.Copy)
                act.activation(wT[0:DB, 1, e, 2, :], ps[0:DB, 1, D:2 * D], ACT.Copy)
                act.activation(wguT[:, e, 0, :], ps[:, 4, 0:2 * D], ACT.Copy).then_inc(s["wt_act"], 1)

            turned_weights(0)
            turned_weights(1)
            act.wait_ge(s["colc_done"], 1)
            act.wait_ge(s["xT_mm"], 1)
            act.activation(xT[:, 0, :], ps[:, 6, :], ACT.Identity, bias=col(R_LNA + 1),
                           scale=col(R_LNA)).then_inc(s["xT_act"], 1)

            def exp0(hp):
                act.wait_ge(s["sub0"], hp + 1)
                act.activation(p0[:, hp % 2], p0[:, hp % 2], ACT.Exp, scale=DH0 ** -0.5).then_inc(s["exp0"], 1)

            def pT_out(hp):
                act.wait_ge(s["t0_mm"], hp + 1)
                if hp >= 2:
                    act.wait_ge(s["pv0_mm"], hp - 1)
                act.activation(pT0[:, hp % 2].rearrange("p a b -> p (a b)"), ps[:, 5, :],
                               ACT.Copy).then_inc(s["pT0_done"], 1)

            act.wait_ge(s["zeros_made"], 1)
            for hp in range(PAIRS):
                act.wait_ge(s["q0_mm"], hp + 1)
                if hp >= 2:
                    act.wait_ge(s["s0_mm"], hp - 1)
                for h in range(2):
                    r = slice(64 * h, 64 * h + 64)
                    ins = act.activation(qbd[r, hp % 2, :, h, :],
                                         ps[r, 0, :].rearrange("p (b i) -> p b i", b=B), ACT.Copy)
                ins.then_inc(s["q0_done"], 1)
                exp0(hp)
                if hp >= 1:
                    pT_out(hp - 1)
            pT_out(PAIRS - 1)
            turned_weights(2)
            turned_weights(3)
            act.wait_ge(s["xT_mm"], 2)
            act.activation(xT[:, 0, :], ps[:, 6, :], ACT.Identity, bias=col(R_LNA + 3),
                           scale=col(R_LNA + 2)).then_inc(s["xT_act"], 1)

            jobs = [0]

            def hidden(dst, bias0, func):
                for f in range(NF):
                    bank = jobs[0] % 4
                    jobs[0] += 1
                    act.wait_ge(s["h_mm"], jobs[0])
                    act.activation(dst[:, f, :], ps[:, bank, :], func, bias=col(bias0 + f)).then_inc(s["h_act"], 1)

            hidden(ffh, R_FF1, ACT.Gelu)
            act.wait_ge(s["xT_mm"], 3)
            act.activation(xT[:, 0, :], ps[:, 6, :], ACT.Copy).then_inc(s["xT_act"], 1)

            def k_out(e):
                for c, (r0, n) in enumerate(CH):
                    act.wait_ge(s["qk1_mm"], 4 * e + 2 * c + 2)
                    if c == 0 and e >= 2:
                        act.wait_ge(s["s1_mm"], NT * (e - 1))
                    act.activation(kT1[0:n, e % 2, c, :], ps[0:n, 4 + 2 * c, :], ACT.Copy).then_inc(s["qk1_act"], 1)

            def exp1(e, t):
                n = NT * e + t
                act.wait_ge(s["sub1"], n + 1)
                act.activation(p1[:, n % 2], p1[:, n % 2], ACT.Exp).then_inc(s["exp1"], 1)

            def pT1_out(e, t):
                n = NT * e + t
                act.wait_ge(s["t1_mm"], n + 1)
                if n >= 2:
                    act.wait_ge(s["pv1_mm"], n - 1)
                act.activation(pT1[:, n % 2].rearrange("p (a b) c -> p a (b c)", a=2), ps[:, 0:2, 0:3 * P],
                               ACT.Copy).then_inc(s["pT1_done"], 1)

            k_out(0)
            exp1(0, 0)
            for e in range(EA):
                for t in range(NT):
                    if t < NT - 1:
                        exp1(e, t + 1)
                    elif e < EA - 1:
                        k_out(e + 1)
                    pT1_out(e, t)
                act.wait_ge(s["wo1_mm"], 2 * e + 1)
                act.activation(fT[:, e, 0, :], ps[:, 0, :], ACT.Copy).then_inc(s["fT_act"], 1)
                if e < EA - 1:
                    exp1(e + 1, 0)
            act.wait_ge(s["dist_ready"], 1)
            for p in range(PAIRS):
                ins = act.activation(decay[:, p, :], dist[:, :], ACT.Exp, scale=slope[:, p:p + 1])
            ins.then_inc(s["decay_exp"], 1)
            for i in range(NT):
                act.wait_ge(s["gu_mm"], i + 1)
                act.activation(gsb[:, i, :], ps[:, i, 0:D], ACT.Silu).then_inc(s["silu_done"], 1)
            act.wait_ge(s["xT_mm"], 4)
            act.activation(xT[:, 0, :], ps[:, 6, :], ACT.Copy).then_inc(s["xT_act"], 1)
            act.wait_ge(s["lg_sub"], 1)
            act.activation(lg, lg, ACT.Exp).then_inc(s["lg_exp"], 1)
            for e in range(EM):
                if e >= 2:
                    act.wait_ge(s["y_mm"], 1 + e - 1)
                hidden(hT[:, e % 2], R_MOE + NF * e, ACT.Gelu_apprx_tanh)
            act.wait_ge(s["xT_mm"], 5)
            act.activation(xT[:, 0, :], ps[:, 6, :], ACT.Copy).then_inc(s["xT_act"], 1)
            act.wait_ge(s["gate1_mm"], 1)
            act.activation(g1T, ps[0:16, 7, :], ACT.Copy).then_inc(s["gate1_done"], 1)
            for c, (r0, n) in enumerate(CH):
                act.wait_ge(s["q3_mm"], 2 * c + 1)
                act.activation(q3[0:n, c, :], ps[0:n, 2 * c, :], ACT.Silu).then_inc(s["q3_done"], 1)
                act.wait_ge(s["q3_mm"], 2 * c + 2)
                act.activation(ksb[0:n, c, :], ps[0:n, 2 * c + 1, :], ACT.Silu).then_inc(s["k3_done"], 1)
            act.wait_ge(s["zeros_made"], 3)
            for j in range(B // 2):
                act.wait_ge(s["v3_mm"], j + 1)
                bank = 4 + j % 2
                for h in range(2):
                    r = slice(64 * h, 64 * h + 64)
                    src = ps[r, bank, 0:2 * D].rearrange("p (m a h d) -> p m a h d", m=2, a=PAIRS, h=2)
                    for m in range(2):
                        ins = act.activation(vbd3[r, 2 * j + m, :, h, :], src[:, m, :, h, :], ACT.Silu)
                ins.then_inc(s["v3_done"], 1)
            act.wait_ge(s["gate3_mm"], 1)
            act.activation(pairs_of(gate3), two(6), ACT.Sigmoid).then_inc(s["gate3_done"], 1)
            act.wait_ge(s["xT_mm"], 6)
            act.activation(xT[:, 0, :], ps[:, 6, :], ACT.Copy).then_inc(s["xT_act"], 1)
            act.wait_ge(s["xT_mm"], 7)
            act.activation(xT[:, 0, :], ps[:, 6, :], ACT.Copy).then_inc(s["xT_act"], 1)
            act.wait_ge(s["cl_sub"], 1)
            act.activation(cls_l, cls_l, ACT.Exp).then_inc(s["cl_exp"], 1)
            hidden(hT[:, 0], R_M0, ACT.Gelu)
            for x in range(5):
                act.wait_ge(s["hc_add"], x + 1)
                act.activation(hcls[:, x], hcls[:, x], ACT.Gelu).then_inc(s["hc_done"], 1)

        @block.vector
        def _(dve):
            steps = [0]

            def link(ins):
                steps[0] += 1
                ins.then_inc(s["dve_step"], 1)
                dve.wait_ge(s["dve_step"], steps[0])

            dve.wait_ge(s["x_in"], 16 * B)
            for c in range(C):
                dve.tensor_copy(xq[:, c].rearrange("p w (r q) -> p r w q", r=8),
                                xr[:, c, :].rearrange("p (r w q) -> p r w q", r=8, w=GRID)).then_inc(s["xq_done"], 1)
            for j in range(3):
                dve.wait_ge(s["xr_T"], 2 * j + 1)
                dve.tensor_copy(patch_out(2 * j), patch_in(2 * j)).then_inc(s["xpT_dve"], 1)
            dve.wait_ge(s["colc_mm"], 1)
            dve.tensor_copy(colc[:, 0:NROWS], ps[:, 7, 384:384 + NROWS]).then_inc(s["colc_done"], 1)
            dve.wait_ge(s["consts_made"], 1)
            link(dve.tensor_scalar(par_i[:, :], par_i[:, :], 4, 1, ALU.logical_shift_right, ALU.bitwise_and))
            link(dve.tensor_copy(parity[:, 1:2], par_i[:, :]))
            link(dve.tensor_scalar(parity[:, 0:1], parity[:, 1:2], -1.0, 1.0, ALU.mult, ALU.add))
            link(dve.tensor_scalar(dist[:, :], dist[:, :], 0.0, None, ALU.max))

            lns = [0]

            def normalise(src, dst, n=NT, rows=P, scaled=None):
                lns[0] += 1
                for i in range(n):
                    ins = dve.bn_stats(bn[0:rows, i, :], src(i))
                link(ins)
                for i in range(n):
                    ins = dve.bn_aggr(mv[0:rows, i, :], bn[0:rows, i, :])
                ins.then_inc(s["var_ready"], 1)
                dve.wait_ge(s["rstd_ready"], lns[0])
                for i in range(n):
                    ins = dve.tensor_scalar(dst(i), src(i), mv[0:rows, i, 0:1], rstd[0:rows, i:i + 1],
                                            ALU.subtract, ALU.mult)
                return ins

            def of(x):
                return lambda i: x[:, i, :]

            dve.wait_ge(s["bcast_in"], 7 * 16)
            for j in range(2):
                dve.wait_ge(s["patch_mm"], j + 1)
                ins = dve.tensor_tensor(tok[:, 2 * j:2 * j + 2, :],
                                        ps[:, 6 + j, 0:2 * D].rearrange("p (a b) -> p a b", a=2),
                                        bc["b_patch"][:, :].unsqueeze(1).to_broadcast([P, 2, D]), ALU.add)
            link(ins)
            for h in range(2):
                r = slice(64 * h, 64 * h + 64)
                dve.tensor_copy(slope[r, :], slopes[r, :].rearrange("p (a h) -> p h a", h=2)[:, h])
            normalise(of(tok), of(xn)).then_inc(s["ln_done"], 1)

            def turned_weights(e):
                dve.wait_ge(s["wt_mm"], e + 1)
                dve.tensor_copy(wT[0:DB, 1, e, 0:2, :], ps[0:DB, 2, 0:2 * D].rearrange("p (a b) -> p a b", a=2))
                dve.tensor_copy(woT[0:96, :, e, :], ps[0:96, 3, 0:2 * D].rearrange("p (a b) -> p a b", a=2))
                dve.tensor_copy(wguT[0:DB, e, 1, :], ps[0:DB, 5, 0:2 * D]).then_inc(s["wt_dve"], 1)

            turned_weights(0)
            turned_weights(1)
            dve.wait_ge(s["xT_mm"], 1)
            dve.tensor_scalar(xT[0:DB, 1, :], ps[0:DB, 7, :], col(R_LNB)[0:DB], col(R_LNB + 1)[0:DB],
                              ALU.mult, ALU.add).then_inc(s["xT_dve"], 1)

            def kv0(hp):
                k = hp % 2
                dve.wait_ge(s["k0_mm"], hp + 1)
                if hp >= 2:
                    dve.wait_ge(s["s0_mm"], hp - 1)
                dve.tensor_copy(kT0[:, k, :], ps[:, 1, :]).then_inc(s["kv0_done"], 1)
                dve.wait_ge(s["v0_mm"], hp + 1)
                if hp >= 2:
                    dve.wait_ge(s["pv0_mm"], hp - 1)
                dve.tensor_copy(v0[:, k].rearrange("p a b -> p (a b)"), ps[:, 2, :]).then_inc(s["kv0_done"], 1)

            def softmax0_in(hp):
                k = hp % 2
                dve.wait_ge(s["s0_mm"], hp + 1)
                if hp >= 2:
                    dve.wait_ge(s["t0_mm"], hp - 1)
                sc = ps[:, 3 + k, :].rearrange("p (b j) -> p b j", b=B)
                link(dve.tensor_reduce(mx0[:, 0, :], sc, AX.X, ALU.max))
                dve.tensor_tensor(p0[:, k], sc, mx0[:, 0, :].unsqueeze(2).to_broadcast([P, B, S]),
                                  ALU.subtract).then_inc(s["sub0"], 1)

            def softmax0_out(hp):
                k = hp % 2
                dve.wait_ge(s["exp0"], hp + 1)
                link(dve.tensor_reduce(mx0[:, 1, :], p0[:, k], AX.X, ALU.add))
                link(dve.reciprocal(mx0[:, 1, :], mx0[:, 1, :]))
                dve.tensor_tensor(p0[:, k], p0[:, k], mx0[:, 1, :].unsqueeze(2).to_broadcast([P, B, S]),
                                  ALU.mult).then_inc(s["p0_done"], 1)

            def out0(hp):
                dve.wait_ge(s["pv0_mm"], hp + 1)
                dve.tensor_copy(oT0[:, hp, :].rearrange("p (t m i) -> p m t i", t=NT, m=2),
                                ps[:, 6:8, 0:NT * S].rearrange("p m (t i) -> p m t i", t=NT)).then_inc(s["oT0_done"], 1)

            for hp in range(PAIRS):
                kv0(hp)
                softmax0_in(hp)
                if hp >= 1:
                    out0(hp - 1)
                softmax0_out(hp)
            out0(PAIRS - 1)

            toks = [0]

            def residual(bank, n):
                toks[0] += 1
                dve.wait_ge(s["tok_mm"], n)
                ins = dve.tensor_tensor(tok2, tok2, two(bank), ALU.add)
                ins.then_inc(s["tok_done"], 1)
                dve.wait_ge(s["tok_done"], toks[0])

            dve.wait_ge(s["bias_added"], 1)
            residual(0, 1)
            normalise(of(tok), of(xn)).then_inc(s["ln_done"], 1)
            turned_weights(2)
            turned_weights(3)
            dve.wait_ge(s["xT_mm"], 2)
            dve.tensor_scalar(xT[0:DB, 1, :], ps[0:DB, 7, :], col(R_LNB + 2)[0:DB], col(R_LNB + 3)[0:DB],
                              ALU.mult, ALU.add).then_inc(s["xT_dve"], 1)
            dve.wait_ge(s["bias_added"], 2)
            residual(4, 2)
            dve.wait_ge(s["xT_mm"], 3)
            dve.tensor_copy(xT[0:DB, 1, :], ps[0:DB, 7, :]).then_inc(s["xT_dve"], 1)
            toks[0] += 1
            dve.engine_nop().then_inc(s["tok_done"], 1)

            def q_out(e):
                for c, (r0, n) in enumerate(CH):
                    dve.wait_ge(s["qk1_mm"], 4 * e + 2 * c + 1)
                    if c == 0 and e >= 2:
                        dve.wait_ge(s["s1_mm"], NT * (e - 1))
                    for h in range(2):
                        ins = dve.tensor_scalar(qm[0:n, e % 2, c, :, h, :],
                                                ps[0:n, 3 + 2 * c, :].rearrange("p (b i) -> p b i", b=B),
                                                parity[0:n, h:h + 1], None, ALU.mult)
                    ins.then_inc(s["qk1_dve"], 1)

            def v_out(e):
                for j in range(2):
                    dve.wait_ge(s["v1_mm"], 2 * e + j + 1)
                    if j == 0 and e >= 2:
                        dve.wait_ge(s["pv1_mm"], NT * (e - 1))
                    for im in range(2):
                        r = slice(64 * im, 64 * im + 64)
                        for m in range(2):
                            ins = dve.tensor_copy(
                                vbd[r, e % 2, 2 * j + m, :, im, 0:2 * DH],
                                ps[r, 3 + j, m * D:m * D + D].rearrange("p (a d) -> p a d", a=PAIRS))
                    ins.then_inc(s["v1_done"], 1)

            def softmax1_in(e, t):
                n = NT * e + t
                k = n % 2
                dve.wait_ge(s["s1_mm"], n + 1)
                if n >= 2:
                    dve.wait_ge(s["t1_mm"], n - 1)
                pk = p1[:, k].rearrange("p a m j -> p (a m) j")
                for p, banks in ((0, 4), (4, PAIRS - 4)):
                    at = p // 4 * P
                    ins = dve.scalar_tensor_tensor(
                        p1[:, k, p:p + banks].rearrange("p a m j -> p a (m j)"), ps[:, 3:3 + banks, at:at + P],
                        DH ** -0.5, causal[:, :].unsqueeze(1).to_broadcast([P, 2 * banks, S]), ALU.mult, ALU.add)
                ins.then_inc(s["s1_read"], 1)
                dve.wait_ge(s["s1_read"], n + 1)
                link(dve.tensor_reduce(mx1[:, k, :], pk, AX.X, ALU.max))
                dve.tensor_tensor(pk, pk, mx1[:, k, :].unsqueeze(2).to_broadcast([P, 2 * PAIRS, S]),
                                  ALU.subtract).then_inc(s["sub1"], 1)

            def out1(e, t):
                n = NT * e + t
                k = n % 2
                dve.wait_ge(s["pv1_mm"], n + 1)
                if n >= 2:
                    dve.wait_ge(s["ot1_mm"], n - 1)
                o = ps[:, 7, 0:PAIRS * 2 * (2 * DH + 1)].rearrange("p (a m d) -> p m a d", a=PAIRS, m=2)
                rk = rc1[:, k, :].rearrange("p (m a) -> p m a", m=2)
                link(dve.reciprocal(rk, o[:, :, :, 2 * DH]))
                for h in range(2):
                    r = slice(64 * h, 64 * h + 64)
                    ins = dve.tensor_tensor(o1[r, k], o[r, :, :, h * DH:(h + 1) * DH],
                                            rk[r].unsqueeze(3).to_broadcast([64, 2, PAIRS, DH]), ALU.mult)
                ins.then_inc(s["o1_done"], 1)

            def oT_out(e, j):
                dve.wait_ge(s["ot1_mm"], NT * e + 2 * j + 2)
                if j == 0 and e >= 1:
                    dve.wait_ge(s["wo1_mm"], 2 * e)
                dve.tensor_copy(
                    oT1[0:96, :, 256 * j:256 * j + 256].rearrange("p h (m i) -> p h m i", m=4),
                    ps[0:96, 2, :].rearrange("p (m h i) -> p h m i", m=4, h=2)).then_inc(s["ot1_done"], 1)

            dve.wait_ge(s["zeros_made"], 2)
            q_out(0)
            v_out(0)
            softmax1_in(0, 0)
            for e in range(EA):
                for t in range(NT):
                    if t < NT - 1:
                        softmax1_in(e, t + 1)
                    elif e < EA - 1:
                        q_out(e + 1)
                        v_out(e + 1)
                    out1(e, t)
                    if t == 2:
                        oT_out(e, 0)
                if e < EA - 1:
                    softmax1_in(e + 1, 0)
                oT_out(e, 1)
                dve.wait_ge(s["wo1_mm"], 2 * e + 2)
                dve.tensor_copy(fT[0:DB, e, 1, :], ps[0:DB, 1, :]).then_inc(s["fT_dve"], 1)
            dve.engine_nop().then_inc(s["dist_ready"], 1)
            for i in range(NT):
                dve.wait_ge(s["silu_done"], i + 1)
                ins = dve.tensor_tensor(gsb[:, i, :], gsb[:, i, :], ps[:, i, D:2 * D], ALU.mult)
            link(ins)
            link(dve.tensor_tensor(tok[:, :, :], tok[:, :, :], gsb, ALU.add))
            normalise(of(tok), of(xn)).then_inc(s["ln_done"], 1)
            dve.wait_ge(s["xT_mm"], 4)
            dve.tensor_copy(xT[0:DB, 1, :], ps[0:DB, 7, :]).then_inc(s["xT_dve"], 1)

            dve.wait_ge(s["small_in"], 16 * 13)
            dve.wait_ge(s["v_mm"], 1)
            link(dve.tensor_scalar(vrow, ps[0:1, 4, :], vb[0:1], 3.0, ALU.add, ALU.min))
            link(dve.tensor_scalar(vrow, vrow, -3.0, -2.0, ALU.max, ALU.add))
            vr = vrow.rearrange("o (b n) -> o b n", n=S)
            dve.tensor_copy(vrev.rearrange("o (b n) -> o b n", n=S), vr[:, :, ::-1]).then_inc(s["chain_in"], 1)
            dve.wait_ge(s["lg_mm"], 1)
            gb = gateb[:, :].unsqueeze(1).to_broadcast([P, NT, EM])
            link(dve.tensor_tensor(lg, ps[:, 5, 0:NT * EM].rearrange("p (a b) -> p a b", a=NT), gb, ALU.add))
            link(dve.tensor_reduce(lmx, lg, AX.X, ALU.max))
            dve.tensor_tensor(lg, lg, lmx.unsqueeze(2).to_broadcast([P, NT, EM]),
                              ALU.subtract).then_inc(s["lg_sub"], 1)
            dve.wait_ge(s["lg_exp"], 1)
            link(dve.tensor_reduce(lmx, lg, AX.X, ALU.add))
            link(dve.reciprocal(lmx, lmx))
            link(dve.tensor_tensor(pr, lg, lmx.unsqueeze(2).to_broadcast([P, NT, EM]), ALU.mult))
            for i in range(NT):
                mine = pr[:, i, :].unsqueeze(2).to_broadcast([P, EM, EM])
                other = pr[:, i, :].unsqueeze(1).to_broadcast([P, EM, EM])
                dve.tensor_tensor(cmp[:, i], other, mine, ALU.is_gt)
                ins = dve.tensor_tensor(ceq[:, i], other, mine, ALU.is_equal)
            link(ins)
            for i in range(NT):
                ins = dve.tensor_tensor(ceq[:, i], ceq[:, i], lower, ALU.mult)
            link(ins)
            link(dve.tensor_tensor(cmp, cmp, ceq, ALU.add))
            link(dve.tensor_reduce(comb, cmp, AX.X, ALU.add))
            link(dve.scalar_tensor_tensor(comb, comb, 1.5, pr, ALU.is_lt, ALU.mult))
            link(dve.tensor_reduce(lmx, comb, AX.X, ALU.add))
            link(dve.reciprocal(lmx, lmx))
            dve.tensor_tensor(comb, comb, lmx.unsqueeze(2).to_broadcast([P, NT, EM]),
                              ALU.mult).then_inc(s["comb_done"], 1)
            dve.wait_ge(s["comb_done"], 1)
            link(dve.tensor_tensor(ow3[0:3], ow3[0:3], bk3[0:3], ALU.mult))
            dve.wait_ge(s["rowmv_in"], 32)
            dve.tensor_tensor(chB[:, :, 0], chA, alt, ALU.mult)
            link(dve.memset(chB[:, :, 1], -1.0))
            link(dve.tensor_copy(chS[:, 0, :], chB[:, 0, :]))
            for n in range(1, S):
                link(dve.tensor_tensor_reduce(out=chr_[:, 0:2], in0=chS[:, n - 1, :], in1=chS[:, n - 1, :], scale=1.0,
                                              scalar=0.0, op0=ALU.mult, op1=ALU.add, accum_out=chr_[:, 2:3]))
                link(dve.reciprocal(chr_[:, 3:4], chr_[:, 2:3]))
                link(dve.scalar_tensor_tensor(chS[:, n, :], chS[:, n - 1, :], chr_[:, 3:4], chB[:, n, :],
                                              ALU.mult, ALU.add))
            link(dve.tensor_tensor(chS[:, :, 0], chS[:, :, 0], alt, ALU.mult))
            dve.engine_nop().then_inc(s["chain_in"], 1)
            dve.wait_ge(s["chE_in"], 16)
            dve.tensor_tensor(chG[:, 0, :], chS[0:8, :, 0], chE[:, ::-1, 0], ALU.add)
            link(dve.tensor_tensor(chG[:, 1, :], chS[0:8, :, 1], chE[:, ::-1, 1], ALU.add))
            dve.tensor_tensor(chG[:, 0, :], chG[:, 0, :], chA[0:8], ALU.subtract)
            link(dve.tensor_scalar(chG[:, 1, :], chG[:, 1, :], 1.0, None, ALU.add))
            link(dve.tensor_tensor(chQ, chG, chG, ALU.mult))
            link(dve.tensor_tensor(chQ[:, 0, :], chQ[:, 0, :], chQ[:, 1, :], ALU.add))
            link(dve.reciprocal(chQ[:, 1, :], chQ[:, 0, :]))
            dve.tensor_tensor(chF[:, 0, :], chG[:, 0, :], chQ[:, 1, :], ALU.mult)
            link(dve.scalar_tensor_tensor(chF[:, 1, :], chG[:, 1, :], -1.0, chQ[:, 1, :], ALU.mult, ALU.mult))
            dve.tensor_scalar(chF, chF, 10.0, -10.0, ALU.min, ALU.max).then_inc(s["feat_out"], 1)
            for e in range(EM):
                dve.wait_ge(s["y_mm"], 1 + e + 1)
                for i in range(NT):
                    ins = dve.scalar_tensor_tensor(xn[:, i, :], two_t(4 + 2 * (e % 2), i), comb[:, i, e:e + 1],
                                                   xn[:, i, :], ALU.mult, ALU.add)
                ins.then_inc(s["y_done"], 1)
                dve.wait_ge(s["y_done"], e + 1)
                if e == 0:
                    dve.wait_ge(s["combT_mm"], 1)
                    dve.tensor_copy(combT[0:EM], ps[0:EM, 6, :]).then_inc(s["combT_done"], 1)
            toks[0] += 1
            dve.wait_ge(s["extra_mm"], 1)
            dve.tensor_tensor(tok2, xn2, two(4), ALU.add).then_inc(s["tok_done"], 1)
            dve.wait_ge(s["tok_done"], toks[0])
            normalise(of(tok), of(xn)).then_inc(s["ln_done"], 1)
            dve.wait_ge(s["xT_mm"], 5)
            dve.tensor_copy(xT[0:DB, 1, :], ps[0:DB, 7, :]).then_inc(s["xT_dve"], 1)

            dve.wait_ge(s["xT_act"], 5)
            dve.wait_ge(s["xT_dve"], 5)
            for c, (r0, n) in enumerate(CH):
                ins = dve.tensor_copy(xd[0:n, c], xT[0:n, c, :].rearrange("p (b i) -> p b i", b=B)
                                      .unsqueeze(2).to_broadcast([n, B, 2, S]))
            ins.then_inc(s["xd_done"], 1)
            for c, (r0, n) in enumerate(CH):
                dve.wait_ge(s["k3_done"], c + 1)
                for h in range(2):
                    ins = dve.tensor_scalar(km3[0:n, c, :, h, :], ksb[0:n, c, :].rearrange("p (b i) -> p b i", b=B),
                                            parity[0:n, h:h + 1], None, ALU.mult)
                ins.then_inc(s["km_done"], 1)
            dve.wait_ge(s["decay_done"], 1)
            for t in range(NT):
                dve.wait_ge(s["e3_mm"], t + 1)
                for p, banks in ((0, 4), (4, PAIRS - 4)):
                    at = p // 4 * P
                    ins = dve.tensor_tensor(
                        E3[t // 2][:, t % 2, p:p + banks],
                        ps[:, 0:banks, at:at + P].rearrange("p a (m i) -> p a m i", m=2),
                        decay[:, p:p + banks, :].unsqueeze(2).to_broadcast([P, banks, 2, S]), ALU.mult)
                ins.then_inc(s["e3_done"], 1)
            dve.wait_ge(s["gate3_done"], 1)
            dve.wait_ge(s["pv3_mm"], 1)
            dve.tensor_tensor(pairs_of(gate3), pairs_of(gate3), two(4), ALU.mult).then_inc(s["og_done"], 1)
            dve.wait_ge(s["xT_mm"], 6)
            dve.tensor_copy(xT[0:DB, 1, :], ps[0:DB, 7, :]).then_inc(s["xT_dve"], 1)
            toks[0] += 1
            dve.wait_ge(s["tok_mm"], 3)
            dve.tensor_copy(tok2, two(0)).then_inc(s["tok_done"], 1)
            dve.wait_ge(s["tok_done"], toks[0])
            link(normalise(of(tok), of(tok)))
            wide_w = bc["ln_w"][:, :].unsqueeze(1).to_broadcast([P, NT, D])
            wide_b = bc["ln_b"][:, :].unsqueeze(1).to_broadcast([P, NT, D])
            link(dve.tensor_tensor(tok[:, :, :], tok[:, :, :], wide_w, ALU.mult))
            link(dve.tensor_tensor(tok[:, :, :], tok[:, :, :], wide_b, ALU.add))
            link(dve.tensor_tensor(tok[:, :, :], tok[:, :, :], xn[:, :, :], ALU.add))
            normalise(of(tok), of(xn)).then_inc(s["ln_done"], 1)
            dve.wait_ge(s["xT_mm"], 7)
            dve.tensor_copy(xT[0:DB, 1, :], ps[0:DB, 7, :]).then_inc(s["xT_dve"], 1)
            toks[0] += 1
            dve.engine_nop().then_inc(s["tok_done"], 1)
            dve.wait_ge(s["xT_act"], 7)
            dve.wait_ge(s["xT_dve"], 7)
            for c, (r0, n) in enumerate(CH):
                ins = dve.tensor_copy(xcls[0:n, c, :].rearrange("p (i b) -> p i b", i=NCLS),
                                      xT[0:n, c, :].rearrange("p (b n) -> p n b", n=S)[:, 0:NCLS, :])
            ins.then_inc(s["xcls_done"], 1)

            dve.wait_ge(s["cl_mm"], 1)
            cl = ps[:, 4, 0:2 * NC].rearrange("p (q n) -> p q n", q=2)
            link(dve.tensor_copy(cls_l, cl))
            link(dve.tensor_tensor(cls_s, cls_l[:, 0, :], cls_l[:, 1, :], ALU.max))
            dve.tensor_tensor(cls_l, cls_l, cls_s.unsqueeze(1).to_broadcast([P, 2, NC]),
                              ALU.subtract).then_inc(s["cl_sub"], 1)
            dve.wait_ge(s["cl_exp"], 1)
            link(dve.tensor_tensor(cls_s, cls_l[:, 0, :], cls_l[:, 1, :], ALU.add))
            link(dve.reciprocal(cls_s, cls_s))
            link(dve.tensor_tensor(cls_l, cls_l, cls_s.unsqueeze(1).to_broadcast([P, 2, NC]), ALU.mult))
            dve.tensor_tensor(cls_m[:, 0, :], cls_l[:, 0, :], cls_l[:, 1, :], ALU.is_gt)
            link(dve.tensor_tensor(cls_m[:, 1, :], cls_l[:, 1, :], cls_l[:, 0, :], ALU.is_gt))
            for i in range(NCLS):
                n = slice(i * B, (i + 1) * B)
                dve.tensor_copy(mcls[:, 3 + i % 2, n], cls_m[:, 0, n])
                ins = dve.tensor_copy(mcls[:, i // 2, n], cls_m[:, 1, n])
            ins.then_inc(s["mcls_done"], 1)
            for x in range(5):
                dve.wait_ge(s["hc_mm"], x + 1)
                src = ps[:, 6 + x % 2, 0:NF * NC].rearrange("p (f n) -> p f n", f=NF)
                bias = colc[:, R_A1 + NF * x:R_A1 + NF * (x + 1)].unsqueeze(2).to_broadcast([P, NF, NC])
                dve.tensor_tensor(hcls[:, x], src, bias, ALU.add).then_inc(s["hc_add"], 1)
            dve.wait_ge(s["bcast_in"], 7 * 16)
            link(dve.tensor_tensor(tok[:, :, :], xn[:, :, :],
                                   bc["m0_b2"][:, :].unsqueeze(1).to_broadcast([P, NT, D]), ALU.add))
            dve.wait_ge(s["zeros_made"], 4)
            dve.wait_ge(s["mcls_done"], 1)
            for x in range(5):
                dve.wait_ge(s["hc_done"], x + 1)
            for i in range(NCLS):
                n = slice(i * B, (i + 1) * B)
                for first, then, g in ((i // 2, 3 + i % 2, 0), (3 + i % 2, i // 2, 1)):
                    ins = dve.tensor_tensor(hmix[:, then, :, n], hcls[:, first, :, n],
                                            cls_m[:, g, n].unsqueeze(1).to_broadcast([P, NF, B]), ALU.mult)
            ins.then_inc(s["hmix_done"], 1)
            toks[0] += 1
            dve.wait_ge(s["y_mm"], 10)
            dve.tensor_tensor(tok2, tok2, two(4), ALU.add).then_inc(s["tok_done"], 1)
            dve.wait_ge(s["tok_done"], toks[0])
            normalise(of(tok), of(xn)).then_inc(s["fin_ready"], 1)
            dve.wait_ge(s["clsx_mm"], 1)
            link(dve.tensor_copy(clsx[0:NC], ps[0:NC, 2, 0:D]))
            dve.wait_ge(s["cls_mm"], 1)
            link(dve.tensor_tensor(clsx[0:NC], clsx[0:NC], ps[0:NC, 3, 0:D], ALU.add))
            normalise(lambda i: clsx[0:NC], lambda i: clsx[0:NC], 1, NC).then_inc(s["fin_ready"], 1)

        @block.tensor
        def _(pe):
            def mm(o, l, r, start, stop):
                return pe.matmul(o, l, r, start=start, stop=stop)

            def tr(o, i):
                k = i.shape[0]
                return pe.transpose(o, i, ident[0:k, 0:k])

            pe.wait_ge(s["ident_made"], 1)
            for j in range(2 * C):
                c, half = divmod(j, 2)
                if half == 0:
                    pe.wait_ge(s["xq_done"], c + 1)
                for w in range(4):
                    ins = tr(ps[:, j, w * P:(w + 1) * P], xq[:, c, 4 * half + w, :])
                ins.then_inc(s["xr_T"], 1)
            pe.wait_ge(s["wpatch_in"], 16)
            pe.wait_ge(s["xpT_act"], 3)
            pe.wait_ge(s["xpT_dve"], 3)
            for i in range(NT):
                for k in range(2 * C):
                    ins = mm(two_t(6, i), xpT[:, k, i * P:(i + 1) * P], wpatch[:, k % 2, k // 2, :],
                             k == 0, k == 2 * C - 1)
                if i % 2:
                    ins.then_inc(s["patch_mm"], 1)
            pe.wait_ge(s["rows_in"], 16 * 12)
            tr(ps[:, 7, 384:384 + NROWS], rowc[0:NROWS, :]).then_inc(s["colc_mm"], 1)

            def turn_weights(e):
                pe.wait_ge(s["raw_in"], 16 * 8)
                pe.wait_ge(s["rawg_in"], 16 * 4)
                pe.wait_ge(s["rawo_done"], 1)
                if e >= 1:
                    pe.wait_ge(s["wt_act"], e)
                    pe.wait_ge(s["wt_dve"], e)
                for oc, (o0, on) in enumerate(CH):
                    for m in range(3):
                        for ic, (i0, n) in enumerate(CH):
                            bank, at = ((2 if ic else 0), m * D) if m < 2 else (1, ic * D)
                            tr(ps[0:n, bank, at + o0:at + o0 + on], raw[0:on, oc, e, m, i0:i0 + n])
                    for h in range(2):
                        tr(ps[0:96, 3, h * D + o0:h * D + o0 + on], rawo[0:on, oc, e, h, :])
                    for m in range(2):
                        for ic, (i0, n) in enumerate(CH):
                            ins = tr(ps[0:n, 4 + ic, m * D + o0:m * D + o0 + on],
                                     rawg[0:on, oc, m, e * D + i0:e * D + i0 + n])
                ins.then_inc(s["wt_mm"], 1)

            turn_weights(0)
            turn_weights(1)

            def turn_tokens(x, n):
                for c, (r0, rn) in enumerate(CH):
                    for i in range(NT):
                        ins = tr(ps[0:rn, 6 + c, i * P:(i + 1) * P], x[:, i, r0:r0 + rn])
                ins.then_inc(s["xT_mm"], 1)

            def xT_ready(n):
                pe.wait_ge(s["xT_act"], n)
                pe.wait_ge(s["xT_dve"], n)

            pe.wait_ge(s["ln_done"], 1)
            pe.wait_ge(s["colc_done"], 1)
            turn_tokens(xn, 1)
            xT_ready(1)
            pe.wait_ge(s["wqkv_in"], 32)
            pe.wait_ge(s["wt_act"], 2)
            pe.wait_ge(s["wt_dve"], 2)

            def project0(hp):
                for m in range(2):
                    if hp >= 1:
                        pe.wait_ge(s["q0_done" if m == 0 else "kv0_done"], hp if m == 0 else 2 * hp - 1)
                    for c, (r0, n) in enumerate(CH):
                        at = m * H * DH0 + hp * P
                        ins = mm(ps[:, m, :], wqkv[0:n, c, at:at + P], xT[0:n, c, :], c == 0, c == 1)
                    ins.then_inc(s["q0_mm" if m == 0 else "k0_mm"], 1)
                if hp >= 1:
                    pe.wait_ge(s["kv0_done"], 2 * hp)
                at = 2 * H * DH0 + hp * P
                for i in range(NT):
                    for c, (r0, n) in enumerate(CH):
                        ins = mm(ps[:, 2, i * P:(i + 1) * P], xT[0:n, c, i * P:(i + 1) * P], wqkv[0:n, c, at:at + P],
                                 c == 0, c == 1)
                ins.then_inc(s["v0_mm"], 1)

            def scores0(hp):
                k = hp % 2
                pe.wait_ge(s["q0_done"], hp + 1)
                pe.wait_ge(s["kv0_done"], 2 * hp + 1)
                if hp >= 2:
                    pe.wait_ge(s["sub0"], hp - 1)
                for b in range(B):
                    ins = mm(ps[:, 3 + k, b * S:(b + 1) * S], qbd[:, k, b].rearrange("p h i -> p (h i)"),
                             kT0[:, k, b * S:(b + 1) * S], True, True)
                ins.then_inc(s["s0_mm"], 1)

            def values0(hp):
                k = hp % 2
                pe.wait_ge(s["p0_done"], hp + 1)
                if hp >= 1:
                    pe.wait_ge(s["pT0_done"], hp)
                for i in range(NT):
                    ins = tr(ps[:, 5, i * P:(i + 1) * P], p0[:, k, 2 * i:2 * i + 2, :].rearrange("p b j -> p (b j)"))
                ins.then_inc(s["t0_mm"], 1)
                pe.wait_ge(s["pT0_done"], hp + 1)
                pe.wait_ge(s["kv0_done"], 2 * hp + 2)
                if hp >= 1:
                    pe.wait_ge(s["oT0_done"], hp)
                for b in range(B):
                    r = slice(64 * (b % 2), 64 * (b % 2) + 64)
                    for h in range(2):
                        ins = mm(ps[64 * h:64 * h + 64, 6 + b % 2, b // 2 * S:(b // 2 + 1) * S], v0[r, k, b // 2, 64 * h:64 * h + 64],
                                 pT0[r, k, b // 2, 64 * h:64 * h + 64], True, True)
                ins.then_inc(s["pv0_mm"], 1)

            project0(0)
            scores0(0)
            for hp in range(PAIRS):
                if hp + 1 < PAIRS:
                    project0(hp + 1)
                    scores0(hp + 1)
                values0(hp)
            pe.wait_ge(s["oT0_done"], PAIRS)
            pe.wait_ge(s["wout_in"], 16)
            for i in range(NT):
                for k in range(PAIRS):
                    ins = mm(two_t(0, i), oT0[:, k, i * P:(i + 1) * P], wout[:, k, :], k == 0, k == PAIRS - 1)
            ins.then_inc(s["tok_mm"], 1)
            pe.wait_ge(s["tok_done"], 1)
            turn_weights(2)
            turn_weights(3)
            pe.wait_ge(s["ln_done"], 2)
            turn_tokens(xn, 2)
            xT_ready(2)
            pe.wait_ge(s["wt_act"], 4)
            pe.wait_ge(s["wt_dve"], 4)

            jobs = [0]

            def up(w):
                for f in range(NF):
                    if jobs[0] >= 4:
                        pe.wait_ge(s["h_act"], jobs[0] - 3)
                    bank = jobs[0] % 4
                    jobs[0] += 1
                    for c, (r0, n) in enumerate(CH):
                        ins = mm(ps[:, bank, :], w[0:n, c, f * P:(f + 1) * P], xT[0:n, c, :], c == 0, c == 1)
                    ins.then_inc(s["h_mm"], 1)

            def down(h, w, bank):
                for i in range(NT):
                    for f in range(NF):
                        ins = mm(two_t(bank, i), h[:, f, i * P:(i + 1) * P], w[:, f, :], f == 0, f == NF - 1)
                ins.then_inc(s["y_mm"], 1)
                return ins

            pe.wait_ge(s["ff_in"], 48)
            up(wff1)
            pe.wait_ge(s["h_act"], jobs[0])
            for i in range(NT):
                for f in range(NF):
                    ins = mm(two_t(4, i), ffh[:, f, i * P:(i + 1) * P], wff2[:, f, :], f == 0, f == NF - 1)
            ins.then_inc(s["tok_mm"], 1)
            pe.wait_ge(s["tok_done"], 2)
            turn_tokens(tok, 3)
            xT_ready(3)
            pe.nop().then_inc(s["y_mm"], 1)

            def project1(e):
                if e >= 1:
                    pe.wait_ge(s["s1_read"], NT * e)
                for c, (r0, n) in enumerate(CH):
                    for m in range(2):
                        for k, (k0, kn) in enumerate(CH):
                            ins = mm(ps[0:n, 3 + 2 * c + m, :], wT[0:kn, k, e, m, r0:r0 + n], xT[0:kn, k, :],
                                     k == 0, k == 1)
                        ins.then_inc(s["qk1_mm"], 1)
                for j in range(2):
                    pe.wait_ge(s["qk1_dve" if j == 0 else "qk1_act"], 2 * e + 1)
                    for m in range(2):
                        i = 2 * j + m
                        for k, (k0, kn) in enumerate(CH):
                            ins = mm(ps[:, 3 + j, m * D:m * D + D], xT[0:kn, k, i * P:(i + 1) * P],
                                     wT[0:kn, k, e, 2, :], k == 0, k == 1)
                    ins.then_inc(s["v1_mm"], 1)

            def scores1(e, t):
                n = NT * e + t
                if t == 0:
                    pe.wait_ge(s["qk1_dve"], 2 * e + 2)
                    pe.wait_ge(s["qk1_act"], 2 * e + 2)
                    pe.wait_ge(s["v1_done"], 2 * e + 2)
                if n >= 1:
                    pe.wait_ge(s["s1_read"], n)
                for m in range(2):
                    b = 2 * t + m
                    for p in range(PAIRS):
                        c, r, at = p // 4, 32 * (p % 4), (2 * (p // 4) + m) * S
                        ins = mm(ps[:, 3 + p % 4, at:at + S],
                                 qm[r:r + 32, e % 2, c, b].rearrange("p h i -> p (h i)"),
                                 kT1[r:r + 32, e % 2, c, b * S:(b + 1) * S], True, True)
                ins.then_inc(s["s1_mm"], 1)

            def values1(e, t):
                n = NT * e + t
                k = n % 2
                pe.wait_ge(s["exp1"], n + 1)
                if n >= 1:
                    pe.wait_ge(s["pT1_done"], n)
                if t == 0 and e >= 1:
                    pe.wait_ge(s["fT_act"], e)
                    pe.wait_ge(s["fT_dve"], e)
                for p in range(PAIRS):
                    ins = tr(ps[:, p // 3, (p % 3) * P:(p % 3 + 1) * P], p1[:, k, p].rearrange("p m j -> p (m j)"))
                ins.then_inc(s["t1_mm"], 1)
                pe.wait_ge(s["pT1_done"], n + 1)
                pe.wait_ge(s["v1_done"], 2 * e + 1 + t // 2)
                if n >= 1:
                    pe.wait_ge(s["o1_done"], n)
                w = 2 * (2 * DH + 1)
                for p in range(PAIRS):
                    ins = mm(ps[:, 7, p * w:(p + 1) * w], pT1[:, k, p, :],
                             vbd[:, e % 2, t, p].rearrange("p m d -> p (m d)"), True, True)
                ins.then_inc(s["pv1_mm"], 1)

            def turn_o(e, t):
                n = NT * e + t
                pe.wait_ge(s["o1_done"], n + 1)
                if t % 2 == 0 and n >= 2:
                    pe.wait_ge(s["ot1_done"], n // 2)
                for m in range(2):
                    at = (2 * (t % 2) + m) * P
                    ins = tr(ps[0:96, 2, at:at + P], o1[:, n % 2, m].rearrange("p a d -> p (a d)"))
                ins.then_inc(s["ot1_mm"], 1)

            def join(e):
                pe.wait_ge(s["ot1_done"], 2 * e + 2)
                pe.wait_ge(s["pT1_done"], NT * (e + 1))
                for c, (r0, n) in enumerate(CH):
                    for h in range(2):
                        ins = mm(ps[0:n, c, :], woT[0:96, h, e, r0:r0 + n], oT1[0:96, h, :], h == 0, h == 1)
                    ins.then_inc(s["wo1_mm"], 1)

            pe.wait_ge(s["zeros_made"], 2)
            project1(0)
            scores1(0, 0)
            for e in range(EA):
                for t in range(NT):
                    if t < NT - 1:
                        scores1(e, t + 1)
                    elif e < EA - 1:
                        project1(e + 1)
                    values1(e, t)
                    if t >= 1:
                        turn_o(e, t - 1)
                if e < EA - 1:
                    scores1(e + 1, 0)
                turn_o(e, NT - 1)
                join(e)
            pe.wait_ge(s["fT_act"], EA)
            pe.wait_ge(s["fT_dve"], EA)
            for i in range(NT):
                for e in range(EA):
                    for c, (r0, n) in enumerate(CH):
                        ins = mm(ps[:, i, 0:2 * D], fT[0:n, e, c, i * P:(i + 1) * P], wguT[0:n, e, c, :],
                                 e == 0 and c == 0, e == EA - 1 and c == 1)
                ins.then_inc(s["gu_mm"], 1)
            pe.wait_ge(s["ln_done"], 3)
            turn_tokens(xn, 4)
            xT_ready(4)

            pe.wait_ge(s["small_in"], 16 * 13)
            for c, (r0, n) in enumerate(CH):
                ins = mm(ps[0:1, 4, :], vw[0:n, c, :], xT[0:n, c, :], c == 0, c == 1)
            ins.then_inc(s["v_mm"], 1)
            for i in range(NT):
                for c, (r0, n) in enumerate(CH):
                    ins = mm(ps[:, 5, i * EM:(i + 1) * EM], xT[0:n, c, i * P:(i + 1) * P], gw[0:n, c, :],
                             c == 0, c == 1)
            ins.then_inc(s["lg_mm"], 1)
            for e in range(EM + 1):
                if e < EM:
                    pe.wait_ge(slot_in[e % NSLOT], 48 * (e // NSLOT + 1))
                    up(w1s[:, e % NSLOT])
                if e == 1:
                    pe.wait_ge(s["comb_done"], 1)
                    for i in range(NT):
                        ins = tr(ps[0:EM, 6, i * P:(i + 1) * P], comb[:, i, :])
                    ins.then_inc(s["combT_mm"], 1)
                if e >= 1:
                    d = e - 1
                    if d == 1:
                        pe.wait_ge(s["combT_done"], 1)
                    if d >= 2:
                        pe.wait_ge(s["y_done"], d - 1)
                    pe.wait_ge(s["h_act"], NF * (d + 2))
                    down(hT[:, d % 2], w2s[:, d % NSLOT], 4 + 2 * (d % 2))
            pe.wait_ge(s["combT_done"], 1)
            pe.wait_ge(s["chF_in"], 32)
            pe.wait_ge(s["y_done"], EM - 1)
            for i in range(NT):
                mm(two_t(4, i), combT[0:EM, i * P:(i + 1) * P], b2m[0:EM], True, False)
                ins = mm(two_t(4, i), frow[:, i * P:(i + 1) * P], ow3[0:3], False, True)
            ins.then_inc(s["extra_mm"], 1)
            pe.wait_ge(s["ln_done"], 4)
            turn_tokens(xn, 5)
            xT_ready(5)

            pe.wait_ge(s["s3_in"], 16 * 11)
            for c, (r0, n) in enumerate(CH):
                ins = mm(ps[0:16, 7, :], wg1[0:n, c, :], xT[0:n, c, :], c == 0, c == 1)
            ins.then_inc(s["gate1_mm"], 1)
            for c, (r0, n) in enumerate(CH):
                for m in range(2):
                    for k, (k0, kn) in enumerate(CH):
                        ins = mm(ps[0:n, 2 * c + m, :], wq3[0:kn, m, k, r0:r0 + n], xT[0:kn, k, :], k == 0, k == 1)
                    ins.then_inc(s["q3_mm"], 1)
            pe.wait_ge(s["xd_done"], 1)
            for j in range(B // 2):
                if j >= 2:
                    pe.wait_ge(s["v3_done"], j - 1)
                for m in range(2):
                    b = 2 * j + m
                    for k, (k0, kn) in enumerate(CH):
                        img = xd[0:kn, k, b].rearrange("p h i -> p (h i)")
                        ins = mm(ps[:, 4 + j % 2, m * D:(m + 1) * D], img, wq3[0:kn, 2, k, :], k == 0, k == 1)
                ins.then_inc(s["v3_mm"], 1)
            pe.wait_ge(s["gate1_done"], 1)
            for i in range(NT):
                ins = mm(two_t(6, i), g1T[:, i * P:(i + 1) * P], wg2, True, True)
            ins.then_inc(s["gate3_mm"], 1)
            pe.wait_ge(s["q3_done"], 2)
            pe.wait_ge(s["km_done"], 2)
            pe.wait_ge(s["v3_done"], B // 2)

            def values3(t):
                pe.wait_ge(s["e3_done"], t + 1)
                for m in range(2):
                    for p in range(PAIRS):
                        at = t % 2 * D + p * 2 * DH
                        ins = mm(ps[64 * m:64 * m + 64, 4 + t // 2, at:at + 2 * DH], E3[t // 2][:, t % 2, p, m, :],
                                 vbd3[:, 2 * t + m, p].rearrange("p h d -> p (h d)"), True, True)
                return ins

            for t in range(NT):
                if t >= 1:
                    pe.wait_ge(s["e3_done"], t)
                for m in range(2):
                    for p in range(PAIRS):
                        c, r, at = p // 4, 32 * (p % 4), (2 * (p // 4) + m) * S
                        b = 2 * t + m
                        ins = mm(ps[:, p % 4, at:at + S], km3[r:r + 32, c, b].rearrange("p h i -> p (h i)"),
                                 q3[r:r + 32, c, b * S:(b + 1) * S], True, True)
                ins.then_inc(s["e3_mm"], 1)
                if t >= 1:
                    values3(t - 1)
            values3(NT - 1).then_inc(s["pv3_mm"], 1)
            pe.wait_ge(s["og_done"], 1)
            turn_tokens(gate3, 6)
            xT_ready(6)
            for i in range(NT):
                for k, (k0, kn) in enumerate(CH):
                    ins = mm(two_t(0, i), xT[0:kn, k, i * P:(i + 1) * P], wq3[0:kn, 3, k, :], k == 0, k == 1)
            ins.then_inc(s["tok_mm"], 1)
            pe.wait_ge(s["ln_done"], 5)
            turn_tokens(xn, 7)
            xT_ready(7)

            def cls(c, n):
                return xcls[0:n, c, :]

            pe.wait_ge(s["xcls_done"], 1)

            for i in range(NCLS):
                for q in range(2):
                    for c, (r0, n) in enumerate(CH):
                        ins = mm(ps[:, 4, q * NC + i * B:q * NC + (i + 1) * B],
                                 gwc[0:n, c, i, q:q + 1].to_broadcast([n, P]), cls(c, n)[:, i * B:(i + 1) * B], c == 0, c == 1)
            ins.then_inc(s["cl_mm"], 1)
            pe.wait_ge(s["m0_in"], 48)
            up(m0w1)
            pe.wait_ge(s["a_in"], 16 * 15)
            for x in range(5):
                if x >= 2:
                    pe.wait_ge(s["hc_add"], x - 1)
                for f in range(NF):
                    for c, (r0, n) in enumerate(CH):
                        ins = mm(ps[:, 6 + x % 2, f * NC:(f + 1) * NC], a1w[0:n, x, c, f * P:(f + 1) * P], cls(c, n),
                                 c == 0, c == 1)
                ins.then_inc(s["hc_mm"], 1)
            pe.wait_ge(s["h_act"], jobs[0])
            pe.wait_ge(s["cl_sub"], 1)
            down(hT[:, 0], m0w2, 4)
            for c, (r0, n) in enumerate(CH):
                ins = tr(ps[0:NC, 2, r0:r0 + n], cls(c, n))
            ins.then_inc(s["clsx_mm"], 1)
            pe.wait_ge(s["hmix_done"], 1)
            for x in range(5):
                for f in range(NF):
                    mm(ps[0:NC, 3, 0:D], hmix[:, x, f, :], a2w[:, x, f, :], x == 0 and f == 0, False)
            for x in range(5):
                ins = mm(ps[0:NC, 3, 0:D], mcls[0:1, x, :], a2b[0:1, x, :], False, x == 4)
            ins.then_inc(s["cls_mm"], 1)


_INS = {
    "x": "x", "w_patch": "L0_tok_w_patch", "b_patch": "L0_tok_b_patch", "g1": "L0_tok_g1", "beta1": "L0_tok_beta1",
    "w_qkv": "L0_tok_w_qkv", "w_out": "L0_tok_w_out", "b_out": "L0_tok_b_out", "g2": "L0_tok_g2",
    "beta2": "L0_tok_beta2", "w_ff1": "L0_tok_w_ff1", "b_ff1": "L0_tok_b_ff1", "w_ff2": "L0_tok_w_ff2",
    "b_ff2": "L0_tok_b_ff2", "wq": "L0_attn_wq", "wk": "L0_attn_wk", "wv": "L0_attn_wv", "wo": "L0_attn_wo",
    "w_gate": "L0_attn_w_gate", "w_up": "L0_attn_w_up", "v_w": "L0_ffn_v_w", "v_b": "L0_ffn_v_b",
    "gate_w": "L0_ffn_gate_w", "gate_b": "L0_ffn_gate_b", "w1": "L0_ffn_w1", "b1": "L0_ffn_b1", "w2": "L0_ffn_w2",
    "b2": "L0_ffn_b2", "out_w": "L0_ffn_out_w", "out_b": "L0_ffn_out_b", "bk": "L0_ffn_bk_scale",
    "slope": "L1_attn_log_slope", "Wq": "L1_attn_Wq", "Wk": "L1_attn_Wk", "Wv": "L1_attn_Wv", "Wo": "L1_attn_Wo",
    "Wg1": "L1_attn_Wg1", "Wg2": "L1_attn_Wg2", "ln_w": "L1_attn_ln_w", "ln_b": "L1_attn_ln_b",
    "m0w1": "L1_ffn_moe0_W1", "m0_b1": "L1_ffn_moe0_b1", "m0w2": "L1_ffn_moe0_W2", "m0_b2": "L1_ffn_moe0_b2",
    "a1w": "L1_ffn_A1_W", "a1b": "L1_ffn_A1_b", "a2w": "L1_ffn_A2_W", "a2b": "L1_ffn_A2_b", "gcls": "L1_ffn_G_W",
}


def kernel(**inputs):
    import numpy as _np
    import concourse.bacc as _bacc
    from concourse import mybir as _mybir
    from concourse.bass_utils import run_bass_kernel_spmd as _run

    nc = _bacc.Bacc("TRN2", target_bir_lowering=False, num_devices=1)
    arrays, args = {}, {}
    for short, name in _INS.items():
        v = _np.ascontiguousarray(inputs[name])
        if v.ndim == 0:
            v = v.reshape(1)
        arrays[f"in_{short}"] = v
        args[short] = nc.dram_tensor(f"in_{short}", v.shape, _mybir.dt.from_np(v.dtype), kind="ExternalInput").ap()
    out = nc.dram_tensor("out_0", (8, 64, 192), _mybir.dt.float32, kind="ExternalOutput").ap()
    vit_tower(nc, args, out)
    r = _run(nc, [arrays], core_ids=[0])
    return r.results[0]["out_0"]
```

```python
from contextlib import ExitStack

import numpy as np

import concourse.bass as bass
from concourse import mybir

F32 = mybir.dt.float32
I32 = mybir.dt.int32
ALU = mybir.AluOpType
ACT = mybir.ActivationFunctionType
AX = mybir.AxisListType

P = 128
B, C, IMG, PATCH = 8, 3, 128, 16
GRID = IMG // PATCH
S = GRID * GRID
T = B * S
NT = T // P
D = 192
DB = D - P
CH = ((0, P), (P, DB))
H = 12
PAIRS = H // 2
DH0 = 64
DH = D // H
MLP = 768
NF = MLP // P
EA = 4
EM = 8
NCLS = 6
NC = NCLS * B
EPS = 1e-5
NEG = -1e30
R_FF1, R_MOE, R_M0, R_A1, R_LNA, R_LNB = 0, NF, NF * 9, NF * 10, NF * 15, NF * 15 + 4
NROWS = R_LNB + 4


def vit_tower(nc, a, out):
    ctx = ExitStack()
    with ctx:
        def sb(name, shape, dt=F32):
            return ctx.enter_context(nc.sbuf_tensor(name, shape, dt))

        def sem(name):
            return ctx.enter_context(nc.semaphore(name))

        def carve(region):
            at = [0]

            def take(*dims, rows=P):
                n = int(np.prod(dims))
                v = region[0:rows, at[0]:at[0] + n]
                at[0] += n
                assert at[0] <= region.shape[1], at[0]
                names = ["a", "b", "c", "d", "e"][:len(dims)]
                if len(dims) > 1:
                    v = v.rearrange(f"p ({' '.join(names)}) -> p {' '.join(names)}", **dict(zip(names, dims)))
                return v
            return take

        ps = ctx.enter_context(nc.psum_tensor("ps", [P, 8, 512], F32))

        ident = sb("ident", [P, P])
        tok = sb("tok", [P, NT, D])
        xn = sb("xn", [P, NT, D])
        xT = sb("xT", [P, 2, T])
        rowc = sb("rowc", [P, P])
        colc = sb("colc", [P, P])
        bn = sb("bn", [P, NT, 6])
        mv = sb("mv", [P, NT, 2])
        rstd = sb("rstd", [P, NT])
        neghalf = sb("neghalf", [P, NT])
        causal = sb("causal", [P, S])
        par_i = sb("par_i", [P, 1], I32)
        parity = sb("parity", [P, 2])
        bc = {n: sb("bc_" + n, [P, D]) for n in
              ("b_patch", "b_out", "b_ff2", "ln_w", "ln_b", "m0_b2")}
        gateb = sb("gateb", [P, EM])
        slopes = sb("slopes", [P, H])
        slope = sb("slope", [P, PAIRS])
        dist = sb("dist", [P, S])
        decay = sb("decay", [P, PAIRS, S])

        front = sb("front", [P, 22960])
        wide = sb("wide", [P, 9216])
        turned = sb("turned", [P, 9216])

        take = carve(front)
        wqkv = take(2, 3 * H * DH0)
        wout = take(PAIRS, D)
        wpatch = take(2, C, D)
        wff1 = take(2, MLP)
        wff2 = take(NF, D)
        oT0 = take(PAIRS, T)
        qbd = take(2, B, 2, S)
        kT0 = take(2, T)
        v0 = take(2, NT, P)
        p0 = take(2, B, S)
        pT0 = take(2, NT, P)
        mx0 = take(2, B)
        take = carve(front[:, 9600:])
        xr = take(C, 1024)
        xpT = take(2 * C, T)
        xq = take(C, GRID, P)
        ffh = carve(front[:, 9600 + PAIRS * T:])(NF, T)
        rawo = carve(front[:, 19600:])(2, EA, 2, PAIRS * DH)
        del take

        take = carve(front)
        kbd = take(B, 4, S)
        kbdB = take(B, 2, S)
        vbd = take(2, NT, PAIRS, 2, 2 * DH + 1)
        qm = take(2, B, 2, S)
        p1 = take(2, PAIRS, 2, S)
        pT1 = take(2, PAIRS, P)
        mx1 = take(2, 2 * PAIRS)
        rc1 = take(2, 2 * PAIRS)
        o1 = take(2, 2, PAIRS, DH)
        oT1 = take(2, T)
        fT = take(EA, 2, T)
        gsb = take(NT, D)
        last_at = 19600

        takew = carve(wide)
        raw = takew(2, EA, 4, D)
        rawg = takew(2, 2, MLP)
        takew = carve(wide)
        NSLOT = 3
        w1s = takew(NSLOT, 2, MLP)
        w2s = takew(NSLOT, NF, D)
        m0w2 = takew(NF, D)
        taket = carve(turned)
        wT = taket(2, EA, 3, D)
        woT = taket(2, EA, D)
        wguT = taket(EA, 2, 2 * D)

        take = carve(front[:, last_at:])
        m0w1 = take(2, MLP)
        wq3 = take(4, 2, D)
        wg1 = take(2, 16)
        wg2 = take(D, rows=16)
        take = carve(front)
        hT = take(2, NF, T)
        a1w = take(5, 2, MLP)
        a2w = take(5, NF, D)
        take = carve(turned)
        q3 = take(B, 4, S)
        q3b = take(B, 2, S)
        km3 = take(2, B, 2, S)
        ksb = take(2, T)
        vbd3 = take(B, PAIRS, 2, DH)
        g1T = take(T, rows=16)
        gate3 = take(NT, D)
        takew = carve(wide)
        E3 = takew(2, PAIRS, 2, S), takew(2, PAIRS, 2, S)
        xd = takew(2, B, 2, S)
        take = carve(turned)
        hcls = take(5, NF, NC)
        hmix = take(5, NF, NC)
        small = sb("small", [P, 3540])
        take = carve(small)
        gw = take(2, EM)
        gwc = take(2, NCLS, 2)
        vw = take(2, 1)
        vb = take(1)
        lg = take(NT, EM)
        pr = take(NT, EM)
        cmp = take(NT, EM, EM)
        ceq = take(NT, EM, EM)
        lower = take(EM, EM)
        lmx = take(NT)
        comb = take(NT, EM)
        combT = take(T)
        b2m = take(D)
        ow3 = take(D)
        bk3 = take(D)
        clsx = take(D)
        xcls = take(2, NC)
        cls_l = take(2, NC)
        cls_m = take(2, NC)
        cls_s = take(NC)
        mcls = take(5, NC)
        a2b = take(5, D)
        xg = cmp.rearrange("p a b c -> p (a b c)")[:, 0:4 * NC].rearrange("p (a b c) -> p a b c", a=2, b=2)
        ones = ceq.rearrange("p a b c -> p (a b c)")[:, 0:P]
        del take
        line = sb("line", [16, 5, T])
        vrow, vrev, frow = line[0:1, 0, :], line[0:1, 1, :], line[0:3, 2, :]
        take = carve(line[0:16, 3:5, :].rearrange("p a b -> p (a b)"))
        chA = take(S, rows=16)
        alt = take(S, rows=16)
        chr_ = take(4, rows=16)
        chB = take(S, 2, rows=16)
        chS = take(S, 2, rows=16)
        chE = take(S, 2, rows=8)
        chG = take(2, S, rows=8)
        chQ = take(2, S, rows=8)
        chF = take(2, S, rows=8)

        names = """x_in wpatch_in rows_in bcast_in wqkv_in wout_in ff_in raw_in rawg_in small_in
            s3_in m0_in a_in rowmv_in chE_in chF_in out_done
            ident_made xq_done rawo_done xd_done xcls_done consts_made rows_zero colc_mm colc_done
            xr_T xpT_act xpT_dve patch_mm
            wt_mm wt_act wt_dve
            var_ready rstd_ready ln_done xT_mm xT_act xT_dve
            q0_mm k0_mm v0_mm q0_done kv0_done s0_mm s0_read sub0 exp0 p0_done t0_mm pT0_done
            pv0_mm oT0_done zeros_made
            tok_mm tok_done bias_added
            h_mm h_act y_mm y_done
            qk1_mm qk1_dve qk1_act v1_mm v1_done s1_mm s1_read sub1 exp1 t1_mm pT1_done pv1_mm o1_done
            ot1_mm ot1_done wo1_mm fT_act fT_dve gu_mm silu_done
            lg_mm lg_sub lg_exp comb_done combT_mm combT_done v_mm chain_in spec_ready feat_out extra_mm extra_done
            gate1_mm gate1_done gate3_mm gate3_done q3_mm q3_done k3_done v3_mm v3_done km_done
            e3_mm e3_done pv3_mm og_done decay_exp decay_done dist_ready
            xg_done cl_mm cl_sub cl_exp mcls_done hc_mm hc_add hc_done hmix_done cls_mm clsx_mm cls_out_ready
            fin_ready dve_step pool_step zero_cls""".split()
        s = {n: sem(n) for n in names}
        slot_in = [sem(f"slot_in{i}") for i in range(NSLOT)]

        def col(i):
            return colc[:, i:i + 1]

        def two(bank):
            return ps[:, bank:bank + 2, 0:2 * D]

        def two_t(bank, i):
            return ps[:, bank + i // 2, (i % 2) * D:(i % 2) * D + D]

        def pairs_of(x):
            return x.rearrange("p (a b) d -> p a (b d)", a=2)

        tok2, xn2 = pairs_of(tok[:, :, :]), pairs_of(xn[:, :, :])

        def patch_in(j):
            return ps[:, j, :].rearrange("p (w b h) -> p h b w", w=4, h=2)

        def patch_out(j):
            c, half = divmod(j, 2)
            v = xpT[:, 2 * c:2 * c + 2, :].rearrange("p h (b w) -> p h b w", w=GRID)
            return v[:, :, :, 4 * half:4 * half + 4]

        block = ctx.enter_context(nc.Block())

        @block.sync
        def _(sp):
            def load(dst, src, name):
                sp.dma_start(dst, src).then_inc(s[name], 16)

            for b in range(B):
                load(xr[16 * b:16 * b + 16], a["x"][b].rearrange("c (hh r) w -> hh c (r w)", r=8), "x_in")
            load(wpatch.rearrange("p a c n -> p a (c n)"),
                 a["w_patch"].rearrange("(ph k c) n -> k ph (c n)", ph=2, c=C), "wpatch_in")
            sp.wait_ge(s["rows_zero"], 1)
            for r, name in ((R_FF1, "b_ff1"), (R_M0, "m0_b1")):
                load(rowc[r:r + NF], a[name].rearrange("(f p) -> f p", p=P), "rows_in")
            load(rowc[R_MOE:R_MOE + NF * EM], a["b1"].rearrange("e (f p) -> (e f) p", p=P), "rows_in")
            load(rowc[R_A1:R_A1 + NF * 5], a["a1b"].rearrange("e (f p) -> (e f) p", p=P), "rows_in")
            for k, name in enumerate(("g1", "beta1", "g2", "beta2")):
                g = a[name].rearrange("(o n) -> o n", o=1)
                load(rowc[R_LNA + k:R_LNA + k + 1], g[:, 0:P], "rows_in")
                load(rowc[R_LNB + k:R_LNB + k + 1, 0:DB], g[:, P:D], "rows_in")
            for n in ("b_patch", "b_out", "b_ff2", "ln_w", "ln_b", "m0_b2"):
                load(bc[n][:, :], a[n].partition_broadcast(P), "bcast_in")
            load(slopes[:, :], a["slope"].partition_broadcast(P), "bcast_in")
            load(wqkv[:, 0], a["w_qkv"][0:P], "wqkv_in")
            load(wqkv[0:DB, 1], a["w_qkv"][P:D], "wqkv_in")
            for m, name in enumerate(("wq", "wk", "wv", "wo")):
                w = a[name].rearrange("e o i -> o e i")
                load(raw[:, 0, :, m, :], w[0:P], "raw_in")
                load(raw[0:DB, 1, :, m, :], w[P:D], "raw_in")
            for m, name in enumerate(("w_gate", "w_up")):
                load(rawg[:, 0, m, :], a[name][0:P], "rawg_in")
                load(rawg[0:DB, 1, m, :], a[name][P:D], "rawg_in")
            load(wout, a["w_out"].rearrange("(f p) n -> p f n", p=P), "wout_in")
            load(wff1[:, 0], a["w_ff1"][0:P], "ff_in")
            load(wff1[0:DB, 1], a["w_ff1"][P:D], "ff_in")
            load(wff2, a["w_ff2"].rearrange("(f p) n -> p f n", p=P), "ff_in")
            for c, (r0, n) in enumerate(CH):
                load(gw[0:n, c, :], a["gate_w"][r0:r0 + n], "small_in")
                load(vw[0:n, c, :], a["v_w"].rearrange("(p o) -> p o", o=1)[r0:r0 + n], "small_in")
                load(gwc[0:n, c, :, :], a["gcls"].rearrange("i d q -> d i q")[r0:r0 + n], "small_in")
            load(vb[0:1], a["v_b"].rearrange("(p o) -> p o", o=1), "small_in")
            load(gateb[:, :], a["gate_b"].partition_broadcast(P), "small_in")
            load(b2m[0:EM], a["b2"], "small_in")
            load(ow3[0:2], a["out_w"], "small_in")
            load(ow3[2:3], a["out_b"].rearrange("(o n) -> o n", o=1), "small_in")
            load(bk3[0:3], a["bk"].partition_broadcast(3), "small_in")
            load(a2b[0:1], a["a2b"].rearrange("(o e) n -> o e n", o=1), "small_in")
            sp.wait_ge(s["y_mm"], 1)
            for m, name in enumerate(("Wq", "Wk", "Wv", "Wo")):
                for c, (r0, n) in enumerate(CH):
                    load(wq3[0:n, m, c, :], a[name][r0:r0 + n], "s3_in")
            for c, (r0, n) in enumerate(CH):
                load(wg1[0:n, c, :], a["Wg1"][r0:r0 + n], "s3_in")
                load(m0w1[0:n, c], a["m0w1"][r0:r0 + n], "m0_in")
            load(wg2, a["Wg2"], "s3_in")
            sp.wait_ge(s["wt_mm"], EA)
            load(m0w2, a["m0w2"].rearrange("(f p) n -> p f n", p=P), "m0_in")
            for e in range(EM):
                k = e % NSLOT
                if e >= NSLOT:
                    sp.wait_ge(s["y_mm"], 1 + e - NSLOT + 1)
                for c, (r0, n) in enumerate(CH):
                    sp.dma_start(w1s[0:n, k, c], a["w1"][e, r0:r0 + n]).then_inc(slot_in[k], 16)
                sp.dma_start(w2s[:, k], a["w2"][e].rearrange("(f p) n -> p f n", p=P)).then_inc(slot_in[k], 16)
                if e == NSLOT - 1:
                    sp.wait_ge(s["gu_mm"], NT)
                    sp.wait_ge(s["silu_done"], NT)
                    sp.wait_ge(s["ln_done"], 3 * NT)
                    for x in range(5):
                        for c, (r0, n) in enumerate(CH):
                            load(a1w[0:n, x, c], a["a1w"][x, r0:r0 + n], "a_in")
                        load(a2w[:, x], a["a2w"][x].rearrange("(f p) n -> p f n", p=P), "a_in")
            o3 = out
            for b in range(B):
                sp.wait_ge(s["fin_ready"], b // 2 + 1)
                r = S * (b % 2)
                sp.dma_start(o3[b, NCLS:S, :], xn[r + NCLS:r + S, b // 2, :]).then_inc(s["out_done"], 16)
            sp.wait_ge(s["fin_ready"], NT + 1)
            for i in range(NCLS):
                sp.dma_start(o3[:, i, :], clsx[i * B:(i + 1) * B, :]).then_inc(s["out_done"], 16)
            sp.wait_ge(s["out_done"], 16 * (B + NCLS))

        @block.gpsimd
        def _(pool):
            steps = [0]

            def link(ins):
                steps[0] += 1
                ins.then_inc(s["pool_step"], 1)
                pool.wait_ge(s["pool_step"], steps[0])

            told = {}

            def tell(ins, name):
                told[name] = told.get(name, 0) + 1
                ins.then_inc(s[name], 1)
                pool.wait_ge(s[name], told[name])

            link(pool.memset(ident[:, :], 0.0))
            tell(pool.affine_select(out=ident[:, :], in_=ident[:, :], compare_op=ALU.not_equal, fill=1.0, base=0,
                                    pattern=[[-1, P]], channel_multiplier=1), "ident_made")
            tell(pool.memset(rowc[:, :], 0.0), "rows_zero")
            link(pool.memset(neghalf[:, :], -0.5))
            link(pool.iota(par_i[:, :], pattern=[[0, 1]], base=0, channel_multiplier=1))
            link(pool.memset(causal[:, :], 0.0))
            for h in range(2):
                r = slice(64 * h, 64 * h + 64)
                link(pool.affine_select(out=causal[r], in_=causal[r], compare_op=ALU.is_ge, fill=NEG, base=0,
                                        pattern=[[-1, S]], channel_multiplier=1))
                link(pool.iota(dist[r, :], pattern=[[1, S]], base=0, channel_multiplier=-1,
                               allow_small_or_imprecise_dtypes=True))
            link(pool.memset(lower, 1.0))
            link(pool.affine_select(out=lower, in_=lower, compare_op=ALU.is_gt, fill=0.0, base=0,
                                    pattern=[[1, EM], [-1, EM]], channel_multiplier=0))
            link(pool.memset(alt, -1.0))
            link(pool.memset(alt.rearrange("p (n c) -> p n c", c=2)[:, :, 0], 1.0))
            link(pool.memset(frow, 1.0))
            tell(pool.memset(mcls, 0.0), "consts_made")
            pool.wait_ge(s["patch_mm"], 2)
            for k in range(2):
                for h in range(2):
                    link(pool.memset(qbd[64 * h:64 * h + 64, k, :, 1 - h, :], 0.0))
            tell(pool.memset(qbd[64:P, 0, 0:1, 0, :], 0.0), "zeros_made")

            lns = [0]

            def rsqrt(n=NT, rows=P):
                lns[0] += 1
                pool.wait_ge(s["var_ready"], lns[0])
                link(pool.tensor_scalar(rstd[0:rows, 0:n], mv[0:rows, 0:n, 1], EPS, None, ALU.add))
                tell(pool.tensor_tensor(rstd[0:rows, 0:n], rstd[0:rows, 0:n], neghalf[0:rows, 0:n], ALU.pow),
                     "rstd_ready")

            def add_bias(name, n):
                pool.wait_ge(s["ln_done"], NT * n)
                if n == 1:
                    pool.wait_ge(s["bcast_in"], 7 * 16)
                for i in range(NT):
                    ins = pool.tensor_tensor(tok[:, i, :], tok[:, i, :], bc[name][:, :], ALU.add)
                tell(ins, "bias_added")

            rsqrt()
            add_bias("b_out", 1)
            pool.wait_ge(s["raw_in"], 16 * 8)
            for c, (r0, n) in enumerate(CH):
                for e in range(EA):
                    ins = pool.tensor_copy(rawo[0:n, c, e].rearrange("p h (a d) -> p h a d", a=PAIRS),
                                           raw[0:n, c, e, 3, :].rearrange("p (a h d) -> p h a d", a=PAIRS, h=2))
            tell(ins, "rawo_done")
            rsqrt()
            add_bias("b_ff2", 2)
            link(pool.memset(kbd, 0.0))
            link(pool.memset(kbdB, 0.0))
            link(pool.memset(vbd, 0.0))
            for k in range(2):
                for im in range(2):
                    r = slice(64 * im, 64 * im + 64)
                    ins = pool.memset(vbd[r, k, :, :, im, 2 * DH:2 * DH + 1], 1.0)
                    if (k, im) != (1, 1):
                        link(ins)
            tell(ins, "zeros_made")
            pool.wait_ge(s["decay_exp"], 1)
            for h in range(2):
                r = slice(64 * h, 64 * h + 64)
                ins = pool.affine_select(out=decay[r], in_=decay[r], compare_op=ALU.is_ge, fill=0.0, base=0,
                                         pattern=[[0, PAIRS], [1, S]], channel_multiplier=-1)
                if h == 0:
                    link(ins)
            tell(ins, "decay_done")
            rsqrt()
            pool.wait_ge(s["chain_in"], 1)
            pool.dma_start(chA[0:8], vrow.rearrange("o (b n) -> o b n", n=S)).then_inc(s["rowmv_in"], 16)
            pool.dma_start(chA[8:16], vrev.rearrange("o (b n) -> o b n", n=S)).then_inc(s["rowmv_in"], 16)
            pool.wait_ge(s["gu_mm"], NT)
            link(pool.memset(q3, 0.0))
            link(pool.memset(q3b, 0.0))
            tell(pool.memset(vbd3, 0.0), "zeros_made")
            pool.wait_ge(s["chain_in"], 2)
            pool.dma_start(chE, chS[8:16]).then_inc(s["chE_in"], 16)
            pool.wait_ge(s["feat_out"], 1)
            for k in range(2):
                pool.dma_start(frow[k:k + 1].rearrange("o (b n) -> o b n", n=S), chF[:, k, :]).then_inc(s["chF_in"], 16)
            rsqrt()
            pool.wait_ge(s["xT_mm"], 5)
            for i in range(NT):
                ins = pool.tensor_tensor(xn[:, i, :], xn[:, i, :], bc["ln_b"][:, :], ALU.add)
            tell(ins, "bias_added")
            rsqrt()
            rsqrt()
            pool.wait_ge(s["tok_done"], 4)
            tell(pool.memset(hmix, 0.0), "zeros_made")
            rsqrt()
            rsqrt(1, NC)

        @block.scalar
        def _(act):
            for j in range(3):
                act.wait_ge(s["xr_T"], 2 * j + 2)
                act.activation(patch_out(2 * j + 1), patch_in(2 * j + 1), ACT.Copy).then_inc(s["xpT_act"], 1)

            def turned_weights(e):
                act.wait_ge(s["wt_mm"], e + 1)
                act.activation(wT[:, 0, e, 0:2, :], ps[:, 0, 0:2 * D].rearrange("p (a b) -> p a b", a=2), ACT.Copy)
                act.activation(wT[:, 0, e, 2, :], ps[:, 1, 0:D], ACT.Copy)
                act.activation(wT[0:DB, 1, e, 2, :], ps[0:DB, 1, D:2 * D], ACT.Copy)
                act.activation(wguT[:, e, 0, :], ps[:, 4, 0:2 * D], ACT.Copy).then_inc(s["wt_act"], 1)

            act.wait_ge(s["colc_done"], 1)
            act.wait_ge(s["xT_mm"], 1)
            act.activation(xT[:, 0, :], ps[:, 6, :], ACT.Identity, bias=col(R_LNA + 1),
                           scale=col(R_LNA)).then_inc(s["xT_act"], 1)

            def exp0(hp):
                act.wait_ge(s["sub0"], hp + 1)
                act.activation(p0[:, hp % 2], p0[:, hp % 2], ACT.Exp, scale=DH0 ** -0.5).then_inc(s["exp0"], 1)

            def pT_out(hp):
                act.wait_ge(s["t0_mm"], hp + 1)
                if hp >= 2:
                    act.wait_ge(s["pv0_mm"], hp - 1)
                act.activation(pT0[:, hp % 2].rearrange("p a b -> p (a b)"), ps[:, 5, :],
                               ACT.Copy).then_inc(s["pT0_done"], 1)

            act.wait_ge(s["zeros_made"], 1)
            def q0_out(hp):
                act.wait_ge(s["q0_mm"], hp + 1)
                if hp >= 2:
                    act.wait_ge(s["s0_mm"], hp - 1)
                for h in range(2):
                    r = slice(64 * h, 64 * h + 64)
                    ins = act.activation(qbd[r, hp % 2, :, h, :],
                                         ps[r, 0, :].rearrange("p (b i) -> p b i", b=B), ACT.Copy)
                ins.then_inc(s["q0_done"], 1)

            q0_out(0)
            exp0(0)
            for hp in range(PAIRS):
                if hp + 1 < PAIRS:
                    q0_out(hp + 1)
                pT_out(hp)
                if hp + 1 < PAIRS:
                    exp0(hp + 1)
            turned_weights(0)
            turned_weights(1)
            act.wait_ge(s["xT_mm"], 2)
            act.activation(xT[:, 0, :], ps[:, 6, :], ACT.Identity, bias=col(R_LNA + 3),
                           scale=col(R_LNA + 2)).then_inc(s["xT_act"], 1)

            jobs = [0]

            def hidden(dst, bias0, func):
                for f in range(NF):
                    bank = jobs[0] % 4
                    jobs[0] += 1
                    act.wait_ge(s["h_mm"], jobs[0])
                    act.activation(dst[:, f, :], ps[:, bank, :], func, bias=col(bias0 + f)).then_inc(s["h_act"], 1)

            hidden(ffh, R_FF1, ACT.Gelu)
            turned_weights(2)
            turned_weights(3)
            act.wait_ge(s["xT_mm"], 3)
            act.activation(xT[:, 0, :], ps[:, 6, :], ACT.Copy).then_inc(s["xT_act"], 1)

            def k_out(e):
                for c, (r0, n) in enumerate(CH):
                    act.wait_ge(s["qk1_mm"], 4 * e + 2 * c + 2)
                    if c == 0 and e >= 1:
                        act.wait_ge(s["s1_mm"], NT * e)
                    for g in range(n // 32):
                        r = slice(32 * g, 32 * g + 32)
                        ins = act.activation((kbdB if c else kbd)[r, :, g, :],
                                             ps[r, 4 + 2 * c, :].rearrange("p (b j) -> p b j", b=B), ACT.Copy)
                    ins.then_inc(s["qk1_act"], 1)

            def exp1(n):
                act.wait_ge(s["sub1"], n + 1)
                act.activation(p1[:, n % 2], p1[:, n % 2], ACT.Exp).then_inc(s["exp1"], 1)

            def pT1_out(n):
                act.wait_ge(s["t1_mm"], n + 1)
                if n >= 2:
                    act.wait_ge(s["pv1_mm"], n - 1)
                act.activation(pT1[:, n % 2].rearrange("p (a b) c -> p a (b c)", a=2), ps[:, 0:2, 0:3 * P],
                               ACT.Copy).then_inc(s["pT1_done"], 1)

            act.wait_ge(s["zeros_made"], 2)
            k_out(0)
            exp1(0)
            for n in range(NT * EA + 2):
                e, t = divmod(n, NT)
                if t == 0 and 0 < n < NT * EA:
                    exp1(n)
                if t == NT - 1 and e < EA - 1:
                    k_out(e + 1)
                if n < NT * EA:
                    pT1_out(n)
                if t < NT - 1 and n + 1 < NT * EA:
                    exp1(n + 1)
                if t == 1 and e >= 1:
                    act.wait_ge(s["wo1_mm"], 2 * e - 1)
                    act.activation(fT[:, e - 1, 0, :], ps[:, 2, :], ACT.Copy).then_inc(s["fT_act"], 1)
            act.wait_ge(s["dist_ready"], 1)
            for p in range(PAIRS):
                ins = act.activation(decay[:, p, :], dist[:, :], ACT.Exp, scale=slope[:, p:p + 1])
            ins.then_inc(s["decay_exp"], 1)
            for i in range(NT):
                act.wait_ge(s["gu_mm"], i + 1)
                act.activation(gsb[:, i, :], ps[:, i, 0:D], ACT.Silu).then_inc(s["silu_done"], 1)
            act.wait_ge(s["xT_mm"], 4)
            act.activation(xT[:, 0, :], ps[:, 6, :], ACT.Copy).then_inc(s["xT_act"], 1)
            act.wait_ge(s["lg_sub"], 1)
            act.activation(lg, lg, ACT.Exp).then_inc(s["lg_exp"], 1)
            for e in range(EM):
                if e >= 2:
                    act.wait_ge(s["y_mm"], 1 + e - 1)
                hidden(hT[:, e % 2], R_MOE + NF * e, ACT.Gelu_apprx_tanh)
            act.wait_ge(s["xT_mm"], 5)
            act.activation(xT[:, 0, :], ps[:, 6, :], ACT.Copy).then_inc(s["xT_act"], 1)
            act.wait_ge(s["gate1_mm"], 1)
            act.activation(g1T, ps[0:16, 7, :], ACT.Copy).then_inc(s["gate1_done"], 1)
            act.wait_ge(s["zeros_made"], 3)
            for c, (r0, n) in enumerate(CH):
                act.wait_ge(s["q3_mm"], 2 * c + 1)
                for g in range(n // 32):
                    r = slice(32 * g, 32 * g + 32)
                    ins = act.activation((q3b if c else q3)[r, :, g, :],
                                         ps[r, 2 * c, :].rearrange("p (b i) -> p b i", b=B), ACT.Silu)
                ins.then_inc(s["q3_done"], 1)
                act.wait_ge(s["q3_mm"], 2 * c + 2)
                act.activation(ksb[0:n, c, :], ps[0:n, 2 * c + 1, :], ACT.Silu).then_inc(s["k3_done"], 1)
            for j in range(B // 2):
                act.wait_ge(s["v3_mm"], j + 1)
                bank = 4 + j % 2
                for h in range(2):
                    r = slice(64 * h, 64 * h + 64)
                    src = ps[r, bank, 0:2 * D].rearrange("p (m a h d) -> p m a h d", m=2, a=PAIRS, h=2)
                    for m in range(2):
                        ins = act.activation(vbd3[r, 2 * j + m, :, h, :], src[:, m, :, h, :], ACT.Silu)
                ins.then_inc(s["v3_done"], 1)
            act.wait_ge(s["gate3_mm"], 1)
            act.activation(pairs_of(gate3), two(6), ACT.Sigmoid).then_inc(s["gate3_done"], 1)
            act.wait_ge(s["xT_mm"], 6)
            act.activation(xT[:, 0, :], ps[:, 6, :], ACT.Copy).then_inc(s["xT_act"], 1)
            act.wait_ge(s["xT_mm"], 7)
            act.activation(xT[:, 0, :], ps[:, 6, :], ACT.Copy).then_inc(s["xT_act"], 1)
            act.wait_ge(s["cl_sub"], 1)
            act.activation(cls_l, cls_l, ACT.Exp).then_inc(s["cl_exp"], 1)
            hidden(hT[:, 0], R_M0, ACT.Gelu)
            for x in range(5):
                act.wait_ge(s["hc_add"], x + 1)
                act.activation(hcls[:, x], hcls[:, x], ACT.Gelu).then_inc(s["hc_done"], 1)

        @block.vector
        def _(dve):
            steps = [0]

            def link(ins):
                steps[0] += 1
                ins.then_inc(s["dve_step"], 1)
                dve.wait_ge(s["dve_step"], steps[0])

            dve.wait_ge(s["x_in"], 16 * B)
            for c in range(C):
                dve.tensor_copy(xq[:, c].rearrange("p w (r q) -> p r w q", r=8),
                                xr[:, c, :].rearrange("p (r w q) -> p r w q", r=8, w=GRID)).then_inc(s["xq_done"], 1)
            for j in range(3):
                dve.wait_ge(s["xr_T"], 2 * j + 1)
                dve.tensor_copy(patch_out(2 * j), patch_in(2 * j)).then_inc(s["xpT_dve"], 1)
            dve.wait_ge(s["colc_mm"], 1)
            dve.tensor_copy(colc[:, 0:NROWS], ps[:, 7, 384:384 + NROWS]).then_inc(s["colc_done"], 1)
            dve.wait_ge(s["consts_made"], 1)
            link(dve.tensor_scalar(par_i[:, :], par_i[:, :], 4, 1, ALU.logical_shift_right, ALU.bitwise_and))
            link(dve.tensor_copy(parity[:, 1:2], par_i[:, :]))
            link(dve.tensor_scalar(parity[:, 0:1], parity[:, 1:2], -1.0, 1.0, ALU.mult, ALU.add))
            link(dve.tensor_scalar(dist[:, :], dist[:, :], 0.0, None, ALU.max))

            lns = [0]

            def moments(src, n=NT, rows=P):
                lns[0] += 1
                for i in range(n):
                    ins = dve.bn_stats(bn[0:rows, i, :], src(i))
                link(ins)
                for i in range(n):
                    ins = dve.bn_aggr(mv[0:rows, i, :], bn[0:rows, i, :])
                ins.then_inc(s["var_ready"], 1)

            def normalise(src, dst, n=NT, rows=P, done="ln_done"):
                moments(src, n, rows)
                dve.wait_ge(s["rstd_ready"], lns[0])
                for i in range(n):
                    dve.tensor_scalar(dst(i), src(i), mv[0:rows, i, 0:1], rstd[0:rows, i:i + 1],
                                      ALU.subtract, ALU.mult).then_inc(s[done], 1)

            def of(x):
                return lambda i: x[:, i, :]

            dve.wait_ge(s["bcast_in"], 7 * 16)
            for j in range(2):
                dve.wait_ge(s["patch_mm"], j + 1)
                ins = dve.tensor_tensor(tok[:, 2 * j:2 * j + 2, :],
                                        ps[:, 6 + j, 0:2 * D].rearrange("p (a b) -> p a b", a=2),
                                        bc["b_patch"][:, :].unsqueeze(1).to_broadcast([P, 2, D]), ALU.add)
            link(ins)
            for h in range(2):
                r = slice(64 * h, 64 * h + 64)
                dve.tensor_copy(slope[r, :], slopes[r, :].rearrange("p (a h) -> p h a", h=2)[:, h])
            normalise(of(tok), of(xn))

            def turned_weights(e):
                dve.wait_ge(s["wt_mm"], e + 1)
                dve.tensor_copy(wT[0:DB, 1, e, 0:2, :], ps[0:DB, 2, 0:2 * D].rearrange("p (a b) -> p a b", a=2))
                dve.tensor_copy(woT[0:96, :, e, :], ps[0:96, 3, 0:2 * D].rearrange("p (a b) -> p a b", a=2))
                dve.tensor_copy(wguT[0:DB, e, 1, :], ps[0:DB, 5, 0:2 * D]).then_inc(s["wt_dve"], 1)

            dve.wait_ge(s["xT_mm"], 1)
            dve.tensor_scalar(xT[0:DB, 1, :], ps[0:DB, 7, :], col(R_LNB)[0:DB], col(R_LNB + 1)[0:DB],
                              ALU.mult, ALU.add).then_inc(s["xT_dve"], 1)

            def kv0(hp):
                k = hp % 2
                dve.wait_ge(s["k0_mm"], hp + 1)
                if hp >= 2:
                    dve.wait_ge(s["s0_mm"], hp - 1)
                dve.tensor_copy(kT0[:, k, :], ps[:, 1, :]).then_inc(s["kv0_done"], 1)
                dve.wait_ge(s["v0_mm"], hp + 1)
                if hp >= 2:
                    dve.wait_ge(s["pv0_mm"], hp - 1)
                dve.tensor_copy(v0[:, k].rearrange("p a b -> p (a b)"), ps[:, 2, :]).then_inc(s["kv0_done"], 1)

            def softmax0_in(hp):
                k = hp % 2
                dve.wait_ge(s["s0_mm"], hp + 1)
                if hp >= 2:
                    dve.wait_ge(s["t0_mm"], hp - 1)
                sc = ps[:, 3 + k, :].rearrange("p (b j) -> p b j", b=B)
                link(dve.tensor_reduce(mx0[:, 0, :], sc, AX.X, ALU.max))
                dve.tensor_tensor(p0[:, k], sc, mx0[:, 0, :].unsqueeze(2).to_broadcast([P, B, S]),
                                  ALU.subtract).then_inc(s["sub0"], 1)

            def softmax0_out(hp):
                k = hp % 2
                dve.wait_ge(s["exp0"], hp + 1)
                link(dve.tensor_reduce(mx0[:, 1, :], p0[:, k], AX.X, ALU.add))
                link(dve.reciprocal(mx0[:, 1, :], mx0[:, 1, :]))
                dve.tensor_tensor(p0[:, k], p0[:, k], mx0[:, 1, :].unsqueeze(2).to_broadcast([P, B, S]),
                                  ALU.mult).then_inc(s["p0_done"], 1)

            def out0(hp):
                dve.wait_ge(s["pv0_mm"], hp + 1)
                dve.tensor_copy(oT0[:, hp, :].rearrange("p (t m i) -> p m t i", t=NT, m=2),
                                ps[:, 6:8, 0:NT * S].rearrange("p m (t i) -> p m t i", t=NT)).then_inc(s["oT0_done"], 1)

            kv0(0)
            softmax0_in(0)
            softmax0_out(0)
            for hp in range(PAIRS):
                if hp + 1 < PAIRS:
                    kv0(hp + 1)
                    softmax0_in(hp + 1)
                out0(hp)
                if hp + 1 < PAIRS:
                    softmax0_out(hp + 1)

            toks = [0]

            def residual(bank, n):
                toks[0] += 1
                dve.wait_ge(s["tok_mm"], n)
                ins = dve.tensor_tensor(tok2, tok2, two(bank), ALU.add)
                ins.then_inc(s["tok_done"], 1)
                dve.wait_ge(s["tok_done"], toks[0])

            dve.wait_ge(s["bias_added"], 1)
            residual(0, 1)
            normalise(of(tok), of(xn))
            turned_weights(0)
            turned_weights(1)
            dve.wait_ge(s["xT_mm"], 2)
            dve.tensor_scalar(xT[0:DB, 1, :], ps[0:DB, 7, :], col(R_LNB + 2)[0:DB], col(R_LNB + 3)[0:DB],
                              ALU.mult, ALU.add).then_inc(s["xT_dve"], 1)
            dve.wait_ge(s["bias_added"], 2)
            residual(6, 2)
            turned_weights(2)
            turned_weights(3)
            dve.wait_ge(s["xT_mm"], 3)
            dve.tensor_copy(xT[0:DB, 1, :], ps[0:DB, 7, :]).then_inc(s["xT_dve"], 1)
            toks[0] += 1
            dve.engine_nop().then_inc(s["tok_done"], 1)

            def q_out(e):
                for c, (r0, n) in enumerate(CH):
                    dve.wait_ge(s["qk1_mm"], 4 * e + 2 * c + 1)
                    if c == 0 and e >= 1:
                        dve.wait_ge(s["s1_mm"], NT * e)
                    for h in range(2):
                        ins = dve.tensor_scalar(qm[0:n, c, :, h, :],
                                                ps[0:n, 3 + 2 * c, :].rearrange("p (b i) -> p b i", b=B),
                                                parity[0:n, h:h + 1], None, ALU.mult)
                    ins.then_inc(s["qk1_dve"], 1)

            def v_out(e):
                for j in range(2):
                    dve.wait_ge(s["v1_mm"], 2 * e + j + 1)
                    if j == 0 and e >= 2:
                        dve.wait_ge(s["pv1_mm"], NT * (e - 1))
                    for im in range(2):
                        r = slice(64 * im, 64 * im + 64)
                        ins = dve.tensor_copy(
                            vbd[r, e % 2, 2 * j:2 * j + 2, :, im, 0:2 * DH],
                            ps[r, 3 + j, 0:2 * D].rearrange("p (m a d) -> p m a d", m=2, a=PAIRS))
                    ins.then_inc(s["v1_done"], 1)

            def softmax1_in(n):
                k = n % 2
                dve.wait_ge(s["s1_mm"], n + 1)
                if n >= 2:
                    dve.wait_ge(s["t1_mm"], n - 1)
                pk = p1[:, k].rearrange("p a m j -> p (a m) j")
                for m in range(2):
                    ins = dve.scalar_tensor_tensor(
                        p1[:, k, :, m, :], ps[:, 3 + 2 * k + m, 0:PAIRS * S].rearrange("p (a j) -> p a j", a=PAIRS),
                        DH ** -0.5, causal[:, :].unsqueeze(1).to_broadcast([P, PAIRS, S]), ALU.mult, ALU.add)
                ins.then_inc(s["s1_read"], 1)
                dve.wait_ge(s["s1_read"], n + 1)
                link(dve.tensor_reduce(mx1[:, k, :], pk, AX.X, ALU.max))
                dve.tensor_tensor(pk, pk, mx1[:, k, :].unsqueeze(2).to_broadcast([P, 2 * PAIRS, S]),
                                  ALU.subtract).then_inc(s["sub1"], 1)

            def out1(n):
                k = n % 2
                dve.wait_ge(s["pv1_mm"], n + 1)
                if n >= 2:
                    dve.wait_ge(s["ot1_mm"], n - 1)
                o = ps[:, 7, 0:PAIRS * 2 * (2 * DH + 1)].rearrange("p (a m d) -> p m a d", a=PAIRS, m=2)
                rk = rc1[:, k, :].rearrange("p (m a) -> p m a", m=2)
                link(dve.reciprocal(rk, o[:, :, :, 2 * DH]))
                for h in range(2):
                    r = slice(64 * h, 64 * h + 64)
                    ins = dve.tensor_tensor(o1[r, k], o[r, :, :, h * DH:(h + 1) * DH],
                                            rk[r].unsqueeze(3).to_broadcast([64, 2, PAIRS, DH]), ALU.mult)
                ins.then_inc(s["o1_done"], 1)

            def oT_out(q):
                dve.wait_ge(s["ot1_mm"], 2 * q + 2)
                if q % 2 == 0 and q >= 2:
                    dve.wait_ge(s["wo1_mm"], q)
                at = 256 * (q % 2)
                dve.tensor_copy(
                    oT1[0:96, :, at:at + 256].rearrange("p h (m i) -> p h m i", m=4),
                    ps[0:96, 2, :].rearrange("p (m h i) -> p h m i", m=4, h=2)).then_inc(s["ot1_done"], 1)

            dve.wait_ge(s["zeros_made"], 2)
            q_out(0)
            v_out(0)
            softmax1_in(0)
            N1 = EA * NT
            for n in range(N1 + 3):
                e, t = divmod(n, NT)
                if t == 0 and 0 < n < N1:
                    softmax1_in(n)
                if t < NT - 1 and n + 1 < N1:
                    softmax1_in(n + 1)
                elif t == NT - 1 and e < EA - 1:
                    q_out(e + 1)
                    v_out(e + 1)
                if 1 <= n <= N1:
                    out1(n - 1)
                if t == 1 and e >= 1:
                    oT_out(2 * e - 1)
                elif t == 2 and e >= 1:
                    dve.wait_ge(s["wo1_mm"], 2 * e)
                    dve.tensor_copy(fT[0:DB, e - 1, 1, :], ps[0:DB, 2, :]).then_inc(s["fT_dve"], 1)
                elif t == 3 and n < N1:
                    oT_out(2 * e)
            dve.engine_nop().then_inc(s["dist_ready"], 1)
            for i in range(NT):
                dve.wait_ge(s["silu_done"], i + 1)
                ins = dve.tensor_tensor(gsb[:, i, :], gsb[:, i, :], ps[:, i, D:2 * D], ALU.mult)
            link(ins)
            link(dve.tensor_tensor(tok[:, :, :], tok[:, :, :], gsb, ALU.add))
            normalise(of(tok), of(xn))
            dve.wait_ge(s["xT_mm"], 4)
            dve.tensor_copy(xT[0:DB, 1, :], ps[0:DB, 7, :]).then_inc(s["xT_dve"], 1)

            dve.wait_ge(s["small_in"], 16 * 13)
            dve.wait_ge(s["v_mm"], 1)
            link(dve.tensor_scalar(vrow, ps[0:1, 4, :], vb[0:1], 3.0, ALU.add, ALU.min))
            link(dve.tensor_scalar(vrow, vrow, -3.0, -2.0, ALU.max, ALU.add))
            vr = vrow.rearrange("o (b n) -> o b n", n=S)
            dve.tensor_copy(vrev.rearrange("o (b n) -> o b n", n=S), vr[:, :, ::-1]).then_inc(s["chain_in"], 1)
            dve.wait_ge(s["lg_mm"], 1)
            gb = gateb[:, :].unsqueeze(1).to_broadcast([P, NT, EM])
            link(dve.tensor_tensor(lg, ps[:, 5, 0:NT * EM].rearrange("p (a b) -> p a b", a=NT), gb, ALU.add))
            link(dve.tensor_reduce(lmx, lg, AX.X, ALU.max))
            dve.tensor_tensor(lg, lg, lmx.unsqueeze(2).to_broadcast([P, NT, EM]),
                              ALU.subtract).then_inc(s["lg_sub"], 1)
            dve.wait_ge(s["lg_exp"], 1)
            link(dve.tensor_reduce(lmx, lg, AX.X, ALU.add))
            link(dve.reciprocal(lmx, lmx))
            link(dve.tensor_tensor(pr, lg, lmx.unsqueeze(2).to_broadcast([P, NT, EM]), ALU.mult))
            for i in range(NT):
                mine = pr[:, i, :].unsqueeze(2).to_broadcast([P, EM, EM])
                other = pr[:, i, :].unsqueeze(1).to_broadcast([P, EM, EM])
                dve.tensor_tensor(cmp[:, i], other, mine, ALU.is_gt)
                ins = dve.tensor_tensor(ceq[:, i], other, mine, ALU.is_equal)
            link(ins)
            for i in range(NT):
                ins = dve.tensor_tensor(ceq[:, i], ceq[:, i], lower, ALU.mult)
            link(ins)
            link(dve.tensor_tensor(cmp, cmp, ceq, ALU.add))
            link(dve.tensor_reduce(comb, cmp, AX.X, ALU.add))
            link(dve.scalar_tensor_tensor(comb, comb, 1.5, pr, ALU.is_lt, ALU.mult))
            link(dve.tensor_reduce(lmx, comb, AX.X, ALU.add))
            link(dve.reciprocal(lmx, lmx))
            dve.tensor_tensor(comb, comb, lmx.unsqueeze(2).to_broadcast([P, NT, EM]),
                              ALU.mult).then_inc(s["comb_done"], 1)
            dve.wait_ge(s["comb_done"], 1)
            link(dve.tensor_tensor(ow3[0:3], ow3[0:3], bk3[0:3], ALU.mult))
            dve.wait_ge(s["rowmv_in"], 32)
            dve.tensor_tensor(chB[:, :, 0], chA, alt, ALU.mult)
            link(dve.memset(chB[:, :, 1], -1.0))
            link(dve.tensor_copy(chS[:, 0, :], chB[:, 0, :]))

            def chain_step(n):
                link(dve.tensor_tensor_reduce(out=chr_[:, 0:2], in0=chS[:, n - 1, :], in1=chS[:, n - 1, :], scale=1.0,
                                              scalar=0.0, op0=ALU.mult, op1=ALU.add, accum_out=chr_[:, 2:3]))
                link(dve.reciprocal(chr_[:, 3:4], chr_[:, 2:3]))
                link(dve.scalar_tensor_tensor(chS[:, n, :], chS[:, n - 1, :], chr_[:, 3:4], chB[:, n, :],
                                              ALU.mult, ALU.add))

            def features():
                link(dve.tensor_tensor(chS[:, :, 0], chS[:, :, 0], alt, ALU.mult))
                dve.engine_nop().then_inc(s["chain_in"], 1)
                dve.wait_ge(s["chE_in"], 16)
                dve.tensor_tensor(chG[:, 0, :], chS[0:8, :, 0], chE[:, ::-1, 0], ALU.add)
                link(dve.tensor_tensor(chG[:, 1, :], chS[0:8, :, 1], chE[:, ::-1, 1], ALU.add))
                dve.tensor_tensor(chG[:, 0, :], chG[:, 0, :], chA[0:8], ALU.subtract)
                link(dve.tensor_scalar(chG[:, 1, :], chG[:, 1, :], 1.0, None, ALU.add))
                link(dve.tensor_tensor(chQ, chG, chG, ALU.mult))
                link(dve.tensor_tensor(chQ[:, 0, :], chQ[:, 0, :], chQ[:, 1, :], ALU.add))
                link(dve.reciprocal(chQ[:, 1, :], chQ[:, 0, :]))
                dve.tensor_tensor(chF[:, 0, :], chG[:, 0, :], chQ[:, 1, :], ALU.mult)
                link(dve.scalar_tensor_tensor(chF[:, 1, :], chG[:, 1, :], -1.0, chQ[:, 1, :], ALU.mult, ALU.mult))
                dve.tensor_scalar(chF, chF, 10.0, -10.0, ALU.min, ALU.max).then_inc(s["feat_out"], 1)

            PER = -(-(S - 1) // (EM - 3))
            for e in range(EM):
                if e == EM - 2:
                    dve.wait_ge(s["extra_mm"], 1)
                    dve.tensor_tensor(xn2, xn2, two(6), ALU.add).then_inc(s["extra_done"], 1)
                    dve.wait_ge(s["extra_done"], 1)
                dst = xn if e < EM - 1 else tok
                dve.wait_ge(s["y_mm"], 1 + e + 1)
                for i in range(NT):
                    ins = dve.scalar_tensor_tensor(dst[:, i, :], two_t(4 + 2 * (e % 2), i), comb[:, i, e:e + 1],
                                                   xn[:, i, :], ALU.mult, ALU.add)
                ins.then_inc(s["y_done"], 1)
                dve.wait_ge(s["y_done"], e + 1)
                if e == 0:
                    dve.wait_ge(s["combT_mm"], 1)
                    dve.tensor_copy(combT[0:EM], ps[0:EM, 6, :]).then_inc(s["combT_done"], 1)
                for n in range(1 + PER * e, min(S, 1 + PER * (e + 1))):
                    chain_step(n)
                if e == EM - 4:
                    features()
            normalise(of(tok), of(xn))
            dve.wait_ge(s["xT_mm"], 5)
            dve.tensor_copy(xT[0:DB, 1, :], ps[0:DB, 7, :]).then_inc(s["xT_dve"], 1)

            dve.wait_ge(s["xT_act"], 5)
            dve.wait_ge(s["xT_dve"], 5)
            for c, (r0, n) in enumerate(CH):
                ins = dve.tensor_copy(xd[0:n, c], xT[0:n, c, :].rearrange("p (b i) -> p b i", b=B)
                                      .unsqueeze(2).to_broadcast([n, B, 2, S]))
            ins.then_inc(s["xd_done"], 1)
            for c, (r0, n) in enumerate(CH):
                dve.wait_ge(s["k3_done"], c + 1)
                for h in range(2):
                    ins = dve.tensor_scalar(km3[0:n, c, :, h, :], ksb[0:n, c, :].rearrange("p (b i) -> p b i", b=B),
                                            parity[0:n, h:h + 1], None, ALU.mult)
                ins.then_inc(s["km_done"], 1)
            dve.wait_ge(s["decay_done"], 1)
            for t in range(NT):
                dve.wait_ge(s["e3_mm"], t + 1)
                ins = dve.tensor_tensor(
                    E3[t // 2][:, t % 2].rearrange("p a m i -> p m a i"),
                    ps[:, 2 * (t % 2):2 * (t % 2) + 2, 0:PAIRS * S].rearrange("p m (a i) -> p m a i", a=PAIRS),
                    decay[:, :, :].unsqueeze(1).to_broadcast([P, 2, PAIRS, S]), ALU.mult)
                ins.then_inc(s["e3_done"], 1)
            dve.wait_ge(s["gate3_done"], 1)
            dve.wait_ge(s["pv3_mm"], 1)
            dve.tensor_tensor(pairs_of(gate3), pairs_of(gate3), two(4), ALU.mult).then_inc(s["og_done"], 1)
            dve.wait_ge(s["xT_mm"], 6)
            dve.tensor_copy(xT[0:DB, 1, :], ps[0:DB, 7, :]).then_inc(s["xT_dve"], 1)
            dve.wait_ge(s["tok_mm"], 3)
            moments(lambda i: two_t(0, i))
            link(dve.engine_nop())
            for i in range(NT):
                ins = dve.scalar_tensor_tensor(tok[:, i, :], two_t(0, i), mv[:, i, 0:1], bc["ln_w"][:, :],
                                               ALU.subtract, ALU.mult)
            link(ins)
            dve.wait_ge(s["rstd_ready"], lns[0])
            dve.wait_ge(s["bias_added"], 3)
            for i in range(NT):
                ins = dve.scalar_tensor_tensor(tok[:, i, :], tok[:, i, :], rstd[:, i:i + 1], xn[:, i, :],
                                               ALU.mult, ALU.add)
            link(ins)
            normalise(of(tok), of(xn))
            dve.wait_ge(s["xT_mm"], 7)
            dve.tensor_copy(xT[0:DB, 1, :], ps[0:DB, 7, :]).then_inc(s["xT_dve"], 1)
            toks[0] += 1
            dve.engine_nop().then_inc(s["tok_done"], 1)
            dve.wait_ge(s["xT_act"], 7)
            dve.wait_ge(s["xT_dve"], 7)
            for c, (r0, n) in enumerate(CH):
                ins = dve.tensor_copy(xcls[0:n, c, :].rearrange("p (i b) -> p i b", i=NCLS),
                                      xT[0:n, c, :].rearrange("p (b n) -> p n b", n=S)[:, 0:NCLS, :])
            ins.then_inc(s["xcls_done"], 1)

            dve.wait_ge(s["xcls_done"], 1)
            dve.memset(ones, 1.0)
            for c, (r0, n) in enumerate(CH):
                for q in range(2):
                    ins = dve.tensor_tensor(xg[0:n, c, q, :].rearrange("p (i b) -> p i b", i=NCLS),
                                            xcls[0:n, c, :].rearrange("p (i b) -> p i b", i=NCLS),
                                            gwc[0:n, c, :, q:q + 1].to_broadcast([n, NCLS, B]), ALU.mult)
            ins.then_inc(s["xg_done"], 1)
            dve.wait_ge(s["cl_mm"], 1)
            cl = ps[:, 4, 0:2 * NC].rearrange("p (q n) -> p q n", q=2)
            link(dve.tensor_copy(cls_l, cl))
            link(dve.tensor_tensor(cls_s, cls_l[:, 0, :], cls_l[:, 1, :], ALU.max))
            dve.tensor_tensor(cls_l, cls_l, cls_s.unsqueeze(1).to_broadcast([P, 2, NC]),
                              ALU.subtract).then_inc(s["cl_sub"], 1)
            dve.wait_ge(s["cl_exp"], 1)
            link(dve.tensor_tensor(cls_s, cls_l[:, 0, :], cls_l[:, 1, :], ALU.add))
            link(dve.reciprocal(cls_s, cls_s))
            link(dve.tensor_tensor(cls_l, cls_l, cls_s.unsqueeze(1).to_broadcast([P, 2, NC]), ALU.mult))
            dve.tensor_tensor(cls_m[:, 0, :], cls_l[:, 0, :], cls_l[:, 1, :], ALU.is_gt)
            link(dve.tensor_tensor(cls_m[:, 1, :], cls_l[:, 1, :], cls_l[:, 0, :], ALU.is_gt))
            for i in range(NCLS):
                n = slice(i * B, (i + 1) * B)
                dve.tensor_copy(mcls[:, 3 + i % 2, n], cls_m[:, 0, n])
                ins = dve.tensor_copy(mcls[:, i // 2, n], cls_m[:, 1, n])
            ins.then_inc(s["mcls_done"], 1)
            for x in range(5):
                dve.wait_ge(s["hc_mm"], x + 1)
                src = ps[:, 6 + x % 2, 0:NF * NC].rearrange("p (f n) -> p f n", f=NF)
                bias = colc[:, R_A1 + NF * x:R_A1 + NF * (x + 1)].unsqueeze(2).to_broadcast([P, NF, NC])
                dve.tensor_tensor(hcls[:, x], src, bias, ALU.add).then_inc(s["hc_add"], 1)
            dve.wait_ge(s["bcast_in"], 7 * 16)
            link(dve.tensor_tensor(tok[:, :, :], xn[:, :, :],
                                   bc["m0_b2"][:, :].unsqueeze(1).to_broadcast([P, NT, D]), ALU.add))
            dve.wait_ge(s["zeros_made"], 4)
            dve.wait_ge(s["mcls_done"], 1)
            for x in range(5):
                dve.wait_ge(s["hc_done"], x + 1)
            for i in range(NCLS):
                n = slice(i * B, (i + 1) * B)
                for first, then, g in ((i // 2, 3 + i % 2, 0), (3 + i % 2, i // 2, 1)):
                    ins = dve.tensor_tensor(hmix[:, then, :, n], hcls[:, first, :, n],
                                            cls_m[:, g, n].unsqueeze(1).to_broadcast([P, NF, B]), ALU.mult)
            ins.then_inc(s["hmix_done"], 1)
            toks[0] += 1
            dve.wait_ge(s["y_mm"], 10)
            dve.tensor_tensor(tok2, tok2, two(4), ALU.add).then_inc(s["tok_done"], 1)
            dve.wait_ge(s["tok_done"], toks[0])
            normalise(of(tok), of(xn), done="fin_ready")
            dve.wait_ge(s["clsx_mm"], 1)
            link(dve.tensor_copy(clsx[0:NC], ps[0:NC, 2, 0:D]))
            dve.wait_ge(s["cls_mm"], 1)
            link(dve.tensor_tensor(clsx[0:NC], clsx[0:NC], ps[0:NC, 3, 0:D], ALU.add))
            normalise(lambda i: clsx[0:NC], lambda i: clsx[0:NC], 1, NC, done="fin_ready")

        @block.tensor
        def _(pe):
            def mm(o, l, r, start, stop):
                return pe.matmul(o, l, r, start=start, stop=stop)

            def tr(o, i):
                k = i.shape[0]
                return pe.transpose(o, i, ident[0:k, 0:k])

            pe.wait_ge(s["ident_made"], 1)
            for j in range(2 * C):
                c, half = divmod(j, 2)
                if half == 0:
                    pe.wait_ge(s["xq_done"], c + 1)
                for w in range(4):
                    ins = tr(ps[:, j, w * P:(w + 1) * P], xq[:, c, 4 * half + w, :])
                ins.then_inc(s["xr_T"], 1)
            pe.wait_ge(s["wpatch_in"], 16)
            pe.wait_ge(s["xpT_act"], 3)
            pe.wait_ge(s["xpT_dve"], 3)
            for i in range(NT):
                for k in range(2 * C):
                    ins = mm(two_t(6, i), xpT[:, k, i * P:(i + 1) * P], wpatch[:, k % 2, k // 2, :],
                             k == 0, k == 2 * C - 1)
                if i % 2:
                    ins.then_inc(s["patch_mm"], 1)
            pe.wait_ge(s["rows_in"], 16 * 12)
            tr(ps[:, 7, 384:384 + NROWS], rowc[0:NROWS, :]).then_inc(s["colc_mm"], 1)

            def turn_weights(e):
                pe.wait_ge(s["raw_in"], 16 * 8)
                pe.wait_ge(s["rawg_in"], 16 * 4)
                pe.wait_ge(s["rawo_done"], 1)
                if e >= 1:
                    pe.wait_ge(s["wt_act"], e)
                    pe.wait_ge(s["wt_dve"], e)
                for oc, (o0, on) in enumerate(CH):
                    for m in range(3):
                        for ic, (i0, n) in enumerate(CH):
                            bank, at = ((2 if ic else 0), m * D) if m < 2 else (1, ic * D)
                            tr(ps[0:n, bank, at + o0:at + o0 + on], raw[0:on, oc, e, m, i0:i0 + n])
                    for h in range(2):
                        tr(ps[0:96, 3, h * D + o0:h * D + o0 + on], rawo[0:on, oc, e, h, :])
                    for m in range(2):
                        for ic, (i0, n) in enumerate(CH):
                            ins = tr(ps[0:n, 4 + ic, m * D + o0:m * D + o0 + on],
                                     rawg[0:on, oc, m, e * D + i0:e * D + i0 + n])
                ins.then_inc(s["wt_mm"], 1)

            def turn_tokens(x, n, normed=None):
                for i in range(NT):
                    if normed:
                        pe.wait_ge(s["ln_done"], NT * (normed - 1) + i + 1)
                    for c, (r0, rn) in enumerate(CH):
                        ins = tr(ps[0:rn, 6 + c, i * P:(i + 1) * P], x[:, i, r0:r0 + rn])
                ins.then_inc(s["xT_mm"], 1)

            def xT_ready(n):
                pe.wait_ge(s["xT_act"], n)
                pe.wait_ge(s["xT_dve"], n)

            pe.wait_ge(s["colc_done"], 1)
            turn_tokens(xn, 1, 1)
            xT_ready(1)
            pe.wait_ge(s["wqkv_in"], 32)

            def project0(hp):
                for m in range(2):
                    if hp >= 1:
                        pe.wait_ge(s["q0_done" if m == 0 else "kv0_done"], hp if m == 0 else 2 * hp - 1)
                    for c, (r0, n) in enumerate(CH):
                        at = m * H * DH0 + hp * P
                        ins = mm(ps[:, m, :], wqkv[0:n, c, at:at + P], xT[0:n, c, :], c == 0, c == 1)
                    ins.then_inc(s["q0_mm" if m == 0 else "k0_mm"], 1)
                if hp >= 1:
                    pe.wait_ge(s["kv0_done"], 2 * hp)
                at = 2 * H * DH0 + hp * P
                for i in range(NT):
                    for c, (r0, n) in enumerate(CH):
                        ins = mm(ps[:, 2, i * P:(i + 1) * P], xT[0:n, c, i * P:(i + 1) * P], wqkv[0:n, c, at:at + P],
                                 c == 0, c == 1)
                ins.then_inc(s["v0_mm"], 1)

            def scores0(hp):
                k = hp % 2
                pe.wait_ge(s["q0_done"], hp + 1)
                pe.wait_ge(s["kv0_done"], 2 * hp + 1)
                if hp >= 2:
                    pe.wait_ge(s["sub0"], hp - 1)
                for b in range(B):
                    ins = mm(ps[:, 3 + k, b * S:(b + 1) * S], qbd[:, k, b].rearrange("p h i -> p (h i)"),
                             kT0[:, k, b * S:(b + 1) * S], True, True)
                ins.then_inc(s["s0_mm"], 1)

            def turn0(hp):
                k = hp % 2
                pe.wait_ge(s["p0_done"], hp + 1)
                if hp >= 1:
                    pe.wait_ge(s["pT0_done"], hp)
                for i in range(NT):
                    ins = tr(ps[:, 5, i * P:(i + 1) * P], p0[:, k, 2 * i:2 * i + 2, :].rearrange("p b j -> p (b j)"))
                ins.then_inc(s["t0_mm"], 1)

            def values0(hp):
                k = hp % 2
                pe.wait_ge(s["pT0_done"], hp + 1)
                pe.wait_ge(s["kv0_done"], 2 * hp + 2)
                if hp >= 1:
                    pe.wait_ge(s["oT0_done"], hp)
                for b in range(B):
                    r = slice(64 * (b % 2), 64 * (b % 2) + 64)
                    for h in range(2):
                        ins = mm(ps[64 * h:64 * h + 64, 6 + b % 2, b // 2 * S:(b // 2 + 1) * S], v0[r, k, b // 2, 64 * h:64 * h + 64],
                                 pT0[r, k, b // 2, 64 * h:64 * h + 64], True, True)
                ins.then_inc(s["pv0_mm"], 1)

            project0(0)
            scores0(0)
            for hp in range(PAIRS):
                if hp + 1 < PAIRS:
                    project0(hp + 1)
                turn0(hp)
                if hp + 1 < PAIRS:
                    scores0(hp + 1)
                values0(hp)
            pe.wait_ge(s["oT0_done"], PAIRS)
            pe.wait_ge(s["wout_in"], 16)
            for i in range(NT):
                for k in range(PAIRS):
                    ins = mm(two_t(0, i), oT0[:, k, i * P:(i + 1) * P], wout[:, k, :], k == 0, k == PAIRS - 1)
            ins.then_inc(s["tok_mm"], 1)
            pe.wait_ge(s["tok_done"], 1)
            turn_weights(0)
            turn_weights(1)
            turn_tokens(xn, 2, 2)
            xT_ready(2)
            pe.wait_ge(s["wt_act"], 2)
            pe.wait_ge(s["wt_dve"], 2)

            jobs = [0]

            def up(w, tiles=range(NF)):
                for f in tiles:
                    if jobs[0] >= 4:
                        pe.wait_ge(s["h_act"], jobs[0] - 3)
                    bank = jobs[0] % 4
                    jobs[0] += 1
                    for c, (r0, n) in enumerate(CH):
                        ins = mm(ps[:, bank, :], w[0:n, c, f * P:(f + 1) * P], xT[0:n, c, :], c == 0, c == 1)
                    ins.then_inc(s["h_mm"], 1)

            def down(h, w, bank):
                for i in range(NT):
                    for f in range(NF):
                        ins = mm(two_t(bank, i), h[:, f, i * P:(i + 1) * P], w[:, f, :], f == 0, f == NF - 1)
                ins.then_inc(s["y_mm"], 1)
                return ins

            pe.wait_ge(s["ff_in"], 48)
            up(wff1)
            pe.wait_ge(s["h_act"], jobs[0])
            for i in range(NT):
                for f in range(NF):
                    ins = mm(two_t(6, i), ffh[:, f, i * P:(i + 1) * P], wff2[:, f, :], f == 0, f == NF - 1)
            ins.then_inc(s["tok_mm"], 1)
            turn_weights(2)
            turn_weights(3)
            pe.wait_ge(s["tok_done"], 2)
            turn_tokens(tok, 3)
            xT_ready(3)
            pe.wait_ge(s["wt_act"], 4)
            pe.wait_ge(s["wt_dve"], 4)
            pe.nop().then_inc(s["y_mm"], 1)

            def project1(e):
                for c, (r0, n) in enumerate(CH):
                    if c == 1 and e >= 1:
                        pe.wait_ge(s["s1_read"], NT * e)
                    for m in range(2):
                        for k, (k0, kn) in enumerate(CH):
                            ins = mm(ps[0:n, 3 + 2 * c + m, :], wT[0:kn, k, e, m, r0:r0 + n], xT[0:kn, k, :],
                                     k == 0, k == 1)
                        ins.then_inc(s["qk1_mm"], 1)
                for j in range(2):
                    pe.wait_ge(s["qk1_dve" if j == 0 else "qk1_act"], 2 * e + 1)
                    for m in range(2):
                        i = 2 * j + m
                        for k, (k0, kn) in enumerate(CH):
                            ins = mm(ps[:, 3 + j, m * D:m * D + D], xT[0:kn, k, i * P:(i + 1) * P],
                                     wT[0:kn, k, e, 2, :], k == 0, k == 1)
                    ins.then_inc(s["v1_mm"], 1)

            def scores1(n):
                e, t = divmod(n, NT)
                if t == 0:
                    pe.wait_ge(s["qk1_dve"], 2 * e + 2)
                    pe.wait_ge(s["qk1_act"], 2 * e + 2)
                    pe.wait_ge(s["v1_done"], 2 * e + 2)
                if n >= 2:
                    pe.wait_ge(s["s1_read"], n - 1)
                for m in range(2):
                    b, bank = 2 * t + m, 3 + 2 * (n % 2) + m
                    mm(ps[:, bank, 0:4 * S], qm[:, 0, b].rearrange("p h i -> p (h i)"),
                       kbd[:, b].rearrange("p a j -> p (a j)"), True, True)
                    ins = mm(ps[:, bank, 4 * S:6 * S], qm[0:DB, 1, b].rearrange("p h i -> p (h i)"),
                             kbdB[0:DB, b].rearrange("p a j -> p (a j)"), True, True)
                ins.then_inc(s["s1_mm"], 1)

            def turn1(n):
                pe.wait_ge(s["exp1"], n + 1)
                if n >= 1:
                    pe.wait_ge(s["pT1_done"], n)
                for p in range(PAIRS):
                    ins = tr(ps[:, p // 3, (p % 3) * P:(p % 3 + 1) * P], p1[:, n % 2, p].rearrange("p m j -> p (m j)"))
                ins.then_inc(s["t1_mm"], 1)

            def values1(n):
                e, t = divmod(n, NT)
                pe.wait_ge(s["pT1_done"], n + 1)
                pe.wait_ge(s["v1_done"], 2 * e + 1 + t // 2)
                if n >= 1:
                    pe.wait_ge(s["o1_done"], n)
                w = 2 * (2 * DH + 1)
                for p in range(PAIRS):
                    ins = mm(ps[:, 7, p * w:(p + 1) * w], pT1[:, n % 2, p, :],
                             vbd[:, e % 2, t, p].rearrange("p m d -> p (m d)"), True, True)
                ins.then_inc(s["pv1_mm"], 1)

            def turn_o(n):
                pe.wait_ge(s["o1_done"], n + 1)
                if n % 2 == 0 and n >= 2:
                    pe.wait_ge(s["ot1_done"], n // 2)
                if n % NT == 0 and n >= NT:
                    pe.wait_ge(s["fT_dve"], n // NT)
                for m in range(2):
                    at = (2 * (n % 2) + m) * P
                    ins = tr(ps[0:96, 2, at:at + P], o1[:, n % 2, m].rearrange("p a d -> p (a d)"))
                ins.then_inc(s["ot1_mm"], 1)

            def join(e, c):
                if c == 0:
                    pe.wait_ge(s["ot1_done"], 2 * e + 2)
                else:
                    pe.wait_ge(s["fT_act"], e + 1)
                r0, n = CH[c]
                for h in range(2):
                    ins = mm(ps[0:n, 2, :], woT[0:96, h, e, r0:r0 + n], oT1[0:96, h, :], h == 0, h == 1)
                ins.then_inc(s["wo1_mm"], 1)

            pe.wait_ge(s["zeros_made"], 2)
            project1(0)
            scores1(0)
            N1 = EA * NT
            for n in range(N1 + 3):
                e, t = divmod(n, NT)
                if t == 0 and 0 < n < N1:
                    scores1(n)
                if t < NT - 1 and n + 1 < N1:
                    scores1(n + 1)
                elif t == NT - 1 and e < EA - 1:
                    project1(e + 1)
                if 1 <= n <= N1:
                    values1(n - 1)
                if n < N1:
                    turn1(n)
                if t == 1 and e >= 1:
                    turn_o(n - 2)
                    join(e - 1, 0)
                elif t == 2 and e >= 1:
                    join(e - 1, 1)
                    if n < N1:
                        turn_o(n - 2)
                elif 2 <= n <= N1 + 1:
                    turn_o(n - 2)
            pe.wait_ge(s["fT_act"], EA)
            pe.wait_ge(s["fT_dve"], EA)
            for i in range(NT):
                for e in range(EA):
                    for c, (r0, n) in enumerate(CH):
                        ins = mm(ps[:, i, 0:2 * D], fT[0:n, e, c, i * P:(i + 1) * P], wguT[0:n, e, c, :],
                                 e == 0 and c == 0, e == EA - 1 and c == 1)
                ins.then_inc(s["gu_mm"], 1)
            turn_tokens(xn, 4, 3)
            xT_ready(4)

            pe.wait_ge(s["small_in"], 16 * 13)
            for c, (r0, n) in enumerate(CH):
                ins = mm(ps[0:1, 4, :], vw[0:n, c, :], xT[0:n, c, :], c == 0, c == 1)
            ins.then_inc(s["v_mm"], 1)
            for i in range(NT):
                for c, (r0, n) in enumerate(CH):
                    ins = mm(ps[:, 5, i * EM:(i + 1) * EM], xT[0:n, c, i * P:(i + 1) * P], gw[0:n, c, :],
                             c == 0, c == 1)
            ins.then_inc(s["lg_mm"], 1)
            for e in range(EM + 1):
                if e < EM:
                    pe.wait_ge(slot_in[e % NSLOT], 48 * (e // NSLOT + 1))
                    up(w1s[:, e % NSLOT])
                if e == 1:
                    pe.wait_ge(s["comb_done"], 1)
                    for i in range(NT):
                        ins = tr(ps[0:EM, 6, i * P:(i + 1) * P], comb[:, i, :])
                    ins.then_inc(s["combT_mm"], 1)
                if e == EM - 1:
                    pe.wait_ge(s["chF_in"], 32)
                    pe.wait_ge(s["y_done"], EM - 2)
                    for i in range(NT):
                        mm(two_t(6, i), combT[0:EM, i * P:(i + 1) * P], b2m[0:EM], True, False)
                        ins = mm(two_t(6, i), frow[:, i * P:(i + 1) * P], ow3[0:3], False, True)
                    ins.then_inc(s["extra_mm"], 1)
                if e >= 1:
                    d = e - 1
                    if d == EM - 1:
                        pe.wait_ge(s["extra_done"], 1)
                    if d == 1:
                        pe.wait_ge(s["combT_done"], 1)
                    if d >= 2:
                        pe.wait_ge(s["y_done"], d - 1)
                    pe.wait_ge(s["h_act"], NF * (d + 2))
                    down(hT[:, d % 2], w2s[:, d % NSLOT], 4 + 2 * (d % 2))
            turn_tokens(xn, 5, 4)
            xT_ready(5)

            pe.wait_ge(s["s3_in"], 16 * 11)
            for c, (r0, n) in enumerate(CH):
                ins = mm(ps[0:16, 7, :], wg1[0:n, c, :], xT[0:n, c, :], c == 0, c == 1)
            ins.then_inc(s["gate1_mm"], 1)
            for c, (r0, n) in enumerate(CH):
                for m in range(2):
                    for k, (k0, kn) in enumerate(CH):
                        ins = mm(ps[0:n, 2 * c + m, :], wq3[0:kn, m, k, r0:r0 + n], xT[0:kn, k, :], k == 0, k == 1)
                    ins.then_inc(s["q3_mm"], 1)
            pe.wait_ge(s["xd_done"], 1)
            for j in range(B // 2):
                if j >= 2:
                    pe.wait_ge(s["v3_done"], j - 1)
                for m in range(2):
                    b = 2 * j + m
                    for k, (k0, kn) in enumerate(CH):
                        img = xd[0:kn, k, b].rearrange("p h i -> p (h i)")
                        ins = mm(ps[:, 4 + j % 2, m * D:(m + 1) * D], img, wq3[0:kn, 2, k, :], k == 0, k == 1)
                ins.then_inc(s["v3_mm"], 1)
            pe.wait_ge(s["gate1_done"], 1)
            for i in range(NT):
                ins = mm(two_t(6, i), g1T[:, i * P:(i + 1) * P], wg2, True, True)
            ins.then_inc(s["gate3_mm"], 1)
            pe.wait_ge(s["q3_done"], 2)
            pe.wait_ge(s["km_done"], 2)
            pe.wait_ge(s["v3_done"], B // 2)

            def values3(t):
                pe.wait_ge(s["e3_done"], t + 1)
                for m in range(2):
                    for p in range(PAIRS):
                        at = t % 2 * D + p * 2 * DH
                        ins = mm(ps[64 * m:64 * m + 64, 4 + t // 2, at:at + 2 * DH], E3[t // 2][:, t % 2, p, m, :],
                                 vbd3[:, 2 * t + m, p].rearrange("p h d -> p (h d)"), True, True)
                return ins

            for t in range(NT):
                if t >= 2:
                    pe.wait_ge(s["e3_done"], t - 1)
                for m in range(2):
                    b, bank = 2 * t + m, 2 * (t % 2) + m
                    mm(ps[:, bank, 0:4 * S], km3[:, 0, b].rearrange("p h i -> p (h i)"),
                       q3[:, b].rearrange("p a i -> p (a i)"), True, True)
                    ins = mm(ps[:, bank, 4 * S:6 * S], km3[0:DB, 1, b].rearrange("p h i -> p (h i)"),
                             q3b[0:DB, b].rearrange("p a i -> p (a i)"), True, True)
                ins.then_inc(s["e3_mm"], 1)
                if t >= 1:
                    values3(t - 1)
            values3(NT - 1).then_inc(s["pv3_mm"], 1)
            pe.wait_ge(s["og_done"], 1)
            turn_tokens(gate3, 6)
            xT_ready(6)
            for i in range(NT):
                for k, (k0, kn) in enumerate(CH):
                    ins = mm(two_t(0, i), xT[0:kn, k, i * P:(i + 1) * P], wq3[0:kn, 3, k, :], k == 0, k == 1)
            ins.then_inc(s["tok_mm"], 1)
            turn_tokens(xn, 7, 5)
            xT_ready(7)

            def cls(c, n):
                return xcls[0:n, c, :]

            pe.wait_ge(s["xcls_done"], 1)

            pe.wait_ge(s["m0_in"], 48)
            up(m0w1, range(2))
            pe.wait_ge(s["xg_done"], 1)
            for c, (r0, n) in enumerate(CH):
                ins = mm(ps[:, 4, 0:2 * NC], ones[0:n], xg[0:n, c].rearrange("p q n -> p (q n)"), c == 0, c == 1)
            ins.then_inc(s["cl_mm"], 1)
            up(m0w1, range(2, NF))
            pe.wait_ge(s["a_in"], 16 * 15)
            for x in range(5):
                if x >= 2:
                    pe.wait_ge(s["hc_add"], x - 1)
                for f in range(NF):
                    for c, (r0, n) in enumerate(CH):
                        ins = mm(ps[:, 6 + x % 2, f * NC:(f + 1) * NC], a1w[0:n, x, c, f * P:(f + 1) * P], cls(c, n),
                                 c == 0, c == 1)
                ins.then_inc(s["hc_mm"], 1)
            pe.wait_ge(s["h_act"], jobs[0])
            pe.wait_ge(s["cl_sub"], 1)
            down(hT[:, 0], m0w2, 4)
            for c, (r0, n) in enumerate(CH):
                ins = tr(ps[0:NC, 2, r0:r0 + n], cls(c, n))
            ins.then_inc(s["clsx_mm"], 1)
            pe.wait_ge(s["hmix_done"], 1)
            for x in range(5):
                for f in range(NF):
                    mm(ps[0:NC, 3, 0:D], hmix[:, x, f, :], a2w[:, x, f, :], x == 0 and f == 0, False)
            for x in range(5):
                ins = mm(ps[0:NC, 3, 0:D], mcls[0:1, x, :], a2b[0:1, x, :], False, x == 4)
            ins.then_inc(s["cls_mm"], 1)


_INS = {
    "x": "x", "w_patch": "L0_tok_w_patch", "b_patch": "L0_tok_b_patch", "g1": "L0_tok_g1", "beta1": "L0_tok_beta1",
    "w_qkv": "L0_tok_w_qkv", "w_out": "L0_tok_w_out", "b_out": "L0_tok_b_out", "g2": "L0_tok_g2",
    "beta2": "L0_tok_beta2", "w_ff1": "L0_tok_w_ff1", "b_ff1": "L0_tok_b_ff1", "w_ff2": "L0_tok_w_ff2",
    "b_ff2": "L0_tok_b_ff2", "wq": "L0_attn_wq", "wk": "L0_attn_wk", "wv": "L0_attn_wv", "wo": "L0_attn_wo",
    "w_gate": "L0_attn_w_gate", "w_up": "L0_attn_w_up", "v_w": "L0_ffn_v_w", "v_b": "L0_ffn_v_b",
    "gate_w": "L0_ffn_gate_w", "gate_b": "L0_ffn_gate_b", "w1": "L0_ffn_w1", "b1": "L0_ffn_b1", "w2": "L0_ffn_w2",
    "b2": "L0_ffn_b2", "out_w": "L0_ffn_out_w", "out_b": "L0_ffn_out_b", "bk": "L0_ffn_bk_scale",
    "slope": "L1_attn_log_slope", "Wq": "L1_attn_Wq", "Wk": "L1_attn_Wk", "Wv": "L1_attn_Wv", "Wo": "L1_attn_Wo",
    "Wg1": "L1_attn_Wg1", "Wg2": "L1_attn_Wg2", "ln_w": "L1_attn_ln_w", "ln_b": "L1_attn_ln_b",
    "m0w1": "L1_ffn_moe0_W1", "m0_b1": "L1_ffn_moe0_b1", "m0w2": "L1_ffn_moe0_W2", "m0_b2": "L1_ffn_moe0_b2",
    "a1w": "L1_ffn_A1_W", "a1b": "L1_ffn_A1_b", "a2w": "L1_ffn_A2_W", "a2b": "L1_ffn_A2_b", "gcls": "L1_ffn_G_W",
}


def kernel(**inputs):
    import numpy as _np
    import concourse.bacc as _bacc
    from concourse import mybir as _mybir
    from concourse.bass_utils import run_bass_kernel_spmd as _run

    nc = _bacc.Bacc("TRN2", target_bir_lowering=False, num_devices=1)
    arrays, args = {}, {}
    for short, name in _INS.items():
        v = _np.ascontiguousarray(inputs[name])
        if v.ndim == 0:
            v = v.reshape(1)
        arrays[f"in_{short}"] = v
        args[short] = nc.dram_tensor(f"in_{short}", v.shape, _mybir.dt.from_np(v.dtype), kind="ExternalInput").ap()
    out = nc.dram_tensor("out_0", (8, 64, 192), _mybir.dt.float32, kind="ExternalOutput").ap()
    vit_tower(nc, args, out)
    r = _run(nc, [arrays], core_ids=[0])
    return r.results[0]["out_0"]
```

```python
from contextlib import ExitStack

import numpy as np

import concourse.bass as bass
from concourse import mybir

F32 = mybir.dt.float32
I32 = mybir.dt.int32
F32R = mybir.dt.float32r
ALU = mybir.AluOpType
ACT = mybir.ActivationFunctionType
AX = mybir.AxisListType

P = 128
B, C, IMG, PATCH = 8, 3, 128, 16
GRID = IMG // PATCH
S = GRID * GRID
T = B * S
NT = T // P
D = 192
DB = D - P
CH = ((0, P), (P, DB))
H = 12
PAIRS = H // 2
DH0 = 64
DH = D // H
MLP = 768
NF = MLP // P
EA = 4
EM = 8
NCLS = 6
NC = NCLS * B
EPS = 1e-5
NEG = -1e30
QK = ((0, 0, P, 0), (1, 0, P, P), (0, P, DB, 2 * P), (1, P, DB, 2 * P + DB))
R_FF1, R_MOE, R_M0, R_A1, R_LNA, R_LNB = 0, NF, NF * 9, NF * 10, NF * 15, NF * 15 + 4
NROWS = R_LNB + 4
TURN_OF = {1: 1, 2: 2, 3: 4, 4: 7}


def vit_tower(nc, a, out):
    ctx = ExitStack()
    with ctx:
        def sb(name, shape, dt=F32):
            return ctx.enter_context(nc.sbuf_tensor(name, shape, dt))

        def sem(name):
            return ctx.enter_context(nc.semaphore(name))

        def carve(region):
            at = [0]

            def take(*dims, rows=P):
                n = int(np.prod(dims))
                v = region[0:rows, at[0]:at[0] + n]
                at[0] += n
                assert at[0] <= region.shape[1], at[0]
                names = ["a", "b", "c", "d", "e"][:len(dims)]
                if len(dims) > 1:
                    v = v.rearrange(f"p ({' '.join(names)}) -> p {' '.join(names)}", **dict(zip(names, dims)))
                return v
            return take

        ps = ctx.enter_context(nc.psum_tensor("ps", [P, 8, 512], F32))

        ident = sb("ident", [P, P])
        tok = sb("tok", [P, NT, D])
        xn = sb("xn", [P, NT, D])
        xT = sb("xT", [P, 2, T])
        rowc = sb("rowc", [P, P])
        colc = sb("colc", [P, P])
        bn = sb("bn", [P, NT, 6])
        mv = sb("mv", [P, NT, 2])
        rstd = sb("rstd", [P, NT])
        neghalf = sb("neghalf", [P, NT])
        spare = sb("spare", [P, 1])
        causal = sb("causal", [P, S])
        par_i = sb("par_i", [P, 1], I32)
        parity = sb("parity", [P, 2])
        bc = {n: sb("bc_" + n, [P, D]) for n in
              ("b_patch", "b_out", "b_ff2", "ln_w", "ln_b", "m0_b2")}
        gateb = sb("gateb", [P, EM])
        slopes = sb("slopes", [P, H])
        slope = sb("slope", [P, PAIRS])
        dist = sb("dist", [P, S])
        decay = sb("decay", [P, PAIRS, S])

        front = sb("front", [P, 22960])
        wide_at = nc.sbuf_base
        wide = sb("wide", [P, 9216])
        turned_at = nc.sbuf_base
        turned = sb("turned", [P, 9216])

        take = carve(front)
        wqkv = take(2, 3 * H * DH0)
        wout = take(PAIRS, D)
        wpatch = take(2, C, D)
        wff1 = take(2, MLP)
        wff2 = take(NF, D)
        oT0 = take(PAIRS, T)
        qbd = take(2, B, 2, S)
        kT0 = take(2, T)
        v0 = take(2, NT, P)
        p0 = take(2, B, S)
        pT0 = take(2, NT, P)
        mx0 = take(2, B)
        take = carve(front[:, 9600:])
        xr = take(C, 1024)
        xpT = take(2 * C, T)
        xq = take(C, GRID, P)
        ffh = carve(front[:, 9600 + PAIRS * T:])(NF, T)
        rawo = carve(front[:, 19600:])(2, EA, 2, PAIRS * DH)
        del take

        take = carve(front)
        kbd = take(B, 4, S)
        kbdB = take(B, 2, S)
        vbd = take(2, NT, PAIRS, 2, 2 * DH + 1)
        qm = take(2, B, 2, S)
        p1 = take(2, PAIRS, 2, S)
        pT1 = take(2, PAIRS, P)
        mx1 = take(2, 2 * PAIRS)
        rc1 = take(2, 2 * PAIRS)
        o1 = take(2, 2, PAIRS, DH)
        oT1 = take(2, T)
        fT = take(EA, 2, T)
        gsb = take(NT, D)
        last_at = 19600

        takew = carve(wide)
        raw = takew(2, EA, 4, D)
        rawg = takew(2, 2, MLP)
        takew = carve(wide)
        NSLOT = 3
        w1s = takew(NSLOT, 2, MLP)
        w2s = takew(NSLOT, NF, D)
        m0w2 = takew(NF, D)
        HALF = 2 * 12 * D
        wguT, wT, woT = [], [], []
        for g in range(2):
            taket = carve(turned[:, g * HALF:(g + 1) * HALF])
            for take_one, n in ((wguT, 2 * 2 * D), (wT, 2 * 3 * D), (woT, 2 * D)):
                for e in range(2):
                    v = taket(n)
                    take_one.append(v.rearrange("p (c n) -> p c n", c=2))

        class Split:

            def __init__(self, v, n, tokens=False):
                self.high, self.low, self.both = (v[:, k * n:(k + 1) * n] for k in range(3))
                self.lowB = v[0:DB, 3 * n:4 * n] if tokens else None

        halves = nc.alloc_sbuf_tensor_at("halves", [P, 9216], F32R, offset=turned_at)
        xs_at, w_at = HALF - D * 4, (4 * 2 * D, HALF + 4 * 2 * D)
        xs = Split(halves[:, xs_at:xs_at + 4 * T], T, True)
        w1x = [Split(halves[:, w_at[k]:w_at[k] + 3 * MLP], MLP) for k in (1, 0)]
        xs0 = Split(halves[:, HALF:HALF + 4 * T], T, True)
        wqkx = Split(halves[:, 0:HALF], 2 * H * DH0)
        wffx = Split(halves[:, HALF + 4 * T:HALF + 4 * T + 3 * MLP], MLP)
        halves_w = nc.alloc_sbuf_tensor_at("halves_w", [P, 9216], F32R, offset=wide_at)
        m0_at = 2 * 2 * PAIRS * 2 * S
        wm0x = Split(halves_w[:, m0_at:m0_at + 3 * MLP], MLP)

        take = carve(front[:, last_at:])
        m0w1 = take(2, MLP)
        wqk3 = take(2, 2 * D)
        wvo3 = take(2, 2, D)
        wg1 = take(2, 16)
        wg2 = take(D, rows=16)
        take = carve(front)
        hT = take(2, NF, T)
        a1w = take(5, 2, MLP)
        a2w = take(5, NF, D)
        take = carve(turned[:, xs_at:])
        km3 = take(2, B, 2, S)
        q3 = take(B, 4, S)
        q3b = take(B, 2, S)
        vbd3 = carve(turned)(B, PAIRS, 2, DH)
        assert B * PAIRS * 2 * DH <= w_at[0] and w_at[0] + 3 * MLP <= xs_at
        take = carve(turned[:, w_at[0]:w_at[0] + 3 * MLP])
        ksb = take(2, T)
        g1T = take(T, rows=16)
        gate3 = take(NT, D)
        takew = carve(wide)
        E3 = takew(2, PAIRS, 2, S), takew(2, PAIRS, 2, S)
        take = carve(turned)
        hcls = take(5, NF, NC)
        hmix = take(5, NF, NC)
        small = sb("small", [P, 3540])
        take = carve(small)
        gw = take(2, EM)
        gwc = take(2, NCLS, 2)
        vw = take(2, 1)
        vb = take(1)
        lg = take(NT, EM)
        pr = take(NT, EM)
        cmp = take(NT, EM, EM)
        ceq = take(NT, EM, EM)
        lower = take(EM, EM)
        lmx = take(NT)
        comb = take(NT, EM)
        combT = take(T)
        b2m = take(D)
        ow3 = take(D)
        bk3 = take(D)
        clsx = take(D)
        xcls = take(2, NC)
        cls_l = take(2, NC)
        cls_m = take(2, NC)
        cls_s = take(NC)
        mcls = take(5, NC)
        a2b = take(5, D)
        xg = cmp.rearrange("p a b c -> p (a b c)")[:, 0:4 * NC].rearrange("p (a b c) -> p a b c", a=2, b=2)
        ones = ceq.rearrange("p a b c -> p (a b c)")[:, 0:P]
        del take
        line = sb("line", [16, 5, T])
        vrow, vrev, frow = line[0:1, 0, :], line[0:1, 1, :], line[0:3, 2, :]
        take = carve(line[0:16, 3:5, :].rearrange("p a b -> p (a b)"))
        chA = take(S, rows=16)
        alt = take(S, rows=16)
        chr_ = take(4, rows=16)
        chB = take(S, 2, rows=16)
        chS = take(S, 2, rows=16)
        chE = take(S, 2, rows=8)
        chG = take(2, S, rows=8)
        chQ = take(2, S, rows=8)
        chF = take(2, S, rows=8)

        names = """wpatch_in rows_in bcast_in wqkv_in wout_in ff_in raw_in rawg_in small_in
            s3_in m0_in a_in rowmv_in chE_in chF_in out_done
            ident_made xq_done rawo_done xcls_done consts_made rows_zero colc_mm colc_done
            xr_T xpT_act xpT_dve patch_mm
            wt_mm wt_act wt_dve
            var_ready rstd_ready ln_done xT_mm xT_act xT_dve
            q0_mm k0_mm v0_mm q0_done k0_done v0_done s0_mm sub0 exp0 p0_done t0_mm pT0_done
            pv0_mm oT0_done zeros_made
            tok_mm tok_done bias_added
            mixer_left h_mm h_act y_mm y_half y_done
            qk1_mm qk1_dve qk1_act v1_mm v1_done s1_mm s1_read sub1 exp1 t1_mm pT1_done pv1_mm o1_done
            ot1_mm ot1_done wo1_mm fT_act fT_dve gu_mm silu_done
            lg_mm lg_sub lg_exp comb_done combT_mm combT_done v_mm chain_in feat_out extra_mm extra_done
            gate1_mm gate1_done gate3_mm gate3_done q3_mm q3_done k3_done v3_mm v3_done km_done
            e3_mm e3_done pv3_mm og_done decay_exp decay_done dist_ready
            xg_done cl_mm cl_sub cl_exp mcls_done hc_mm hc_add hc_done hmix_done cls_mm clsx_mm 
            w1_hi w1_lo xs_hiA xs_hi xs_lo wx_hiA wx_hi wx_lo wqkvB_in bpatch_in
            fin_ready dve_step pool_step """.split()
        s = {n: sem(n) for n in names}
        x_in = [sem(f"x_in{i}") for i in range(C)]
        w1_in = [sem(f"w1_in{i}") for i in range(NSLOT)]
        w2_in = [sem(f"w2_in{i}") for i in range(NSLOT)]

        def col(i):
            return colc[:, i:i + 1]

        def two(bank):
            return ps[:, bank:bank + 2, 0:2 * D]

        def two_t(bank, i):
            return ps[:, bank + i // 2, (i % 2) * D:(i % 2) * D + D]

        def pairs_of(x):
            return x.rearrange("p (a b) d -> p a (b d)", a=2)

        tok2, xn2 = pairs_of(tok[:, :, :]), pairs_of(xn[:, :, :])

        def patch_in(j):
            return ps[:, j, :].rearrange("p (w b h) -> p h b w", w=4, h=2)

        def patch_out(j):
            c, half = divmod(j, 2)
            v = xpT[:, 2 * c:2 * c + 2, :].rearrange("p h (b w) -> p h b w", w=GRID)
            return v[:, :, :, 4 * half:4 * half + 4]

        block = ctx.enter_context(nc.Block())

        @block.sync
        def _(sp):
            def load(dst, src, name):
                sp.dma_start(dst, src).then_inc(s[name], 16)

            for c in range(C):
                sp.dma_start(xr[:, c, :], a["x"][:, c].rearrange("b (hh r) w -> b hh (r w)", r=8)).then_inc(x_in[c], 16)
            load(wpatch.rearrange("p a c n -> p a (c n)"),
                 a["w_patch"].rearrange("(ph k c) n -> k ph (c n)", ph=2, c=C), "wpatch_in")
            QKC = 2 * H * DH0
            load(wqkv[:, 0], a["w_qkv"][0:P], "wqkv_in")
            load(wqkv[0:DB, 1], a["w_qkv"][P:D], "wqkvB_in")
            load(wqkv[DB:P, 1, 0:QKC], a["w_qkv"][P:D, 0:QKC], "wqkvB_in")
            load(bc["b_patch"][:, :], a["b_patch"].partition_broadcast(P), "bpatch_in")
            sp.wait_ge(s["rows_zero"], 1)
            for r, name in ((R_FF1, "b_ff1"), (R_M0, "m0_b1")):
                load(rowc[r:r + NF], a[name].rearrange("(f p) -> f p", p=P), "rows_in")
            load(rowc[R_MOE:R_MOE + NF * EM], a["b1"].rearrange("e (f p) -> (e f) p", p=P), "rows_in")
            load(rowc[R_A1:R_A1 + NF * 5], a["a1b"].rearrange("e (f p) -> (e f) p", p=P), "rows_in")
            for k, name in enumerate(("g1", "beta1", "g2", "beta2")):
                g = a[name].rearrange("(o n) -> o n", o=1)
                load(rowc[R_LNA + k:R_LNA + k + 1], g[:, 0:P], "rows_in")
                for at in (0, DB):
                    load(rowc[R_LNB + k:R_LNB + k + 1, at:at + DB], g[:, P:D], "rows_in")
            for n in ("b_out", "b_ff2", "ln_w", "ln_b", "m0_b2"):
                load(bc[n][:, :], a[n].partition_broadcast(P), "bcast_in")
            load(slopes[:, :], a["slope"].partition_broadcast(P), "bcast_in")
            for m, name in enumerate(("wq", "wk", "wv", "wo")):
                w = a[name].rearrange("e o i -> o e i")
                load(raw[:, 0, :, m, :], w[0:P], "raw_in")
                load(raw[0:DB, 1, :, m, :], w[P:D], "raw_in")
            for m, name in enumerate(("w_gate", "w_up")):
                load(rawg[:, 0, m, :], a[name][0:P], "rawg_in")
                load(rawg[0:DB, 1, m, :], a[name][P:D], "rawg_in")
            load(wout, a["w_out"].rearrange("(f p) n -> p f n", p=P), "wout_in")
            load(wff1[:, 0], a["w_ff1"][0:P], "ff_in")
            load(wff1[0:DB, 1], a["w_ff1"][P:D], "ff_in")
            load(wff1[DB:P, 1], a["w_ff1"][P:D], "ff_in")
            load(wff2, a["w_ff2"].rearrange("(f p) n -> p f n", p=P), "ff_in")
            for c, (r0, n) in enumerate(CH):
                load(gw[0:n, c, :], a["gate_w"][r0:r0 + n], "small_in")
                load(vw[0:n, c, :], a["v_w"].rearrange("(p o) -> p o", o=1)[r0:r0 + n], "small_in")
                load(gwc[0:n, c, :, :], a["gcls"].rearrange("i d q -> d i q")[r0:r0 + n], "small_in")
            load(vb[0:1], a["v_b"].rearrange("(p o) -> p o", o=1), "small_in")
            load(gateb[:, :], a["gate_b"].partition_broadcast(P), "small_in")
            load(b2m[0:EM], a["b2"], "small_in")
            load(ow3[0:2], a["out_w"], "small_in")
            load(ow3[2:3], a["out_b"].rearrange("(o n) -> o n", o=1), "small_in")
            load(bk3[0:3], a["bk"].partition_broadcast(3), "small_in")
            load(a2b[0:1], a["a2b"].rearrange("(o e) n -> o e n", o=1), "small_in")
            sp.wait_ge(s["mixer_left"], 1)
            for c, (r0, n) in enumerate(CH):
                for m, c0, cn, at in QK:
                    load(wqk3[0:n, c, at:at + cn], a[("Wq", "Wk")[m]][r0:r0 + n, c0:c0 + cn], "s3_in")
                for m, name in enumerate(("Wv", "Wo")):
                    load(wvo3[0:n, m, c, :], a[name][r0:r0 + n], "s3_in")
            for c, (r0, n) in enumerate(CH):
                load(wg1[0:n, c, :], a["Wg1"][r0:r0 + n], "s3_in")
                load(m0w1[0:n, c], a["m0w1"][r0:r0 + n], "m0_in")
            load(m0w1[DB:P, 1], a["m0w1"][P:D], "m0_in")
            load(wg2, a["Wg2"], "s3_in")
            sp.wait_ge(s["wt_mm"], EA)
            load(m0w2, a["m0w2"].rearrange("(f p) n -> p f n", p=P), "m0_in")
            for e in range(EM):
                k = e % NSLOT
                if e >= NSLOT:
                    sp.wait_ge(s["w1_lo"], e - NSLOT + 1)
                for r0, n, at in ((0, P, slice(0, P)), (P, DB, slice(0, DB)), (P, DB, slice(DB, P))):
                    sp.dma_start(w1s[at, k, min(r0, 1)], a["w1"][e, r0:r0 + n]).then_inc(w1_in[k], 16)
                if e >= NSLOT:
                    sp.wait_ge(s["y_mm"], e - NSLOT + 1)
                sp.dma_start(w2s[:, k], a["w2"][e].rearrange("(f p) n -> p f n", p=P)).then_inc(w2_in[k], 16)
                if e == NSLOT - 1:
                    sp.wait_ge(s["gu_mm"], NT)
                    sp.wait_ge(s["silu_done"], NT)
                    sp.wait_ge(s["ln_done"], 3 * NT)
                    for x in range(5):
                        for c, (r0, n) in enumerate(CH):
                            load(a1w[0:n, x, c], a["a1w"][x, r0:r0 + n], "a_in")
                        load(a2w[:, x], a["a2w"][x].rearrange("(f p) n -> p f n", p=P), "a_in")
            o3 = out
            for b in range(B):
                sp.wait_ge(s["fin_ready"], b // 2 + 1)
                r = S * (b % 2)
                sp.dma_start(o3[b, NCLS:S, :], xn[r + NCLS:r + S, b // 2, :]).then_inc(s["out_done"], 16)
            sp.wait_ge(s["fin_ready"], NT + 1)
            sp.dma_start(o3[:, 0:NCLS, :].rearrange("b i d -> i b d"), clsx[0:NC, :]).then_inc(s["out_done"], 16)
            sp.wait_ge(s["out_done"], 16 * (B + 1))

        @block.gpsimd
        def _(pool):
            steps = [0]

            def link(ins):
                steps[0] += 1
                ins.then_inc(s["pool_step"], 1)
                pool.wait_ge(s["pool_step"], steps[0])

            told = {}

            def tell(ins, name):
                told[name] = told.get(name, 0) + 1
                ins.then_inc(s[name], 1)
                pool.wait_ge(s[name], told[name])

            link(pool.memset(ident[:, :], 0.0))
            tell(pool.affine_select(out=ident[:, :], in_=ident[:, :], compare_op=ALU.not_equal, fill=1.0, base=0,
                                    pattern=[[-1, P]], channel_multiplier=1), "ident_made")
            tell(pool.memset(rowc[:, :], 0.0), "rows_zero")
            link(pool.memset(neghalf[:, :], -0.5))
            link(pool.iota(par_i[:, :], pattern=[[0, 1]], base=0, channel_multiplier=1))
            link(pool.memset(causal[:, :], 0.0))
            for h in range(2):
                r = slice(64 * h, 64 * h + 64)
                link(pool.affine_select(out=causal[r], in_=causal[r], compare_op=ALU.is_ge, fill=NEG, base=0,
                                        pattern=[[-1, S]], channel_multiplier=1))
                link(pool.iota(dist[r, :], pattern=[[1, S]], base=0, channel_multiplier=-1,
                               allow_small_or_imprecise_dtypes=True))
            link(pool.memset(lower, 1.0))
            link(pool.affine_select(out=lower, in_=lower, compare_op=ALU.is_gt, fill=0.0, base=0,
                                    pattern=[[1, EM], [-1, EM]], channel_multiplier=0))
            link(pool.memset(alt, -1.0))
            link(pool.memset(alt.rearrange("p (n c) -> p n c", c=2)[:, :, 0], 1.0))
            link(pool.memset(frow, 1.0))
            tell(pool.memset(mcls, 0.0), "consts_made")
            pool.wait_ge(s["patch_mm"], 2)
            for k in range(2):
                for h in range(2):
                    ins = pool.memset(qbd[64 * h:64 * h + 64, k, :, 1 - h, :], 0.0)
                    if (k, h) != (1, 1):
                        link(ins)
            tell(ins, "zeros_made")

            lns = [0]

            def rsqrt(g, rows=P, n=2):
                lns[0] += 1
                i = slice(2 * g, 2 * g + n)
                pool.wait_ge(s["var_ready"], lns[0])
                link(pool.tensor_scalar(rstd[0:rows, i], mv[0:rows, i, 1], EPS, None, ALU.add))
                tell(pool.tensor_tensor(rstd[0:rows, i], rstd[0:rows, i], neghalf[0:rows, i], ALU.pow), "rstd_ready")

            def norm():
                rsqrt(0)
                rsqrt(1)

            def add_bias(name, n):
                pool.wait_ge(s["ln_done"], NT * n)
                if n == 1:
                    pool.wait_ge(s["bcast_in"], 6 * 16)
                for i in range(NT):
                    ins = pool.tensor_tensor(tok[:, i, :], tok[:, i, :], bc[name][:, :], ALU.add)
                tell(ins, "bias_added")

            norm()
            add_bias("b_out", 1)
            pool.wait_ge(s["raw_in"], 16 * 8)
            for c, (r0, n) in enumerate(CH):
                for e in range(EA):
                    ins = pool.tensor_copy(rawo[0:n, c, e].rearrange("p h (a d) -> p h a d", a=PAIRS),
                                           raw[0:n, c, e, 3, :].rearrange("p (a h d) -> p h a d", a=PAIRS, h=2))
            tell(ins, "rawo_done")
            norm()
            add_bias("b_ff2", 2)
            link(pool.memset(kbd, 0.0))
            link(pool.memset(kbdB, 0.0))
            link(pool.memset(vbd, 0.0))
            for k in range(2):
                for im in range(2):
                    r = slice(64 * im, 64 * im + 64)
                    ins = pool.memset(vbd[r, k, :, :, im, 2 * DH:2 * DH + 1], 1.0)
                    if (k, im) != (1, 1):
                        link(ins)
            tell(ins, "zeros_made")
            pool.wait_ge(s["decay_exp"], 1)
            for h in range(2):
                r = slice(64 * h, 64 * h + 64)
                ins = pool.affine_select(out=decay[r], in_=decay[r], compare_op=ALU.is_ge, fill=0.0, base=0,
                                         pattern=[[0, PAIRS], [1, S]], channel_multiplier=-1)
                if h == 0:
                    link(ins)
            tell(ins, "decay_done")
            norm()
            pool.wait_ge(s["chain_in"], 1)
            pool.dma_start(chA[0:8], vrow.rearrange("o (b n) -> o b n", n=S)).then_inc(s["rowmv_in"], 16)
            pool.dma_start(chA[8:16], vrev.rearrange("o (b n) -> o b n", n=S)).then_inc(s["rowmv_in"], 16)
            pool.wait_ge(s["chain_in"], 2)
            pool.dma_start(chE, chS[8:16]).then_inc(s["chE_in"], 16)
            pool.wait_ge(s["feat_out"], 1)
            for k in range(2):
                pool.dma_start(frow[k:k + 1].rearrange("o (b n) -> o b n", n=S), chF[:, k, :]).then_inc(s["chF_in"], 16)
            pool.wait_ge(s["h_mm"], NF * EM)
            link(pool.memset(q3, 0.0))
            link(pool.memset(q3b, 0.0))
            tell(pool.memset(vbd3, 0.0), "zeros_made")
            norm()
            pool.wait_ge(s["xT_mm"], 5)
            for i in range(NT):
                ins = pool.tensor_tensor(xn[:, i, :], xn[:, i, :], bc["ln_b"][:, :], ALU.add)
            tell(ins, "bias_added")
            norm()
            norm()
            pool.wait_ge(s["xT_mm"], 7)
            tell(pool.memset(hmix, 0.0), "zeros_made")
            norm()
            rsqrt(0, NC, 1)

        @block.scalar
        def _(act):
            for j in range(3):
                act.wait_ge(s["xr_T"], 2 * j + 2)
                act.activation(patch_out(2 * j + 1), patch_in(2 * j + 1), ACT.Copy).then_inc(s["xpT_act"], 1)

            def weights_high(w, raw_w, second=None):
                act.activation(w.high, raw_w[:, 0, 0:w.high.shape[1]], ACT.Copy).then_inc(s["wx_hiA"], 1)
                if second is not None:
                    act.wait_ge(second, 32)
                act.activation(w.both, raw_w[:, 1, 0:w.high.shape[1]], ACT.Copy).then_inc(s["wx_hi"], 1)

            def tokens_out(n, x, bank, norm=None):
                def out_of(dst, src, c):
                    if norm is None:
                        return act.activation(dst, src, ACT.Copy)
                    r = (R_LNA, R_LNB)[c] + norm
                    return act.activation(dst, src, ACT.Identity, bias=col(r + 1), scale=col(r))

                act.wait_ge(s["xT_mm"], n)
                out_of(xT[:, 0, :], ps[:, bank, :], 0).then_inc(s["xT_act"], 1)
                out_of(x.high, ps[:, bank, :], 0).then_inc(s["xs_hiA"], 1)
                act.wait_ge(s["xT_dve"], n)
                out_of(x.both, ps[:, bank + 1, :], 1).then_inc(s["xs_hi"], 1)

            act.wait_ge(s["wqkv_in"], 16)
            weights_high(wqkx, wqkv, s["wqkvB_in"])

            def turned_weights(e):
                act.wait_ge(s["wt_mm"], e + 1)
                act.activation(wT[e][:, 0, 0:2 * D], ps[:, 0, 0:2 * D], ACT.Copy)
                act.activation(wT[e][:, 0, 2 * D:3 * D], ps[:, 1, 0:D], ACT.Copy)
                act.activation(wT[e][0:DB, 1, 2 * D:3 * D], ps[0:DB, 1, D:2 * D], ACT.Copy)
                act.activation(wguT[e][:, 0, :], ps[:, 4, 0:2 * D], ACT.Copy).then_inc(s["wt_act"], 1)

            act.wait_ge(s["colc_done"], 1)
            tokens_out(1, xs0, 6, norm=0)

            def exp0(hp):
                act.wait_ge(s["sub0"], hp + 1)
                act.activation(p0[:, hp % 2], p0[:, hp % 2], ACT.Exp, scale=DH0 ** -0.5).then_inc(s["exp0"], 1)

            def pT_out(hp):
                act.wait_ge(s["t0_mm"], hp + 1)
                if hp >= 2:
                    act.wait_ge(s["pv0_mm"], hp - 1)
                act.activation(pT0[:, hp % 2].rearrange("p a b -> p (a b)"), ps[:, 5, :],
                               ACT.Copy).then_inc(s["pT0_done"], 1)

            act.wait_ge(s["zeros_made"], 1)
            def q0_out(hp):
                act.wait_ge(s["q0_mm"], hp + 1)
                if hp >= 2:
                    act.wait_ge(s["s0_mm"], hp - 1)
                for h in range(2):
                    r = slice(64 * h, 64 * h + 64)
                    ins = act.activation(qbd[r, hp % 2, :, h, :],
                                         ps[r, 0, :].rearrange("p (b i) -> p b i", b=B), ACT.Copy)
                ins.then_inc(s["q0_done"], 1)

            def v0_out(hp):
                act.wait_ge(s["v0_mm"], hp + 1)
                if hp >= 2:
                    act.wait_ge(s["pv0_mm"], hp - 1)
                act.activation(v0[:, hp % 2].rearrange("p a b -> p (a b)"), ps[:, 2, :],
                               ACT.Copy).then_inc(s["v0_done"], 1)

            v0_out(0)
            q0_out(0)
            exp0(0)
            for hp in range(PAIRS):
                if hp + 1 < PAIRS:
                    q0_out(hp + 1)
                    v0_out(hp + 1)
                pT_out(hp)
                if hp + 1 < PAIRS:
                    exp0(hp + 1)
            act.wait_ge(s["ff_in"], 64)
            weights_high(wffx, wff1)
            turned_weights(0)
            turned_weights(1)
            tokens_out(2, xs0, 6, norm=2)

            jobs = [0]

            def hidden(dst, bias0, func, tiles=range(NF)):
                for f in tiles:
                    bank = jobs[0] % 4
                    jobs[0] += 1
                    act.wait_ge(s["h_mm"], jobs[0])
                    act.activation(dst[:, f, :], ps[:, bank, :], func, bias=col(bias0 + f)).then_inc(s["h_act"], 1)

            hidden(ffh, R_FF1, ACT.Gelu)
            turned_weights(2)
            turned_weights(3)
            act.wait_ge(s["xT_mm"], 3)
            act.activation(xT[:, 0, :], ps[:, 6, :], ACT.Copy).then_inc(s["xT_act"], 1)

            def k_out(e):
                for c, (r0, n) in enumerate(CH):
                    act.wait_ge(s["qk1_mm"], 3 * e + c + 2)
                    if c == 0 and e >= 1:
                        act.wait_ge(s["s1_mm"], NT * e)
                    for g in range(n // 32):
                        r = slice(32 * g, 32 * g + 32)
                        src = ps[DB + 32 * g:DB + 32 * g + 32, 5, :] if c else ps[r, 4, :]
                        ins = act.activation((kbdB if c else kbd)[r, :, g, :],
                                             src.rearrange("p (b j) -> p b j", b=B), ACT.Copy)
                    ins.then_inc(s["qk1_act"], 1)

            def v_out(e):
                for j in range(2):
                    act.wait_ge(s["v1_mm"], 2 * e + j + 1)
                    if j == 0 and e >= 2:
                        act.wait_ge(s["pv1_mm"], NT * (e - 1))
                    for im in range(2):
                        r = slice(64 * im, 64 * im + 64)
                        ins = act.activation(
                            vbd[r, e % 2, 2 * j:2 * j + 2, :, im, 0:2 * DH],
                            ps[r, 5 + j, 0:2 * D].rearrange("p (m a d) -> p m a d", m=2, a=PAIRS), ACT.Copy)
                    ins.then_inc(s["v1_done"], 1)

            def exp1(n):
                act.wait_ge(s["sub1"], n + 1)
                act.activation(p1[:, n % 2], p1[:, n % 2], ACT.Exp).then_inc(s["exp1"], 1)

            def pT1_out(n):
                act.wait_ge(s["t1_mm"], n + 1)
                if n >= 2:
                    act.wait_ge(s["pv1_mm"], n - 1)
                act.activation(pT1[:, n % 2].rearrange("p (a b) c -> p a (b c)", a=2), ps[:, 0:2, 0:3 * P],
                               ACT.Copy).then_inc(s["pT1_done"], 1)

            act.wait_ge(s["dist_ready"], 2)
            for p in range(PAIRS):
                ins = act.activation(decay[:, p, :], dist[:, :], ACT.Exp, scale=slope[:, p:p + 1])
            ins.then_inc(s["decay_exp"], 1)
            def w1_high(e):
                act.wait_ge(w1_in[e % NSLOT], 48 * (e // NSLOT + 1))
                if e >= 2:
                    act.wait_ge(s["h_mm"], NF * e)
                act.activation(w1x[e % 2].high, w1s[:, e % NSLOT, 0], ACT.Copy)
                act.activation(w1x[e % 2].both, w1s[:, e % NSLOT, 1], ACT.Copy).then_inc(s["w1_hi"], 1)

            act.wait_ge(s["zeros_made"], 2)
            k_out(0)
            v_out(0)
            exp1(0)
            N1 = NT * EA
            for n in range(N1 + 2):
                e, t = divmod(n, NT)
                if t == 0 and 0 < n < NT * EA:
                    v_out(e)
                    exp1(n)
                if t == NT - 1 and e < EA - 1:
                    k_out(e + 1)
                if n < NT * EA:
                    pT1_out(n)
                if t < NT - 1 and n + 1 < NT * EA:
                    exp1(n + 1)
                if t == 1 and e >= 1:
                    act.wait_ge(s["wo1_mm"], 2 * e - 1)
                    act.activation(fT[:, e - 1, 0, :], ps[:, 2, :], ACT.Copy).then_inc(s["fT_act"], 1)
                if n in (N1 - 3, N1 - 2):
                    act.wait_ge(s["v1_mm"], 2 * EA)
                    w1_high(n - (N1 - 3))
            for i in range(NT):
                act.wait_ge(s["gu_mm"], i + 1)
                act.activation(gsb[:, i, :], ps[:, 3 + i, 0:D], ACT.Silu).then_inc(s["silu_done"], 1)
            tokens_out(4, xs, 0)
            act.wait_ge(s["lg_sub"], 1)
            act.activation(lg, lg, ACT.Exp).then_inc(s["lg_exp"], 1)
            for e in range(EM):
                if e >= 2:
                    act.wait_ge(s["y_mm"], e - 1)
                hidden(hT[:, e % 2], R_MOE + NF * e, ACT.Gelu_apprx_tanh)
                if e + 2 < EM:
                    w1_high(e + 2)
            act.wait_ge(s["xT_mm"], 5)
            act.activation(xT[:, 0, :], ps[:, 0, :], ACT.Copy).then_inc(s["xT_act"], 1)
            act.activation(spare[:, :], neghalf[:, 0:1], ACT.Silu)
            act.wait_ge(s["zeros_made"], 3)
            for c, (r0, n) in enumerate(CH):
                act.wait_ge(s["q3_mm"], 2 * c + 1)
                for g in range(n // 32):
                    r = slice(32 * g, 32 * g + 32)
                    ins = act.activation((q3b if c else q3)[r, :, g, :],
                                         ps[r, 2 * c, :].rearrange("p (b i) -> p b i", b=B), ACT.Silu)
                ins.then_inc(s["q3_done"], 1)
                if c == 0:
                    act.wait_ge(s["q3_mm"], 2)
                    act.activation(ksb[:, 0, :], ps[:, 1, :], ACT.Silu).then_inc(s["k3_done"], 1)
                else:
                    for g in range(2):
                        ins = act.activation(ksb[32 * g:32 * g + 32, 1, :], ps[DB + 32 * g:DB + 32 * g + 32, 2, :],
                                             ACT.Silu)
                    ins.then_inc(s["k3_done"], 1)
            for j in range(2):
                act.wait_ge(s["v3_mm"], j + 1)
                for m in range(2):
                    for h in range(2):
                        rows = [(64 * m, 64 * h, 64)] if m == h else [(64 * m + o, 64 * h + o, 32) for o in (0, 32)]
                        for src, dst, n in rows:
                            ins = act.activation(
                                vbd3[dst:dst + n, 4 * j + m:4 * j + 4:2, :, h, :],
                                ps[src:src + n, 4 + j, 0:2 * D].rearrange(
                                    "p (t a h d) -> p t a h d", t=2, a=PAIRS, h=2)[:, :, :, h, :], ACT.Silu)
                ins.then_inc(s["v3_done"], 1)
            act.wait_ge(s["gate3_mm"], 1)
            act.activation(pairs_of(gate3), two(6), ACT.Sigmoid).then_inc(s["gate3_done"], 1)
            act.wait_ge(s["m0_in"], 64)
            act.wait_ge(s["y_half"], 2)
            weights_high(wm0x, m0w1)
            act.wait_ge(s["xT_mm"], 6)
            act.activation(xT[:, 0, :], ps[:, 6, :], ACT.Copy).then_inc(s["xT_act"], 1)
            tokens_out(7, xs, 0)
            act.wait_ge(s["cl_sub"], 1)
            act.activation(cls_l, cls_l, ACT.Exp).then_inc(s["cl_exp"], 1)
            hidden(hT[:, 0], R_M0, ACT.Gelu, range(3))
            for x in range(5):
                act.wait_ge(s["hc_add"], x + 1)
                act.activation(hcls[:, x], hcls[:, x], ACT.Gelu).then_inc(s["hc_done"], 1)
                if x < 3:
                    hidden(hT[:, 0], R_M0, ACT.Gelu, range(3 + x, 4 + x))

        @block.vector
        def _(dve):
            steps = [0]

            def link(ins):
                steps[0] += 1
                ins.then_inc(s["dve_step"], 1)
                dve.wait_ge(s["dve_step"], steps[0])

            for c in range(C):
                dve.wait_ge(x_in[c], 16)
                dve.tensor_copy(xq[:, c].rearrange("p w (r q) -> p r w q", r=8),
                                xr[:, c, :].rearrange("p (r w q) -> p r w q", r=8, w=GRID)).then_inc(s["xq_done"], 1)
            dve.wait_ge(s["consts_made"], 1)
            link(dve.tensor_scalar(par_i[:, :], par_i[:, :], 4, 1, ALU.logical_shift_right, ALU.bitwise_and))
            link(dve.tensor_copy(parity[:, 1:2], par_i[:, :]))
            link(dve.tensor_scalar(parity[:, 0:1], parity[:, 1:2], -1.0, 1.0, ALU.mult, ALU.add))
            dve.tensor_scalar(dist[:, :], dist[:, :], 0.0, None, ALU.max).then_inc(s["dist_ready"], 1)

            for j in range(3):
                dve.wait_ge(s["xr_T"], 2 * j + 1)
                dve.tensor_copy(patch_out(2 * j), patch_in(2 * j)).then_inc(s["xpT_dve"], 1)

            def weights_low(w, raw_w, n):
                k = w.high.shape[1]
                dve.wait_ge(s["wx_hiA"], n)
                dve.tensor_tensor(w.low, raw_w[:, 0, 0:k], w.high.bitcast(F32), ALU.subtract)
                dve.wait_ge(s["wx_hi"], n)
                dve.tensor_tensor(w.both[DB:P], raw_w[DB:P, 1, 0:k], w.both[DB:P].bitcast(F32),
                                  ALU.subtract).then_inc(s["wx_lo"], 1)

            def tokens_low(x, n):
                dve.wait_ge(s["xs_hiA"], n)
                dve.wait_ge(s["xT_dve"], TURN_OF[n])
                dve.tensor_tensor(x.low, xT[:, 0, :], x.high.bitcast(F32), ALU.subtract)
                dve.wait_ge(s["xs_hi"], n)
                dve.tensor_tensor(x.lowB, xT[0:DB, 1, :], x.both[0:DB].bitcast(F32),
                                  ALU.subtract).then_inc(s["xs_lo"], 1)

            weights_low(wqkx, wqkv, 1)
            lns = [0]

            def moments(src, g, rows=P, n=2):
                tiles = range(2 * g, 2 * g + n)
                for i in tiles:
                    ins = dve.bn_stats(bn[0:rows, i, :], src(i))
                link(ins)
                for i in tiles:
                    ins = dve.bn_aggr(mv[0:rows, i, :], bn[0:rows, i, :])
                ins.then_inc(s["var_ready"], 1)

            def deviation():
                lns[0] += 1
                dve.wait_ge(s["rstd_ready"], lns[0])

            def centre(src, dst, g, rows=P, n=2, done="ln_done"):
                deviation()
                for i in range(2 * g, 2 * g + n):
                    dve.tensor_scalar(dst(i), src(i), mv[0:rows, i, 0:1], rstd[0:rows, i:i + 1],
                                      ALU.subtract, ALU.mult).then_inc(s[done], 1)

            def of(x):
                return lambda i: x[:, i, :]

            dve.wait_ge(s["bpatch_in"], 16)
            for j in range(2):
                dve.wait_ge(s["patch_mm"], j + 1)
                ins = dve.tensor_tensor(tok[:, 2 * j:2 * j + 2, :],
                                        ps[:, 6 + j, 0:2 * D].rearrange("p (a b) -> p a b", a=2),
                                        bc["b_patch"][:, :].unsqueeze(1).to_broadcast([P, 2, D]), ALU.add)
                link(ins)
                moments(of(tok), j)
            dve.wait_ge(s["colc_mm"], 1)
            dve.tensor_copy(colc[:, 0:NROWS], ps[:, 1, 0:NROWS]).then_inc(s["colc_done"], 1)
            dve.wait_ge(s["bcast_in"], 6 * 16)
            for h in range(2):
                r = slice(64 * h, 64 * h + 64)
                ins = dve.tensor_copy(slope[r, :], slopes[r, :].rearrange("p (a h) -> p h a", h=2)[:, h])
            ins.then_inc(s["dist_ready"], 1)
            for g in range(2):
                centre(of(tok), of(xn), g)

            def turned_weights(e):
                dve.wait_ge(s["wt_mm"], e + 1)
                dve.tensor_copy(wT[e][0:DB, 1, 0:2 * D], ps[0:DB, 2, 0:2 * D])
                dve.tensor_copy(woT[e][0:96, :, :], ps[0:96, 3, 0:2 * D].rearrange("p (a b) -> p a b", a=2))
                dve.tensor_copy(wguT[e][0:DB, 1, :], ps[0:DB, 5, 0:2 * D]).then_inc(s["wt_dve"], 1)

            dve.wait_ge(s["xT_mm"], 1)
            dve.tensor_scalar(xT[0:DB, 1, :], ps[0:DB, 7, :], col(R_LNB)[0:DB], col(R_LNB + 1)[0:DB],
                              ALU.mult, ALU.add).then_inc(s["xT_dve"], 1)
            tokens_low(xs0, 1)

            def k0_out(hp):
                dve.wait_ge(s["k0_mm"], hp + 1)
                if hp >= 2:
                    dve.wait_ge(s["s0_mm"], hp - 1)
                dve.tensor_copy(kT0[:, hp % 2, :], ps[:, 1, :]).then_inc(s["k0_done"], 1)

            def softmax0_in(hp):
                k = hp % 2
                dve.wait_ge(s["s0_mm"], hp + 1)
                if hp >= 2:
                    dve.wait_ge(s["t0_mm"], hp - 1)
                sc = ps[:, 3 + k, :].rearrange("p (b j) -> p b j", b=B)
                link(dve.tensor_reduce(mx0[:, 0, :], sc, AX.X, ALU.max))
                dve.tensor_tensor(p0[:, k], sc, mx0[:, 0, :].unsqueeze(2).to_broadcast([P, B, S]),
                                  ALU.subtract).then_inc(s["sub0"], 1)

            def softmax0_out(hp):
                k = hp % 2
                dve.wait_ge(s["exp0"], hp + 1)
                link(dve.tensor_reduce(mx0[:, 1, :], p0[:, k], AX.X, ALU.add))
                link(dve.reciprocal(mx0[:, 1, :], mx0[:, 1, :]))
                dve.tensor_tensor(p0[:, k], p0[:, k], mx0[:, 1, :].unsqueeze(2).to_broadcast([P, B, S]),
                                  ALU.mult).then_inc(s["p0_done"], 1)

            def out0(hp):
                dve.wait_ge(s["pv0_mm"], hp + 1)
                dve.tensor_copy(oT0[:, hp, :].rearrange("p (t m i) -> p m t i", t=NT, m=2),
                                ps[:, 6:8, 0:NT * S].rearrange("p m (t i) -> p m t i", t=NT)).then_inc(s["oT0_done"], 1)

            k0_out(0)
            softmax0_in(0)
            softmax0_out(0)
            for hp in range(PAIRS):
                if hp + 1 < PAIRS:
                    k0_out(hp + 1)
                    softmax0_in(hp + 1)
                out0(hp)
                if hp + 1 < PAIRS:
                    softmax0_out(hp + 1)

            toks = [0]

            def residual(bank, g):
                toks[0] += 1
                dve.wait_ge(s["tok_mm"], toks[0])
                dve.tensor_tensor(tok2[:, g], tok2[:, g], ps[:, bank + g, 0:2 * D], ALU.add).then_inc(s["tok_done"], 1)
                dve.wait_ge(s["tok_done"], toks[0])

            weights_low(wffx, wff1, 2)
            dve.wait_ge(s["bias_added"], 1)
            for g in range(2):
                residual(6, g)
                moments(of(tok), g)
                centre(of(tok), of(xn), g)
                turned_weights(g)
            dve.wait_ge(s["xT_mm"], 2)
            dve.tensor_scalar(xT[0:DB, 1, :], ps[0:DB, 7, :], col(R_LNB + 2)[0:DB], col(R_LNB + 3)[0:DB],
                              ALU.mult, ALU.add).then_inc(s["xT_dve"], 1)
            tokens_low(xs0, 2)
            dve.wait_ge(s["bias_added"], 2)
            residual(6, 0)
            turned_weights(2)
            turned_weights(3)
            residual(6, 1)
            dve.wait_ge(s["xT_mm"], 3)
            dve.tensor_copy(xT[0:DB, 1, :], ps[0:DB, 7, :]).then_inc(s["xT_dve"], 1)
            def q_out(e):
                for c, (r0, n) in enumerate(CH):
                    dve.wait_ge(s["qk1_mm"], 3 * e + 2 * c + 1)
                    if c == 0 and e >= 1:
                        dve.wait_ge(s["s1_mm"], NT * e)
                    for h in range(2):
                        ins = dve.tensor_scalar(qm[0:n, c, :, h, :],
                                                ps[0:n, 3 + 2 * c, :].rearrange("p (b i) -> p b i", b=B),
                                                parity[0:n, h:h + 1], None, ALU.mult)
                    ins.then_inc(s["qk1_dve"], 1)

            def softmax1_in(n):
                k = n % 2
                dve.wait_ge(s["s1_mm"], n + 1)
                if n >= 2:
                    dve.wait_ge(s["t1_mm"], n - 1)
                pk = p1[:, k].rearrange("p a m j -> p (a m) j")
                for m in range(2):
                    ins = dve.scalar_tensor_tensor(
                        p1[:, k, :, m, :], ps[:, 3 + 2 * k + m, 0:PAIRS * S].rearrange("p (a j) -> p a j", a=PAIRS),
                        DH ** -0.5, causal[:, :].unsqueeze(1).to_broadcast([P, PAIRS, S]), ALU.mult, ALU.add)
                ins.then_inc(s["s1_read"], 1)
                dve.wait_ge(s["s1_read"], n + 1)
                link(dve.tensor_reduce(mx1[:, k, :], pk, AX.X, ALU.max))
                dve.tensor_tensor(pk, pk, mx1[:, k, :].unsqueeze(2).to_broadcast([P, 2 * PAIRS, S]),
                                  ALU.subtract).then_inc(s["sub1"], 1)

            def out1(n):
                k = n % 2
                dve.wait_ge(s["pv1_mm"], n + 1)
                if n >= 2:
                    dve.wait_ge(s["ot1_mm"], n - 1)
                o = ps[:, 7, 0:PAIRS * 2 * (2 * DH + 1)].rearrange("p (a m d) -> p m a d", a=PAIRS, m=2)
                rk = rc1[:, k, :].rearrange("p (m a) -> p m a", m=2)
                link(dve.reciprocal(rk, o[:, :, :, 2 * DH]))
                for h in range(2):
                    r = slice(64 * h, 64 * h + 64)
                    ins = dve.tensor_tensor(o1[r, k], o[r, :, :, h * DH:(h + 1) * DH],
                                            rk[r].unsqueeze(3).to_broadcast([64, 2, PAIRS, DH]), ALU.mult)
                ins.then_inc(s["o1_done"], 1)

            def oT_out(q):
                dve.wait_ge(s["ot1_mm"], 2 * q + 2)
                if q % 2 == 0 and q >= 2:
                    dve.wait_ge(s["wo1_mm"], q)
                at = 256 * (q % 2)
                dve.tensor_copy(
                    oT1[0:96, :, at:at + 256].rearrange("p h (m i) -> p h m i", m=4),
                    ps[0:96, 2, :].rearrange("p (m h i) -> p h m i", m=4, h=2)).then_inc(s["ot1_done"], 1)

            dve.wait_ge(s["zeros_made"], 2)
            def w1_low(e):
                dve.wait_ge(s["w1_hi"], e + 1)
                w = w1x[e % 2]
                dve.tensor_tensor(w.low, w1s[:, e % NSLOT, 0], w.high.bitcast(F32), ALU.subtract)
                dve.tensor_tensor(w.both[DB:P], w1s[DB:P, e % NSLOT, 1], w.both[DB:P].bitcast(F32),
                                  ALU.subtract).then_inc(s["w1_lo"], 1)

            q_out(0)
            softmax1_in(0)
            N1 = EA * NT
            for n in range(N1 + 3):
                e, t = divmod(n, NT)
                if t == 0 and 0 < n < N1:
                    softmax1_in(n)
                    out1(n - 1)
                if t < NT - 1 and n + 1 < N1:
                    softmax1_in(n + 1)
                elif t == NT - 1 and e < EA - 1:
                    q_out(e + 1)
                if 1 <= n <= N1 and (t > 0 or n == N1):
                    out1(n - 1)
                if t == 0 and e >= 1:
                    oT_out(2 * e - 1)
                elif t == 2 and e >= 1:
                    if e == EA:
                        w1_low(0)
                        w1_low(1)
                    dve.wait_ge(s["wo1_mm"], 2 * e)
                    dve.tensor_copy(fT[0:DB, e - 1, 1, :], ps[0:DB, 2, :]).then_inc(s["fT_dve"], 1)
                elif t == 3 and n < N1:
                    oT_out(2 * e)
            def gated(g):
                for i in (2 * g, 2 * g + 1):
                    dve.wait_ge(s["silu_done"], i + 1)
                    ins = dve.tensor_tensor(gsb[:, i, :], gsb[:, i, :], ps[:, 3 + i, D:2 * D], ALU.mult)
                link(ins)
                link(dve.tensor_tensor(tok[:, 2 * g:2 * g + 2, :], tok[:, 2 * g:2 * g + 2, :],
                                       gsb[:, 2 * g:2 * g + 2, :], ALU.add))

            gated(0)
            moments(of(tok), 0)
            gated(1)
            centre(of(tok), of(xn), 0)
            moments(of(tok), 1)
            centre(of(tok), of(xn), 1)
            dve.wait_ge(s["xT_mm"], 4)
            dve.tensor_copy(xT[0:DB, 1, :], ps[0:DB, 1, :]).then_inc(s["xT_dve"], 1)

            tokens_low(xs, 3)

            dve.wait_ge(s["small_in"], 16 * 13)
            dve.wait_ge(s["v_mm"], 1)
            link(dve.tensor_scalar(vrow, ps[0:1, 4, :], vb[0:1], 3.0, ALU.add, ALU.min))
            link(dve.tensor_scalar(vrow, vrow, -3.0, -2.0, ALU.max, ALU.add))
            vr = vrow.rearrange("o (b n) -> o b n", n=S)
            dve.tensor_copy(vrev.rearrange("o (b n) -> o b n", n=S), vr[:, :, ::-1]).then_inc(s["chain_in"], 1)
            dve.wait_ge(s["lg_mm"], 1)
            gb = gateb[:, :].unsqueeze(1).to_broadcast([P, NT, EM])
            link(dve.tensor_tensor(lg, ps[:, 5, 0:NT * EM].rearrange("p (a b) -> p a b", a=NT), gb, ALU.add))
            link(dve.tensor_reduce(lmx, lg, AX.X, ALU.max))
            dve.tensor_tensor(lg, lg, lmx.unsqueeze(2).to_broadcast([P, NT, EM]),
                              ALU.subtract).then_inc(s["lg_sub"], 1)
            dve.wait_ge(s["lg_exp"], 1)
            link(dve.tensor_reduce(lmx, lg, AX.X, ALU.add))
            link(dve.reciprocal(lmx, lmx))
            link(dve.tensor_tensor(pr, lg, lmx.unsqueeze(2).to_broadcast([P, NT, EM]), ALU.mult))
            for i in range(NT):
                mine = pr[:, i, :].unsqueeze(2).to_broadcast([P, EM, EM])
                other = pr[:, i, :].unsqueeze(1).to_broadcast([P, EM, EM])
                dve.tensor_tensor(cmp[:, i], other, mine, ALU.is_gt)
                ins = dve.tensor_tensor(ceq[:, i], other, mine, ALU.is_equal)
            link(ins)
            for i in range(NT):
                ins = dve.tensor_tensor(ceq[:, i], ceq[:, i], lower, ALU.mult)
            link(ins)
            link(dve.tensor_tensor(cmp, cmp, ceq, ALU.add))
            link(dve.tensor_reduce(comb, cmp, AX.X, ALU.add))
            link(dve.scalar_tensor_tensor(comb, comb, 1.5, pr, ALU.is_lt, ALU.mult))
            link(dve.tensor_reduce(lmx, comb, AX.X, ALU.add))
            link(dve.reciprocal(lmx, lmx))
            dve.tensor_tensor(comb, comb, lmx.unsqueeze(2).to_broadcast([P, NT, EM]),
                              ALU.mult).then_inc(s["comb_done"], 1)
            dve.wait_ge(s["comb_done"], 1)
            link(dve.tensor_tensor(ow3[0:3], ow3[0:3], bk3[0:3], ALU.mult))
            dve.wait_ge(s["rowmv_in"], 32)
            dve.tensor_tensor(chB[:, :, 0], chA, alt, ALU.mult)
            link(dve.memset(chB[:, :, 1], -1.0))
            link(dve.tensor_copy(chS[:, 0, :], chB[:, 0, :]))

            def chain_step(n):
                link(dve.tensor_tensor_reduce(out=chr_[:, 0:2], in0=chS[:, n - 1, :], in1=chS[:, n - 1, :], scale=1.0,
                                              scalar=0.0, op0=ALU.mult, op1=ALU.add, accum_out=chr_[:, 2:3]))
                link(dve.reciprocal(chr_[:, 3:4], chr_[:, 2:3]))
                link(dve.scalar_tensor_tensor(chS[:, n, :], chS[:, n - 1, :], chr_[:, 3:4], chB[:, n, :],
                                              ALU.mult, ALU.add))

            def chains_end():
                dve.tensor_tensor(chS[:, :, 0], chS[:, :, 0], alt, ALU.mult).then_inc(s["chain_in"], 1)

            def features():
                dve.wait_ge(s["chE_in"], 16)
                dve.tensor_tensor(chG[:, 0, :], chS[0:8, :, 0], chE[:, ::-1, 0], ALU.add)
                link(dve.tensor_tensor(chG[:, 1, :], chS[0:8, :, 1], chE[:, ::-1, 1], ALU.add))
                dve.tensor_tensor(chG[:, 0, :], chG[:, 0, :], chA[0:8], ALU.subtract)
                link(dve.tensor_scalar(chG[:, 1, :], chG[:, 1, :], 1.0, None, ALU.add))
                link(dve.tensor_tensor(chQ, chG, chG, ALU.mult))
                link(dve.tensor_tensor(chQ[:, 0, :], chQ[:, 0, :], chQ[:, 1, :], ALU.add))
                link(dve.reciprocal(chQ[:, 1, :], chQ[:, 0, :]))
                dve.tensor_tensor(chF[:, 0, :], chG[:, 0, :], chQ[:, 1, :], ALU.mult)
                link(dve.scalar_tensor_tensor(chF[:, 1, :], chG[:, 1, :], -1.0, chQ[:, 1, :], ALU.mult, ALU.mult))
                dve.tensor_scalar(chF, chF, 10.0, -10.0, ALU.min, ALU.max).then_inc(s["feat_out"], 1)

            PER = 11
            FIRST = S - PER * (EM - 3)
            for n in range(1, FIRST):
                chain_step(n)
            def weighted(dst, e, i):
                return dve.scalar_tensor_tensor(dst[:, i, :], two_t(4 + 2 * (e % 2), i), comb[:, i, e:e + 1],
                                                xn[:, i, :], ALU.mult, ALU.add)

            for e in range(EM):
                if e == EM - 2:
                    dve.wait_ge(s["extra_mm"], 1)
                    dve.tensor_tensor(xn2, xn2, two(6), ALU.add).then_inc(s["extra_done"], 1)
                    dve.wait_ge(s["extra_done"], 1)
                if e + 2 < EM - 1:
                    w1_low(e + 2)
                if e == EM - 1:
                    break
                dve.wait_ge(s["y_mm"], e + 1)
                for i in range(NT):
                    ins = weighted(xn, e, i)
                ins.then_inc(s["y_done"], 1)
                dve.wait_ge(s["y_done"], e + 1)
                if e == 0:
                    dve.wait_ge(s["combT_mm"], 1)
                    dve.tensor_copy(combT[0:EM], ps[0:EM, 6, :]).then_inc(s["combT_done"], 1)
                for n in range(FIRST + PER * e, min(S, FIRST + PER * (e + 1))):
                    chain_step(n)
                if e == EM - 4:
                    chains_end()
                    w1_low(EM - 1)
                    features()
            for g in range(2):
                dve.wait_ge(s["y_half"], g + 1)
                weighted(tok, EM - 1, 2 * g)
                link(weighted(tok, EM - 1, 2 * g + 1))
                moments(of(tok), g)
                centre(of(tok), of(xn), g)
            dve.wait_ge(s["xT_mm"], 5)
            dve.tensor_copy(xT[0:DB, 1, :], ps[0:DB, 1, :]).then_inc(s["xT_dve"], 1)

            for c, (r0, n) in enumerate(CH):
                dve.wait_ge(s["k3_done"], c + 1)
                for h in range(2):
                    ins = dve.tensor_scalar(km3[0:n, c, :, h, :], ksb[0:n, c, :].rearrange("p (b i) -> p b i", b=B),
                                            parity[0:n, h:h + 1], None, ALU.mult)
                ins.then_inc(s["km_done"], 1)
            dve.wait_ge(s["gate1_mm"], 1)
            dve.tensor_copy(g1T, ps[0:16, 7, :]).then_inc(s["gate1_done"], 1)
            dve.wait_ge(s["decay_done"], 1)
            for t in range(NT):
                dve.wait_ge(s["e3_mm"], t + 1)
                ins = dve.tensor_tensor(
                    E3[t // 2][:, t % 2].rearrange("p a m i -> p m a i"),
                    ps[:, 2 * (t % 2):2 * (t % 2) + 2, 0:PAIRS * S].rearrange("p m (a i) -> p m a i", a=PAIRS),
                    decay[:, :, :].unsqueeze(1).to_broadcast([P, 2, PAIRS, S]), ALU.mult)
                ins.then_inc(s["e3_done"], 1)
                if t == 1:
                    weights_low(wm0x, m0w1, 3)
            dve.wait_ge(s["gate3_done"], 1)
            for g in range(2):
                dve.wait_ge(s["pv3_mm"], g + 1)
                og = pairs_of(gate3)[:, g]
                dve.tensor_tensor(og, og, ps[:, 4 + g, 0:2 * D], ALU.mult).then_inc(s["og_done"], 1)
            dve.wait_ge(s["xT_mm"], 6)
            dve.tensor_copy(xT[0:DB, 1, :], ps[0:DB, 7, :]).then_inc(s["xT_dve"], 1)
            def branch(i):
                return two_t(0, i)

            def scaled(g):
                for i in (2 * g, 2 * g + 1):
                    ins = dve.scalar_tensor_tensor(tok[:, i, :], branch(i), mv[:, i, 0:1], bc["ln_w"][:, :],
                                                   ALU.subtract, ALU.mult)
                link(ins)

            def joined(g):
                deviation()
                for i in (2 * g, 2 * g + 1):
                    ins = dve.scalar_tensor_tensor(tok[:, i, :], tok[:, i, :], rstd[:, i:i + 1], xn[:, i, :],
                                                   ALU.mult, ALU.add)
                link(ins)

            for g in range(2):
                dve.wait_ge(s["tok_mm"], 5 + g)
                moments(branch, g)
                dve.wait_ge(s["var_ready"], lns[0] + g + 1)
                scaled(g)
                if g == 0:
                    dve.wait_ge(s["bias_added"], 3)
            for g in range(2):
                joined(g)
                moments(of(tok), g)
            for g in range(2):
                centre(of(tok), of(xn), g)
            dve.wait_ge(s["xT_mm"], 7)
            dve.tensor_copy(xT[0:DB, 1, :], ps[0:DB, 1, :]).then_inc(s["xT_dve"], 1)
            dve.wait_ge(s["xT_act"], 7)
            dve.wait_ge(s["xT_dve"], 7)
            for c, (r0, n) in enumerate(CH):
                ins = dve.tensor_copy(xcls[0:n, c, :].rearrange("p (i b) -> p i b", i=NCLS),
                                      xT[0:n, c, :].rearrange("p (b n) -> p n b", n=S)[:, 0:NCLS, :])
            ins.then_inc(s["xcls_done"], 1)

            dve.wait_ge(s["xcls_done"], 1)
            dve.memset(ones, 1.0)
            for c, (r0, n) in enumerate(CH):
                for q in range(2):
                    ins = dve.tensor_tensor(xg[0:n, c, q, :].rearrange("p (i b) -> p i b", i=NCLS),
                                            xcls[0:n, c, :].rearrange("p (i b) -> p i b", i=NCLS),
                                            gwc[0:n, c, :, q:q + 1].to_broadcast([n, NCLS, B]), ALU.mult)
            ins.then_inc(s["xg_done"], 1)
            tokens_low(xs, 4)
            dve.wait_ge(s["cl_mm"], 1)
            cl = ps[:, 4, 0:2 * NC].rearrange("p (q n) -> p q n", q=2)
            link(dve.tensor_copy(cls_l, cl))
            link(dve.tensor_tensor(cls_s, cls_l[:, 0, :], cls_l[:, 1, :], ALU.max))
            dve.tensor_tensor(cls_l, cls_l, cls_s.unsqueeze(1).to_broadcast([P, 2, NC]),
                              ALU.subtract).then_inc(s["cl_sub"], 1)
            dve.wait_ge(s["cl_exp"], 1)
            link(dve.tensor_tensor(cls_s, cls_l[:, 0, :], cls_l[:, 1, :], ALU.add))
            link(dve.reciprocal(cls_s, cls_s))
            link(dve.tensor_tensor(cls_l, cls_l, cls_s.unsqueeze(1).to_broadcast([P, 2, NC]), ALU.mult))
            dve.tensor_tensor(cls_m[:, 0, :], cls_l[:, 0, :], cls_l[:, 1, :], ALU.is_gt)
            link(dve.tensor_tensor(cls_m[:, 1, :], cls_l[:, 1, :], cls_l[:, 0, :], ALU.is_gt))
            for i in range(NCLS):
                n = slice(i * B, (i + 1) * B)
                dve.tensor_copy(mcls[:, 3 + i % 2, n], cls_m[:, 0, n])
                ins = dve.tensor_copy(mcls[:, i // 2, n], cls_m[:, 1, n])
            ins.then_inc(s["mcls_done"], 1)
            for x in range(5):
                dve.wait_ge(s["hc_mm"], x + 1)
                src = ps[:, 6 + x % 2, 0:NF * NC].rearrange("p (f n) -> p f n", f=NF)
                bias = colc[:, R_A1 + NF * x:R_A1 + NF * (x + 1)].unsqueeze(2).to_broadcast([P, NF, NC])
                dve.tensor_tensor(hcls[:, x], src, bias, ALU.add).then_inc(s["hc_add"], 1)
            dve.wait_ge(s["bcast_in"], 6 * 16)
            link(dve.tensor_tensor(tok[:, :, :], xn[:, :, :],
                                   bc["m0_b2"][:, :].unsqueeze(1).to_broadcast([P, NT, D]), ALU.add))
            dve.wait_ge(s["zeros_made"], 4)
            dve.wait_ge(s["mcls_done"], 1)
            for x in range(5):
                dve.wait_ge(s["hc_done"], x + 1)
            for i in range(NCLS):
                n = slice(i * B, (i + 1) * B)
                for first, then, g in ((i // 2, 3 + i % 2, 0), (3 + i % 2, i // 2, 1)):
                    ins = dve.tensor_tensor(hmix[:, then, :, n], hcls[:, first, :, n],
                                            cls_m[:, g, n].unsqueeze(1).to_broadcast([P, NF, B]), ALU.mult)
            ins.then_inc(s["hmix_done"], 1)
            for g in range(2):
                dve.wait_ge(s["y_half"], 2 + g + 1)
                link(dve.tensor_tensor(tok2[:, g], tok2[:, g], ps[:, 4 + g, 0:2 * D], ALU.add))
                moments(of(tok), g)
                centre(of(tok), of(xn), g, done="fin_ready")
            dve.wait_ge(s["clsx_mm"], 1)
            link(dve.tensor_copy(clsx[0:NC], ps[0:NC, 2, 0:D]))
            dve.wait_ge(s["cls_mm"], 1)
            link(dve.tensor_tensor(clsx[0:NC], clsx[0:NC], ps[0:NC, 3, 0:D], ALU.add))
            moments(lambda i: clsx[0:NC], 0, NC, 1)
            centre(lambda i: clsx[0:NC], lambda i: clsx[0:NC], 0, NC, 1, done="fin_ready")

        @block.tensor
        def _(pe):
            def mm(o, l, r, start, stop):
                return pe.matmul(o, l, r, start=start, stop=stop)

            def tr(o, i):
                k = i.shape[0]
                return pe.transpose(o, i, ident[0:k, 0:k])

            pe.wait_ge(s["ident_made"], 1)
            for j in range(2 * C):
                c, half = divmod(j, 2)
                if half == 0:
                    pe.wait_ge(s["xq_done"], c + 1)
                for w in range(4):
                    ins = tr(ps[:, j, w * P:(w + 1) * P], xq[:, c, 4 * half + w, :])
                ins.then_inc(s["xr_T"], 1)
            pe.wait_ge(s["wpatch_in"], 16)
            pe.wait_ge(s["xpT_act"], 3)
            pe.wait_ge(s["xpT_dve"], 3)
            for i in range(NT):
                for k in range(2 * C):
                    ins = mm(two_t(6, i), xpT[:, k, i * P:(i + 1) * P], wpatch[:, k % 2, k // 2, :],
                             k == 0, k == 2 * C - 1)
                if i % 2:
                    ins.then_inc(s["patch_mm"], 1)
            pe.wait_ge(s["rows_in"], 16 * 16)
            tr(ps[:, 1, 0:NROWS], rowc[0:NROWS, :]).then_inc(s["colc_mm"], 1)

            def turn_weights(e):
                pe.wait_ge(s["raw_in"], 16 * 8)
                pe.wait_ge(s["rawg_in"], 16 * 4)
                pe.wait_ge(s["rawo_done"], 1)
                if e >= 1:
                    pe.wait_ge(s["wt_act"], e)
                    pe.wait_ge(s["wt_dve"], e)
                for oc, (o0, on) in enumerate(CH):
                    for m in range(3):
                        for ic, (i0, n) in enumerate(CH):
                            bank, at = ((2 if ic else 0), QK[2 * oc + m][3]) if m < 2 else (1, ic * D + o0)
                            tr(ps[0:n, bank, at:at + on], raw[0:on, oc, e, m, i0:i0 + n])
                    for h in range(2):
                        tr(ps[0:96, 3, h * D + o0:h * D + o0 + on], rawo[0:on, oc, e, h, :])
                    for m in range(2):
                        for ic, (i0, n) in enumerate(CH):
                            ins = tr(ps[0:n, 4 + ic, m * D + o0:m * D + o0 + on],
                                     rawg[0:on, oc, m, e * D + i0:e * D + i0 + n])
                ins.then_inc(s["wt_mm"], 1)

            def keep_busy(n, bank):
                for _ in range(n):
                    pe.matmul(ps[:, bank, 0:P], ident[:, :], ident[:, :], start=True, stop=True)

            def turn_tokens(x, n, normed=None, bank=6, twice=False, halves=None):
                for i in range(NT):
                    if halves:
                        pe.wait_ge(s[halves], i // 2 + 1)
                    if normed:
                        pe.wait_ge(s["ln_done"], NT * (normed - 1) + i + 1)
                    for c, (r0, rn) in enumerate(CH):
                        ins = tr(ps[0:rn, bank + c, i * P:(i + 1) * P], x[:, i, r0:r0 + rn])
                    if twice:
                        ins = mm(ps[DB:P, bank + 1, i * P:(i + 1) * P], x[:, i, P:D], ident[:, :], True, True)
                ins.then_inc(s["xT_mm"], 1)

            def xT_ready(n):
                pe.wait_ge(s["xT_act"], n)
                pe.wait_ge(s["xT_dve"], n)

            pe.wait_ge(s["colc_done"], 1)
            keep_busy(10, 5)
            turn_tokens(xn, 1, 1, twice=True)
            xT_ready(1)
            pe.wait_ge(s["wqkv_in"], 16)
            pe.wait_ge(s["wqkvB_in"], 32)

            def split_product(o, w, n, x, turn=0):
                if turn:
                    pe.wait_ge(s["xs_hi"], turn)
                mm(o, w.high[:, n], x.high, True, False)
                mm(o, w.low[:, n], x.high, False, False)
                mm(o, w.both[:, n], x.both, False, False)
                if turn:
                    pe.wait_ge(s["xs_lo"], turn)
                mm(o, w.high[:, n], x.low, False, False)
                return mm(o, w.both[0:DB, n], x.lowB, False, True)

            def values_in0(hp):
                if hp >= 1:
                    pe.wait_ge(s["v0_done"], hp)
                at = 2 * H * DH0 + hp * P
                for i in range(NT):
                    for c, (r0, n) in enumerate(CH):
                        ins = mm(ps[:, 2, i * P:(i + 1) * P], xT[0:n, c, i * P:(i + 1) * P], wqkv[0:n, c, at:at + P],
                                 c == 0, c == 1)
                ins.then_inc(s["v0_mm"], 1)

            def project0(hp):
                for m, (made, read) in enumerate((("q0_mm", "q0_done"), ("k0_mm", "k0_done"))):
                    if hp >= 1:
                        pe.wait_ge(s[read], hp)
                    at = m * H * DH0 + hp * P
                    split_product(ps[:, m, :], wqkx, slice(at, at + P), xs0,
                                  turn=int(hp == 0 and m == 0)).then_inc(s[made], 1)

            def scores0(hp):
                k = hp % 2
                pe.wait_ge(s["q0_done"], hp + 1)
                pe.wait_ge(s["k0_done"], hp + 1)
                if hp >= 2:
                    pe.wait_ge(s["sub0"], hp - 1)
                for b in range(B):
                    ins = mm(ps[:, 3 + k, b * S:(b + 1) * S], qbd[:, k, b].rearrange("p h i -> p (h i)"),
                             kT0[:, k, b * S:(b + 1) * S], True, True)
                ins.then_inc(s["s0_mm"], 1)

            def turn0(hp):
                k = hp % 2
                pe.wait_ge(s["p0_done"], hp + 1)
                if hp >= 1:
                    pe.wait_ge(s["pT0_done"], hp)
                for i in range(NT):
                    ins = tr(ps[:, 5, i * P:(i + 1) * P], p0[:, k, 2 * i:2 * i + 2, :].rearrange("p b j -> p (b j)"))
                ins.then_inc(s["t0_mm"], 1)

            def values0(hp):
                k = hp % 2
                pe.wait_ge(s["pT0_done"], hp + 1)
                pe.wait_ge(s["v0_done"], hp + 1)
                if hp >= 1:
                    pe.wait_ge(s["oT0_done"], hp)
                for b in range(B):
                    r = slice(64 * (b % 2), 64 * (b % 2) + 64)
                    for h in range(2):
                        ins = mm(ps[64 * h:64 * h + 64, 6 + b % 2, b // 2 * S:(b // 2 + 1) * S],
                                 v0[r, k, b // 2, 64 * h:64 * h + 64],
                                 pT0[r, k, b // 2, 64 * h:64 * h + 64], True, True)
                ins.then_inc(s["pv0_mm"], 1)

            values_in0(0)
            pe.wait_ge(s["wx_lo"], 1)
            project0(0)
            scores0(0)
            for hp in range(PAIRS):
                if hp + 1 < PAIRS:
                    project0(hp + 1)
                    values_in0(hp + 1)
                turn0(hp)
                if hp + 1 < PAIRS:
                    scores0(hp + 1)
                values0(hp)
            pe.wait_ge(s["oT0_done"], PAIRS)
            pe.wait_ge(s["wout_in"], 16)
            for i in range(NT):
                for k in range(PAIRS):
                    ins = mm(two_t(6, i), oT0[:, k, i * P:(i + 1) * P], wout[:, k, :], k == 0, k == PAIRS - 1)
                if i % 2:
                    ins.then_inc(s["tok_mm"], 1)
                if i == 1:
                    turn_weights(0)
            turn_weights(1)
            pe.wait_ge(s["tok_done"], 2)
            turn_tokens(xn, 2, 2, twice=True)
            xT_ready(2)
            pe.wait_ge(s["wt_act"], 2)
            pe.wait_ge(s["wt_dve"], 2)

            jobs = [0]

            def up(w, x, tiles=range(NF), turn=0):
                for f in tiles:
                    if jobs[0] >= 4:
                        pe.wait_ge(s["h_act"], jobs[0] - 3)
                    split_product(ps[:, jobs[0] % 4, :], w, slice(f * P, (f + 1) * P), x,
                                  turn if f == 0 else 0).then_inc(s["h_mm"], 1)
                    jobs[0] += 1

            def down(h, w, bank, halves=False):
                for i in range(NT):
                    for f in range(NF):
                        ins = mm(two_t(bank, i), h[:, f, i * P:(i + 1) * P], w[:, f, :], f == 0, f == NF - 1)
                    if halves and i % 2:
                        ins.then_inc(s["y_half"], 1)
                if not halves:
                    ins.then_inc(s["y_mm"], 1)

            pe.wait_ge(s["ff_in"], 64)
            pe.wait_ge(s["wx_lo"], 2)
            up(wffx, xs0, turn=2)
            pe.wait_ge(s["h_act"], jobs[0])
            for i in range(NT):
                for f in range(NF):
                    ins = mm(two_t(6, i), ffh[:, f, i * P:(i + 1) * P], wff2[:, f, :], f == 0, f == NF - 1)
                if i % 2:
                    ins.then_inc(s["tok_mm"], 1)
                if i in (1, 2):
                    turn_weights(i + 1)
            pe.wait_ge(s["tok_done"], 4)
            turn_tokens(tok, 3)
            xT_ready(3)
            pe.wait_ge(s["wt_act"], 4)
            pe.wait_ge(s["wt_dve"], 4)
            pe.nop().then_inc(s["mixer_left"], 1)

            def project1(e):
                for x in range(3):
                    if x == 2 and e >= 1:
                        pe.wait_ge(s["s1_read"], NT * e)
                    for k, (k0, kn) in enumerate(CH):
                        ins = mm(ps[:, 3 + x, :], wT[e][0:kn, k, x * P:(x + 1) * P], xT[0:kn, k, :], k == 0, k == 1)
                    ins.then_inc(s["qk1_mm"], 1)

            def values_in(e):
                for j in range(2):
                    for m in range(2):
                        i = 2 * j + m
                        for k, (k0, kn) in enumerate(CH):
                            ins = mm(ps[:, 5 + j, m * D:m * D + D], xT[0:kn, k, i * P:(i + 1) * P],
                                     wT[e][0:kn, k, 2 * D:3 * D], k == 0, k == 1)
                    ins.then_inc(s["v1_mm"], 1)

            def scores1(n):
                e, t = divmod(n, NT)
                if t == 0:
                    pe.wait_ge(s["qk1_dve"], 2 * e + 2)
                    pe.wait_ge(s["qk1_act"], 2 * e + 2)
                if t == 1:
                    pe.wait_ge(s["v1_done"], 2 * e + 2)
                if n >= 2:
                    pe.wait_ge(s["s1_read"], n - 1)
                for m in range(2):
                    b, bank = 2 * t + m, 3 + 2 * (n % 2) + m
                    mm(ps[:, bank, 0:4 * S], qm[:, 0, b].rearrange("p h i -> p (h i)"),
                       kbd[:, b].rearrange("p a j -> p (a j)"), True, True)
                    ins = mm(ps[:, bank, 4 * S:6 * S], qm[0:DB, 1, b].rearrange("p h i -> p (h i)"),
                             kbdB[0:DB, b].rearrange("p a j -> p (a j)"), True, True)
                ins.then_inc(s["s1_mm"], 1)

            def turn1(n):
                pe.wait_ge(s["exp1"], n + 1)
                if n >= 1:
                    pe.wait_ge(s["pT1_done"], n)
                for p in range(PAIRS):
                    ins = tr(ps[:, p // 3, (p % 3) * P:(p % 3 + 1) * P], p1[:, n % 2, p].rearrange("p m j -> p (m j)"))
                ins.then_inc(s["t1_mm"], 1)

            def values1(n):
                e, t = divmod(n, NT)
                pe.wait_ge(s["pT1_done"], n + 1)
                pe.wait_ge(s["v1_done"], 2 * e + 1 + t // 2)
                if n >= 1:
                    pe.wait_ge(s["o1_done"], n)
                w = 2 * (2 * DH + 1)
                for p in range(PAIRS):
                    ins = mm(ps[:, 7, p * w:(p + 1) * w], pT1[:, n % 2, p, :],
                             vbd[:, e % 2, t, p].rearrange("p m d -> p (m d)"), True, True)
                ins.then_inc(s["pv1_mm"], 1)

            def turn_o(n):
                pe.wait_ge(s["o1_done"], n + 1)
                if n % 2 == 0 and n >= 2:
                    pe.wait_ge(s["ot1_done"], n // 2)
                if n % NT == 0 and n >= NT:
                    pe.wait_ge(s["fT_dve"], n // NT)
                for m in range(2):
                    at = (2 * (n % 2) + m) * P
                    ins = tr(ps[0:96, 2, at:at + P], o1[:, n % 2, m].rearrange("p a d -> p (a d)"))
                ins.then_inc(s["ot1_mm"], 1)

            def join(e, c):
                if c == 0:
                    pe.wait_ge(s["ot1_done"], 2 * e + 2)
                else:
                    pe.wait_ge(s["fT_act"], e + 1)
                r0, n = CH[c]
                for h in range(2):
                    ins = mm(ps[0:n, 2, :], woT[e][0:96, h, r0:r0 + n], oT1[0:96, h, :], h == 0, h == 1)
                ins.then_inc(s["wo1_mm"], 1)

            pe.wait_ge(s["zeros_made"], 2)
            def gate_up(i, experts, chunks=(0, 1)):
                for e in experts:
                    for c in chunks:
                        r0, n = CH[c]
                        ins = mm(ps[:, 3 + i, 0:2 * D], fT[0:n, e, c, i * P:(i + 1) * P], wguT[e][0:n, c, :],
                                 e == 0 and c == 0, e == EA - 1 and c == 1)
                return ins

            project1(0)
            N1 = EA * NT
            for n in range(N1):
                e, t = divmod(n, NT)
                if t == 0:
                    scores1(n)
                    values_in(e)
                    if n >= 1:
                        values1(n - 1)
                        turn_o(n - 2)
                    scores1(n + 1)
                else:
                    if t < NT - 1:
                        scores1(n + 1)
                    elif e < EA - 1:
                        project1(e + 1)
                    values1(n - 1)
                if e >= 1 and t in (1, 2):
                    join(e - 1, t - 1)
                turn1(n)
                if t == 0 and e >= 1:
                    turn_o(n - 1)
                elif t >= 2:
                    turn_o(n - 2)
            first = range(EA - 1)
            pe.wait_ge(s["fT_act"], EA - 1)
            pe.wait_ge(s["fT_dve"], EA - 1)
            pe.wait_ge(s["s1_read"], N1)
            gate_up(0, first)
            values1(N1 - 1)
            turn_o(N1 - 2)
            gate_up(1, first)
            turn_o(N1 - 1)
            gate_up(2, first)
            join(EA - 1, 0)
            gate_up(3, first)
            join(EA - 1, 1)
            last = (EA - 1,)
            pe.wait_ge(s["fT_act"], EA)
            gate_up(0, last, (0,))
            gate_up(1, last, (0,))
            pe.wait_ge(s["fT_dve"], EA)
            gate_up(0, last, (1,)).then_inc(s["gu_mm"], 1)
            gate_up(1, last, (1,)).then_inc(s["gu_mm"], 1)
            gate_up(2, last).then_inc(s["gu_mm"], 1)
            gate_up(3, last).then_inc(s["gu_mm"], 1)
            keep_busy(14, 2)
            turn_tokens(xn, 4, 3, bank=0, twice=True)
            xT_ready(4)

            pe.wait_ge(s["small_in"], 16 * 13)
            for c, (r0, n) in enumerate(CH):
                ins = mm(ps[0:1, 4, :], vw[0:n, c, :], xT[0:n, c, :], c == 0, c == 1)
            ins.then_inc(s["v_mm"], 1)
            for i in range(NT):
                for c, (r0, n) in enumerate(CH):
                    ins = mm(ps[:, 5, i * EM:(i + 1) * EM], xT[0:n, c, i * P:(i + 1) * P], gw[0:n, c, :],
                             c == 0, c == 1)
            ins.then_inc(s["lg_mm"], 1)
            for e in range(EM + 1):
                if e < EM:
                    pe.wait_ge(s["w1_lo"], e + 1)
                    up(w1x[e % 2], xs, turn=3 if e == 0 else 0)
                if e == 1:
                    pe.wait_ge(s["comb_done"], 1)
                    for i in range(NT):
                        ins = tr(ps[0:EM, 6, i * P:(i + 1) * P], comb[:, i, :])
                    ins.then_inc(s["combT_mm"], 1)
                if e == EM - 1:
                    pe.wait_ge(s["chF_in"], 32)
                    pe.wait_ge(s["y_done"], EM - 2)
                    for i in range(NT):
                        mm(two_t(6, i), combT[0:EM, i * P:(i + 1) * P], b2m[0:EM], True, False)
                        ins = mm(two_t(6, i), frow[:, i * P:(i + 1) * P], ow3[0:3], False, True)
                    ins.then_inc(s["extra_mm"], 1)
                if e >= 1:
                    d = e - 1
                    if d == EM - 1:
                        pe.wait_ge(s["extra_done"], 1)
                    if d == 1:
                        pe.wait_ge(s["combT_done"], 1)
                    if d >= 2:
                        pe.wait_ge(s["y_done"], d - 1)
                    pe.wait_ge(s["h_act"], NF * (d + 2))
                    pe.wait_ge(w2_in[d % NSLOT], 16 * (d // NSLOT + 1))
                    down(hT[:, d % 2], w2s[:, d % NSLOT], 4 + 2 * (d % 2), halves=d == EM - 1)
            keep_busy(10, 2)
            turn_tokens(xn, 5, 4, bank=0)
            xT_ready(5)

            pe.wait_ge(s["s3_in"], 16 * 15)
            for x in range(3):
                for k, (k0, kn) in enumerate(CH):
                    ins = mm(ps[:, x, :], wqk3[0:kn, k, x * P:(x + 1) * P], xT[0:kn, k, :], k == 0, k == 1)
                ins.then_inc(s["q3_mm"], 1)
            for i in range(NT):
                for k, (k0, kn) in enumerate(CH):
                    ins = mm(two_t(4, i), xT[0:kn, k, i * P:(i + 1) * P], wvo3[0:kn, 0, k, :], k == 0, k == 1)
                if i % 2:
                    ins.then_inc(s["v3_mm"], 1)
            for c, (r0, n) in enumerate(CH):
                ins = mm(ps[0:16, 7, :], wg1[0:n, c, :], xT[0:n, c, :], c == 0, c == 1)
            ins.then_inc(s["gate1_mm"], 1)
            pe.wait_ge(s["q3_done"], 2)
            pe.wait_ge(s["km_done"], 2)
            pe.wait_ge(s["v3_done"], 2)

            def values3(t):
                pe.wait_ge(s["e3_done"], t + 1)
                for m in range(2):
                    for p in range(PAIRS):
                        at = t % 2 * D + p * 2 * DH
                        ins = mm(ps[64 * m:64 * m + 64, 4 + t // 2, at:at + 2 * DH], E3[t // 2][:, t % 2, p, m, :],
                                 vbd3[:, 2 * t + m, p].rearrange("p h d -> p (h d)"), True, True)
                return ins

            for t in range(NT):
                if t >= 2:
                    pe.wait_ge(s["e3_done"], t - 1)
                for m in range(2):
                    b, bank = 2 * t + m, 2 * (t % 2) + m
                    mm(ps[:, bank, 0:4 * S], km3[:, 0, b].rearrange("p h i -> p (h i)"),
                       q3[:, b].rearrange("p a i -> p (a i)"), True, True)
                    ins = mm(ps[:, bank, 4 * S:6 * S], km3[0:DB, 1, b].rearrange("p h i -> p (h i)"),
                             q3b[0:DB, b].rearrange("p a i -> p (a i)"), True, True)
                ins.then_inc(s["e3_mm"], 1)
                if t == 0:
                    pe.wait_ge(s["gate1_done"], 1)
                    for i in range(NT):
                        ins = mm(two_t(6, i), g1T[:, i * P:(i + 1) * P], wg2, True, True)
                    ins.then_inc(s["gate3_mm"], 1)
                else:
                    ins = values3(t - 1)
                if t == 2:
                    ins.then_inc(s["pv3_mm"], 1)
            values3(NT - 1).then_inc(s["pv3_mm"], 1)
            turn_tokens(gate3, 6, halves="og_done")
            xT_ready(6)
            for i in range(NT):
                for k, (k0, kn) in enumerate(CH):
                    ins = mm(two_t(0, i), xT[0:kn, k, i * P:(i + 1) * P], wvo3[0:kn, 1, k, :], k == 0, k == 1)
                if i % 2:
                    ins.then_inc(s["tok_mm"], 1)
            keep_busy(25, 2)
            turn_tokens(xn, 7, 5, bank=0, twice=True)
            xT_ready(7)

            def cls(c, n):
                return xcls[0:n, c, :]

            pe.wait_ge(s["xcls_done"], 1)

            pe.wait_ge(s["a_in"], 16 * 15)

            def class_hidden(x):
                if x >= 2:
                    pe.wait_ge(s["hc_add"], x - 1)
                for f in range(NF):
                    for c, (r0, n) in enumerate(CH):
                        ins = mm(ps[:, 6 + x % 2, f * NC:(f + 1) * NC], a1w[0:n, x, c, f * P:(f + 1) * P], cls(c, n),
                                 c == 0, c == 1)
                ins.then_inc(s["hc_mm"], 1)

            class_hidden(0)
            pe.wait_ge(s["wx_lo"], 3)
            up(wm0x, xs, range(2), turn=4)
            pe.wait_ge(s["xg_done"], 1)
            for c, (r0, n) in enumerate(CH):
                ins = mm(ps[:, 4, 0:2 * NC], ones[0:n], xg[0:n, c].rearrange("p q n -> p (q n)"), c == 0, c == 1)
            ins.then_inc(s["cl_mm"], 1)
            up(wm0x, xs, range(2, 3))
            for x in range(3):
                class_hidden(x + 1)
                up(wm0x, xs, range(3 + x, 4 + x))
            class_hidden(4)
            pe.wait_ge(s["h_act"], jobs[0])
            pe.wait_ge(s["cl_sub"], 1)
            pe.wait_ge(s["m0_in"], 64)
            down(hT[:, 0], m0w2, 4, halves=True)
            for c, (r0, n) in enumerate(CH):
                ins = tr(ps[0:NC, 2, r0:r0 + n], cls(c, n))
            ins.then_inc(s["clsx_mm"], 1)
            pe.wait_ge(s["hmix_done"], 1)
            for x in range(5):
                for f in range(NF):
                    mm(ps[0:NC, 3, 0:D], hmix[:, x, f, :], a2w[:, x, f, :], x == 0 and f == 0, False)
            for x in range(5):
                ins = mm(ps[0:NC, 3, 0:D], mcls[0:1, x, :], a2b[0:1, x, :], False, x == 4)
            ins.then_inc(s["cls_mm"], 1)


_INS = {
    "x": "x", "w_patch": "L0_tok_w_patch", "b_patch": "L0_tok_b_patch", "g1": "L0_tok_g1", "beta1": "L0_tok_beta1",
    "w_qkv": "L0_tok_w_qkv", "w_out": "L0_tok_w_out", "b_out": "L0_tok_b_out", "g2": "L0_tok_g2",
    "beta2": "L0_tok_beta2", "w_ff1": "L0_tok_w_ff1", "b_ff1": "L0_tok_b_ff1", "w_ff2": "L0_tok_w_ff2",
    "b_ff2": "L0_tok_b_ff2", "wq": "L0_attn_wq", "wk": "L0_attn_wk", "wv": "L0_attn_wv", "wo": "L0_attn_wo",
    "w_gate": "L0_attn_w_gate", "w_up": "L0_attn_w_up", "v_w": "L0_ffn_v_w", "v_b": "L0_ffn_v_b",
    "gate_w": "L0_ffn_gate_w", "gate_b": "L0_ffn_gate_b", "w1": "L0_ffn_w1", "b1": "L0_ffn_b1", "w2": "L0_ffn_w2",
    "b2": "L0_ffn_b2", "out_w": "L0_ffn_out_w", "out_b": "L0_ffn_out_b", "bk": "L0_ffn_bk_scale",
    "slope": "L1_attn_log_slope", "Wq": "L1_attn_Wq", "Wk": "L1_attn_Wk", "Wv": "L1_attn_Wv", "Wo": "L1_attn_Wo",
    "Wg1": "L1_attn_Wg1", "Wg2": "L1_attn_Wg2", "ln_w": "L1_attn_ln_w", "ln_b": "L1_attn_ln_b",
    "m0w1": "L1_ffn_moe0_W1", "m0_b1": "L1_ffn_moe0_b1", "m0w2": "L1_ffn_moe0_W2", "m0_b2": "L1_ffn_moe0_b2",
    "a1w": "L1_ffn_A1_W", "a1b": "L1_ffn_A1_b", "a2w": "L1_ffn_A2_W", "a2b": "L1_ffn_A2_b", "gcls": "L1_ffn_G_W",
}


def kernel(**inputs):
    import numpy as _np
    import concourse.bacc as _bacc
    from concourse import mybir as _mybir
    from concourse.bass_utils import run_bass_kernel_spmd as _run

    nc = _bacc.Bacc("TRN2", target_bir_lowering=False, num_devices=1)
    arrays, args = {}, {}
    for short, name in _INS.items():
        v = _np.ascontiguousarray(inputs[name])
        if v.ndim == 0:
            v = v.reshape(1)
        arrays[f"in_{short}"] = v
        args[short] = nc.dram_tensor(f"in_{short}", v.shape, _mybir.dt.from_np(v.dtype), kind="ExternalInput").ap()
    out = nc.dram_tensor("out_0", (8, 64, 192), _mybir.dt.float32, kind="ExternalOutput").ap()
    vit_tower(nc, args, out)
    r = _run(nc, [arrays], core_ids=[0])
    return r.results[0]["out_0"]
```
